# Optimizing a Trainium2 kernel written in Bass

```python
import numpy as np
import jax
import jax.numpy as jnp

def _softmax(x, axis=-1):
    return jax.nn.softmax(x, axis=axis)

def _gelu(x):
    return jax.nn.gelu(x, approximate=True)

def _silu(x):
    return jax.nn.silu(x)

def _sigmoid(x):
    return jax.nn.sigmoid(x)

def _layernorm(x, axis=-1, eps=1e-05):
    m = jnp.mean(x, axis=axis, keepdims=True)
    v = jnp.var(x, axis=axis, keepdims=True)
    return (x - m) / jnp.sqrt(v + eps)

def _scatter_add(tgt, idx, src, axis=0):
    return tgt.at[idx].add(src)

def _segment_sum(src, seg, n):
    return jax.ops.segment_sum(src, seg, n)
kernel_name = 'mk_decoder_postln_d1_seqx_r8_ea371e'

def setup_inputs(seed: int=0):
    np.random.seed(seed)
    _w = jnp.asarray

    def _rec_inputs():
        import jax
        import jax.numpy as jnp
        _rk = jax.random.key(seed)
        x = -0.000125 + 0.9999 * jax.random.normal(jax.random.fold_in(_rk, 1), (8, 128, 256), jnp.float32)
        _lenS = 128 - jax.random.randint(jax.random.fold_in(_rk, 7), (8,), 0, max(1, 128 // 4) + 1, jnp.int32)
        _lenS2 = 128 - jax.random.randint(jax.random.fold_in(_rk, 8), (8,), 0, max(1, 128 // 4) + 1, jnp.int32)
        _ctx_2048P = jax.random.normal(jax.random.fold_in(_rk, 11), (8, 16, 256), jnp.float32)
        _ctx_2048c = jax.random.dirichlet(jax.random.fold_in(_rk, 511), 0.3 * jnp.ones((16,), jnp.float32), (8, 128))
        _ctx_2048t = jnp.einsum('bsk,bkd->bsd', _ctx_2048c, _ctx_2048P)
        _ctx_2048t = _ctx_2048t * jax.lax.rsqrt(jnp.mean(jnp.square(_ctx_2048t)) + 1e-12) * 0.953939
        ctx_2048 = -1.52775e-05 + 0.999936 * (_ctx_2048t + 0.3 * jax.random.normal(jax.random.fold_in(_rk, 611), (8, 128, 256), jnp.float32))
        return (x, ctx_2048)
    x, ctx_2048 = _rec_inputs()

    def _L0_attn_setup():
        import jax, jax.numpy as jnp
        import numpy as np
        B, T, HIDDEN = (2, 512, 256)
        NUM_HEADS, HEAD_K, HEAD_V = (6, 32, 64)
        KEY_DIM, VALUE_DIM = (NUM_HEADS * HEAD_K, NUM_HEADS * HEAD_V)
        CONV_K, CHUNK, EPS = (4, 64, 1e-05)

        def short_conv(x, w):
            K = w.shape[1]
            xp = jnp.pad(x, ((0, 0), (K - 1, 0), (0, 0)))
            y = sum((xp[:, i:i + x.shape[1], :] * w[:, i] for i in range(K)))
            return jax.nn.silu(y)

        def l2norm(x):
            return x * jax.lax.rsqrt(jnp.sum(x * x, -1, keepdims=True))

        def _step(S, xs):
            qt, kt, vt, gt, bt = xs
            S = S * jnp.exp(gt)[..., None, None]
            pred = jnp.einsum('bhk,bhkv->bhv', kt, S)
            delta = (vt - pred) * bt[..., None]
            S = S + jnp.einsum('bhk,bhv->bhkv', kt, delta)
            return (S, jnp.einsum('bhk,bhkv->bhv', qt, S))

        def _chunk(S, xs):
            return jax.lax.scan(_step, S, xs)
        _chunk_ckpt = jax.checkpoint(_chunk)

        def gated_delta_rule(q, k, v, g, beta):
            b, t, h, dk = q.shape
            dv = v.shape[-1]
            q = l2norm(q) * dk ** (-0.5)
            k = l2norm(k)
            nc = t // CHUNK

            def to_scan(x):
                x = x.reshape(b, nc, CHUNK, *x.shape[2:])
                return jnp.moveaxis(x, 0, 2)
            xs = tuple(map(to_scan, (q, k, v, g, beta)))
            S0 = jnp.zeros((b, h, dk, dv), q.dtype)
            _, o = jax.lax.scan(_chunk_ckpt, S0, xs)
            return jnp.moveaxis(o, 2, 0).reshape(b, t, h, dv)
        key = jax.random.key(seed)
        ks = jax.random.split(key, 14)

        def lin(k, fi, fo):
            return jax.random.normal(k, (fi, fo), jnp.float32) / np.sqrt(fi)
        A = jax.random.uniform(ks[11], (NUM_HEADS,), minval=0.001, maxval=16.0)
        dt = jnp.exp(jax.random.uniform(ks[12], (NUM_HEADS,)) * (np.log(0.1) - np.log(0.001)) + np.log(0.001))
        dt = jnp.clip(dt, 0.0001)
        return {'hidden_states': jax.random.normal(ks[0], (B, T, HIDDEN), jnp.float32), 'Wq': lin(ks[1], HIDDEN, KEY_DIM), 'Wk': lin(ks[2], HIDDEN, KEY_DIM), 'Wv': lin(ks[3], HIDDEN, VALUE_DIM), 'Wa': lin(ks[4], HIDDEN, NUM_HEADS), 'Wb': lin(ks[5], HIDDEN, NUM_HEADS), 'Wg': lin(ks[6], HIDDEN, VALUE_DIM), 'Wo': lin(ks[7], VALUE_DIM, HIDDEN), 'conv_wq': jax.random.normal(ks[8], (KEY_DIM, CONV_K), jnp.float32) / np.sqrt(CONV_K), 'conv_wk': jax.random.normal(ks[9], (KEY_DIM, CONV_K), jnp.float32) / np.sqrt(CONV_K), 'conv_wv': jax.random.normal(ks[10], (VALUE_DIM, CONV_K), jnp.float32) / np.sqrt(CONV_K), 'A_log': jnp.log(A), 'dt_bias': dt + jnp.log(-jnp.expm1(-dt)), 'norm_weight': jnp.ones((HEAD_V,), jnp.float32)}
    _L0_attn_all = _L0_attn_setup()
    _L0_attn_in = {k: v for k, v in _L0_attn_all.items() if k in ('Wq', 'Wk', 'Wv', 'Wa', 'Wb', 'Wg', 'Wo', 'conv_wq', 'conv_wk', 'conv_wv', 'A_log', 'dt_bias', 'norm_weight')}
    del _L0_attn_all

    def _L0_xattn_setup():
        import jax, jax.numpy as jnp
        import numpy as np
        B, DIM1, DIM2, LATENT, T = (16, 128, 128, 64, 256)
        LN_EPS = 1e-05
        key = jax.random.key(seed)
        ks = jax.random.split(key, 8)

        def xavier(k, shape):
            fan_out, fan_in = shape
            std = float(np.sqrt(2.0 / (fan_in + fan_out)))
            return jax.random.normal(k, shape, dtype=jnp.float32) * std
        return {'input1': jax.random.normal(ks[0], (B, DIM1, T), dtype=jnp.float32), 'input2': jax.random.normal(ks[1], (B, DIM2, T), dtype=jnp.float32), 'theta_w': xavier(ks[2], (LATENT, DIM2)), 'theta_b': jnp.zeros((LATENT,), jnp.float32), 'phi_w': xavier(ks[3], (LATENT, DIM1)), 'phi_b': jnp.zeros((LATENT,), jnp.float32), 'g_w': xavier(ks[4], (LATENT, DIM1)), 'g_b': jnp.zeros((LATENT,), jnp.float32), 'ln_gamma': jnp.ones((LATENT, T), jnp.float32), 'ln_beta': jnp.zeros((LATENT, T), jnp.float32), 'out_w': xavier(ks[5], (DIM2, LATENT)), 'out_b': jnp.zeros((DIM2,), jnp.float32)}
    _L0_xattn_all = _L0_xattn_setup()
    _L0_xattn_in = {k: v for k, v in _L0_xattn_all.items() if k in ('theta_w', 'theta_b', 'phi_w', 'phi_b', 'g_w', 'g_b', 'ln_gamma', 'ln_beta', 'out_w', 'out_b')}
    del _L0_xattn_all

    def _L0_ffn_setup():
        import jax, jax.numpy as jnp
        import numpy as np
        _FP8_MAX = 448.0
        _BLOCK = 32
        _EPS = 1e-30

        def _mx_dequant(t):
            rows, feat = t.shape
            blocks = t.reshape(rows, feat // _BLOCK, _BLOCK)
            max_abs = jnp.max(jnp.abs(blocks), axis=-1)
            scales = jnp.maximum(max_abs / _FP8_MAX, _EPS)
            q = (blocks / scales[..., None]).astype(jnp.float8_e4m3fn).astype(jnp.float32)
            return (q * scales[..., None]).reshape(rows, feat)

        def _mx_linear(x2d, w):
            return _mx_dequant(x2d) @ _mx_dequant(w).T
        key = jax.random.key(seed)
        k1, k2, k3, k4 = jax.random.split(key, 4)
        B, S, H, I = (2, 128, 256, 1024)
        return {'x': jax.random.normal(k1, (B, S, H), dtype=jnp.float32), 'gate_w': jax.random.normal(k2, (I, H), dtype=jnp.float32) * 0.02, 'up_w': jax.random.normal(k3, (I, H), dtype=jnp.float32) * 0.02, 'down_w': jax.random.normal(k4, (H, I), dtype=jnp.float32) * 0.02}
    _L0_ffn_all = _L0_ffn_setup()
    _L0_ffn_in = {k: v for k, v in _L0_ffn_all.items() if k in ('gate_w', 'up_w', 'down_w')}
    del _L0_ffn_all
    return {'x': x, 'ctx_2048': ctx_2048, 'L0_attn_Wq': _L0_attn_in['Wq'], 'L0_attn_Wk': _L0_attn_in['Wk'], 'L0_attn_Wv': _L0_attn_in['Wv'], 'L0_attn_Wa': _L0_attn_in['Wa'], 'L0_attn_Wb': _L0_attn_in['Wb'], 'L0_attn_Wg': _L0_attn_in['Wg'], 'L0_attn_Wo': _L0_attn_in['Wo'], 'L0_attn_conv_wq': _L0_attn_in['conv_wq'], 'L0_attn_conv_wk': _L0_attn_in['conv_wk'], 'L0_attn_conv_wv': _L0_attn_in['conv_wv'], 'L0_attn_A_log': _L0_attn_in['A_log'], 'L0_attn_dt_bias': _L0_attn_in['dt_bias'], 'L0_attn_norm_weight': _L0_attn_in['norm_weight'], 'L0_xattn_theta_w': _L0_xattn_in['theta_w'], 'L0_xattn_theta_b': _L0_xattn_in['theta_b'], 'L0_xattn_phi_w': _L0_xattn_in['phi_w'], 'L0_xattn_phi_b': _L0_xattn_in['phi_b'], 'L0_xattn_g_w': _L0_xattn_in['g_w'], 'L0_xattn_g_b': _L0_xattn_in['g_b'], 'L0_xattn_ln_gamma': _L0_xattn_in['ln_gamma'], 'L0_xattn_ln_beta': _L0_xattn_in['ln_beta'], 'L0_xattn_out_w': _L0_xattn_in['out_w'], 'L0_xattn_out_b': _L0_xattn_in['out_b'], 'L0_ffn_gate_w': _L0_ffn_in['gate_w'], 'L0_ffn_up_w': _L0_ffn_in['up_w'], 'L0_ffn_down_w': _L0_ffn_in['down_w']}

def reference(x, ctx_2048, L0_attn_Wq, L0_attn_Wk, L0_attn_Wv, L0_attn_Wa, L0_attn_Wb, L0_attn_Wg, L0_attn_Wo, L0_attn_conv_wq, L0_attn_conv_wk, L0_attn_conv_wv, L0_attn_A_log, L0_attn_dt_bias, L0_attn_norm_weight, L0_xattn_theta_w, L0_xattn_theta_b, L0_xattn_phi_w, L0_xattn_phi_b, L0_xattn_g_w, L0_xattn_g_b, L0_xattn_ln_gamma, L0_xattn_ln_beta, L0_xattn_out_w, L0_xattn_out_b, L0_ffn_gate_w, L0_ffn_up_w, L0_ffn_down_w):
    import jax
    import jax.numpy as jnp

    def _L0_attn_ref(hidden_states, Wq, Wk, Wv, Wa, Wb, Wg, Wo, conv_wq, conv_wk, conv_wv, A_log, dt_bias, norm_weight):
        import jax, jax.numpy as jnp
        import numpy as np
        B, T, HIDDEN = (2, 512, 256)
        NUM_HEADS, HEAD_K, HEAD_V = (6, 32, 64)
        KEY_DIM, VALUE_DIM = (NUM_HEADS * HEAD_K, NUM_HEADS * HEAD_V)
        CONV_K, CHUNK, EPS = (4, 64, 1e-05)

        def short_conv(x, w):
            K = w.shape[1]
            xp = jnp.pad(x, ((0, 0), (K - 1, 0), (0, 0)))
            y = sum((xp[:, i:i + x.shape[1], :] * w[:, i] for i in range(K)))
            return jax.nn.silu(y)

        def l2norm(x):
            return x * jax.lax.rsqrt(jnp.sum(x * x, -1, keepdims=True))

        def _step(S, xs):
            qt, kt, vt, gt, bt = xs
            S = S * jnp.exp(gt)[..., None, None]
            pred = jnp.einsum('bhk,bhkv->bhv', kt, S)
            delta = (vt - pred) * bt[..., None]
            S = S + jnp.einsum('bhk,bhv->bhkv', kt, delta)
            return (S, jnp.einsum('bhk,bhkv->bhv', qt, S))

        def _chunk(S, xs):
            return jax.lax.scan(_step, S, xs)
        _chunk_ckpt = jax.checkpoint(_chunk)

        def gated_delta_rule(q, k, v, g, beta):
            b, t, h, dk = q.shape
            dv = v.shape[-1]
            q = l2norm(q) * dk ** (-0.5)
            k = l2norm(k)
            nc = t // CHUNK

            def to_scan(x):
                x = x.reshape(b, nc, CHUNK, *x.shape[2:])
                return jnp.moveaxis(x, 0, 2)
            xs = tuple(map(to_scan, (q, k, v, g, beta)))
            S0 = jnp.zeros((b, h, dk, dv), q.dtype)
            _, o = jax.lax.scan(_chunk_ckpt, S0, xs)
            return jnp.moveaxis(o, 2, 0).reshape(b, t, h, dv)
        b, t, _ = hidden_states.shape
        q = short_conv(hidden_states @ Wq, conv_wq).reshape(b, t, NUM_HEADS, HEAD_K)
        k = short_conv(hidden_states @ Wk, conv_wk).reshape(b, t, NUM_HEADS, HEAD_K)
        v = short_conv(hidden_states @ Wv, conv_wv).reshape(b, t, NUM_HEADS, HEAD_V)
        beta = jax.nn.sigmoid(hidden_states @ Wb)
        g = -jnp.exp(A_log) * jax.nn.softplus(hidden_states @ Wa + dt_bias)
        o = gated_delta_rule(q, k, v, g, beta)
        gate = (hidden_states @ Wg).reshape(b, t, NUM_HEADS, HEAD_V)
        o = o * jax.lax.rsqrt(jnp.mean(o * o, -1, keepdims=True) + EPS) * norm_weight
        o = o * jax.nn.silu(gate)
        return o.reshape(b, t, VALUE_DIM) @ Wo

    def _L0_xattn_ref(input1, input2, theta_w, theta_b, phi_w, phi_b, g_w, g_b, ln_gamma, ln_beta, out_w, out_b):
        import jax, jax.numpy as jnp
        import numpy as np
        B, DIM1, DIM2, LATENT, T = (16, 128, 128, 64, 256)
        LN_EPS = 1e-05
        theta_x = jnp.einsum('ld,bdt->btl', theta_w, input2) + theta_b
        phi_x = jnp.einsum('ld,bdt->blt', phi_w, input1) + phi_b[:, None]
        scores = jnp.einsum('btl,bls->bts', theta_x, phi_x)
        p = jax.nn.softmax(scores, axis=-1)
        g_x = jnp.einsum('ld,bdt->btl', g_w, input1) + g_b
        t_x = jnp.einsum('bts,bsl->blt', p, g_x)
        mu = jnp.mean(t_x, axis=(1, 2), keepdims=True)
        var = jnp.var(t_x, axis=(1, 2), keepdims=True)
        h = (t_x - mu) * jax.lax.rsqrt(var + LN_EPS) * ln_gamma + ln_beta
        h = jax.nn.relu(h)
        w_t = jnp.einsum('ol,blt->bot', out_w, h) + out_b[None, :, None]
        return w_t + input2

    def _L0_ffn_ref(x, gate_w, up_w, down_w):
        import jax, jax.numpy as jnp
        import numpy as np
        _FP8_MAX = 448.0
        _BLOCK = 32
        _EPS = 1e-30

        def _mx_dequant(t):
            rows, feat = t.shape
            blocks = t.reshape(rows, feat // _BLOCK, _BLOCK)
            max_abs = jnp.max(jnp.abs(blocks), axis=-1)
            scales = jnp.maximum(max_abs / _FP8_MAX, _EPS)
            q = (blocks / scales[..., None]).astype(jnp.float8_e4m3fn).astype(jnp.float32)
            return (q * scales[..., None]).reshape(rows, feat)

        def _mx_linear(x2d, w):
            return _mx_dequant(x2d) @ _mx_dequant(w).T
        B, S, H = x.shape
        x2d = x.reshape(B * S, H)
        gate = _mx_linear(x2d, gate_w)
        up = _mx_linear(x2d, up_w)
        h = jax.nn.silu(gate) * up
        out = _mx_linear(h, down_w)
        return out.reshape(B, S, H)
    x = _layernorm(x + _L0_attn_ref(x, L0_attn_Wq, L0_attn_Wk, L0_attn_Wv, L0_attn_Wa, L0_attn_Wb, L0_attn_Wg, L0_attn_Wo, L0_attn_conv_wq, L0_attn_conv_wk, L0_attn_conv_wv, L0_attn_A_log, L0_attn_dt_bias, L0_attn_norm_weight), axis=-1)
    x = _layernorm(x + _L0_xattn_ref(x, ctx_2048, L0_xattn_theta_w, L0_xattn_theta_b, L0_xattn_phi_w, L0_xattn_phi_b, L0_xattn_g_w, L0_xattn_g_b, L0_xattn_ln_gamma, L0_xattn_ln_beta, L0_xattn_out_w, L0_xattn_out_b), axis=-1)
    x = _layernorm(x + _L0_ffn_ref(x, L0_ffn_gate_w, L0_ffn_up_w, L0_ffn_down_w), axis=-1)
    return x

_drawn_inputs = setup_inputs


def setup_inputs(seed=0):
    import zlib

    import numpy as np

    out = dict(_drawn_inputs(seed))
    spreads = {'L0_attn_norm_weight': (1.0, 0.2),
     'L0_xattn_theta_b': (0.0, 0.1),
     'L0_xattn_phi_b': (0.0, 0.8),
     'L0_xattn_g_b': (0.0, 0.285),
     'L0_xattn_ln_gamma': (1.0, 0.2),
     'L0_xattn_ln_beta': (0.0, 0.1),
     'L0_xattn_out_b': (0.0, 0.8)}
    factors = {}
    for name, (base, spread) in spreads.items():
        noise = np.random.default_rng([zlib.crc32(name.encode()), seed]).standard_normal(out[name].shape)
        drawn = base * np.exp(spread * noise) if base else spread * noise
        out[name] = jnp.asarray(drawn.astype(out[name].dtype))
    for name, factor in factors.items():
        out[name] = (out[name] * factor).astype(out[name].dtype)
    return out
```

```python
from contextlib import ExitStack

import concourse.bass as bass
from concourse import mybir

F32 = mybir.dt.float32
I32 = mybir.dt.int32
ALU = mybir.AluOpType
ACT = mybir.ActivationFunctionType
X = mybir.AxisListType.X

P = 128
SEQ = 8
HALF = 4
HID = 256
NH, DK, DV = 6, 32, 64
TAPS = 4
NQ = HALF * NH
LAT, INTER = 64, 1024
BLK = 32
NBANK = 8
EPS = 1e-5
FP8_MAX, SCALE_MIN = 448.0, 1e-30
MIN_NORMAL = 2.0 ** -6
MAGIC_SHIFT = 2.0 ** 20
EXP_MASK, HALF_BIT = 0x7F800000, 0x00400000

FT = [(0, 128), (128, 128), (256, 64), (320, 64), (384, 128), (512, 128), (640, 128)]
NFT = len(FT)


class Tiles:

    def __init__(self):
        self.names, self.at, self.count = [], {}, {"act": 0, "dve": 0}
        self.drain = []

    def add(self, name, reader):
        self.at[name] = len(self.names)
        self.names.append(name)
        self.count[reader] += 1
        self.drain.append((reader, self.count[reader]))


def half_tiles(t, f):
    t.add((f, "xT", 0), "act")
    t.add((f, "xT", 1), "dve")
    t.add((f, "ab"), "dve")
    for i in range(NFT):
        t.add((f, "feat", i), "dve")
    for b in range(HALF):
        t.add((f, "gate", b), "act")
    t.add((f, "norm"), "dve")
    for g in range(NQ // 4):
        t.add((f, "decay", g), "act")
    for b in range(HALF):
        t.add((f, "vT", b), "dve")
    for j in range(HALF // 2):
        for h in range(NH):
            t.add((f, "kq", j, h), "dve")
    for g in range(NQ // 8):
        t.add((f, "y0", g), "act")
    for k in range(1, P // BLK):
        for g in range(NQ // 8):
            t.add((f, "r", k, g), "act")
        for g in range(NQ // 8):
            t.add((f, "z", k, g), "dve")
    for g in range(NQ // 8):
        t.add((f, "o", g), "act")
    for b in range(HALF):
        t.add((f, "ogT", b), "act")
    for b in range(HALF):
        t.add((f, "y", b), "dve")


ST = ["thph", "g", "sc", "pT", "tx", "mu", "var", "ow", "x2T",
      "gate0", "up0", "gate1", "up1", "hT0", "hT1", "dn"]
ST_READER = {k: ("act" if k in ("sc", "pT", "x2T", "hT0", "hT1") else "dve") for k in ST}
ST_AT = {k: i for i, k in enumerate(ST)}
ST_N = {e: sum(r == e for r in ST_READER.values()) for e in ("act", "dve")}
ST_DRAIN = {k: sum(ST_READER[j] == ST_READER[k] for j in ST[:i + 1]) for i, k in enumerate(ST)}


def program(nc, x, ctxt, Wq, Wk, Wv, Wa, Wb, Wg, Wo, conv_wq, conv_wk, conv_wv, A_log, dt_bias,
            norm_weight, theta_w, theta_b, phi_w, phi_b, g_w, g_b, ln_gamma, ln_beta, out_w,
            out_b, gate_w, up_w, down_w, out):
    tiles = Tiles()
    WPREP = [("gw", 4), ("uw", 4), ("dw", 4)]
    for f in range(2):
        half_tiles(tiles, f)
        if f == 0:
            for w, n in WPREP:
                for i in range(n):
                    tiles.add((w, i), "act")

    with ExitStack() as stack:
        def sb(name, shape, dt=F32):
            return stack.enter_context(nc.sbuf_tensor(name, shape, dt))

        def sem(name):
            return stack.enter_context(nc.semaphore(name))

        bank = [stack.enter_context(nc.psum_tensor(f"bank{i}", [P, 512], F32)) for i in range(NBANK)]

        ident = sb("ident", [P, P])
        upto = sb("upto", [P, P])
        after = sb("after", [P, P])
        headsel = sb("headsel", [P, 4])
        mean64 = sb("mean64", [LAT, P])
        powers = sb("powers", [P, HALF, 2 * NH])
        mhalf = sb("mhalf", [P, NQ])
        W_f = sb("W_f", [P, 2, 768])
        W_g = sb("W_g", [P, 2, NH * DV])
        W_ab = sb("W_ab", [P, 2, 2 * NH])
        W_o = sb("W_o", [P, 3, HID])
        conv_w = sb("conv_w", [P, NFT, TAPS])
        ab_bias = sb("ab_bias", [P, 2 * NH])
        expA = sb("expA", [P, NH])
        norm_w = sb("norm_w", [P, DV])
        gateT = sb("gateT", [P, 2, INTER])
        upT = sb("upT", [P, 2, INTER])
        downT = sb("downT", [P, INTER // P, HID])
        xw_in = sb("xw_in", [LAT, 3, P])
        xw = sb("xw", [P, 3, LAT])
        ow_in = sb("ow_in", [P, LAT])
        owT = sb("owT", [LAT, P])
        th_b = sb("th_b", [LAT, 1])
        ph_b = sb("ph_b", [LAT, 1])
        g_bb = sb("g_bb", [P, LAT])
        gamma = sb("gamma", [LAT, HID])
        beta_ln = sb("beta_ln", [LAT, HID])
        o_b = sb("o_b", [P, 1])

        x1 = sb("x1", [P, SEQ, HID])
        x_h = sb("x_h", [P, HALF, HID])
        xT = sb("xT", [P, 2, 512])
        F = sb("F", [P, NFT, 512])
        SG = sb("SG", [P, NQ, DV])
        sq = sb("sq", [P, 4, 512])
        MP = sb("MP", [P, NQ, 2, P])
        E = sb("E", [P, NQ, P])
        TTe = sb("TTe", [P, NQ, P])
        CD = sb("CD", [P, BLK, BLK])
        L = sb("L", [P, BLK, BLK])
        T = sb("T", [P, BLK, BLK])
        CT = sb("CT", [P, BLK, BLK])
        Wl = sb("Wl", [P, 16, 16])
        u = sb("u", [P, NQ, DV])
        Y0 = sb("Y0", [P, NQ, DV])
        R = sb("R", [P, NQ, DV])
        om = sb("om", [P, NQ, DV])
        small = sb("small", [P, 12, HALF, 2 * NH])
        stats = sb("stats", [P, HALF, 6])
        mv = sb("mv", [P, HALF, 2])
        GU = MP[:, :, :, :].rearrange("p q a t -> p (q a t)")[:, 0:NQ * P].rearrange("p (q t) -> p q t", t=P)
        prod = E[:, :, :].rearrange("p q t -> p (q t)")
        osb, osq = Y0, R
        ogT = u[:, :, :].rearrange("p q d -> p (q d)").rearrange("p (b c t) -> p b c t", b=HALF, c=3)

        arena = sb("arena", [P, 3, 2048])
        wn, wx, ww = (arena[:, i, :] for i in range(3))
        wsc = sb("wsc", [P, 3, 64])

        Eb = E[:, :, :].rearrange("p q t -> p (q t)")
        Tb = TTe[:, :, :].rearrange("p q t -> p (q t)")
        MPb = MP[:, :, :, :].rearrange("p q a t -> p (q a t)")
        S = []
        for s in range(2):
            d = {n: sb(f"{n}{s}", shape) for n, shape in [
                ("sm", [P, 32]), ("st", [P, 8]), ("bs", [P, 6]), ("qs", [P, 3, 32])]}
            a = arena[:, :, :].rearrange("p i n -> p (i n)")[:, 3072 * s:3072 * s + 3072]
            for i, n in enumerate(["ctx", "xb", "xc", "x2"]):
                d[n] = a[:, HID * i:HID * i + HID]
            d["thph"] = a[0:LAT, 1024:1536].rearrange("p (k t) -> p k t", k=2)
            d["p"] = a[:, 1536:2048].rearrange("p (k t) -> p k t", k=2)
            d["g"] = a[:, 2048:2176].rearrange("p (k t) -> p k t", k=2)
            d["h1"] = a[0:LAT, 2176:2176 + HID]
            base = [MPb[:, 0:3072], MPb[:, 3072:6144]][s]
            d["th"] = base[:, 0:1024]
            d["hh"] = base[:, 1024:2048]
            d["w"] = base[:, 2048:3072]
            o2 = [Eb, Tb][s]
            d["xq"] = o2[:, 0:1024]
            d["hT"] = o2[:, 1024:2048].rearrange("p (k t) -> p k t", t=P)
            d["x2T"] = o2[:, 2048:2304].rearrange("p (k t) -> p k t", t=P)
            d["xw"] = o2[:, 2304:2560]
            d["pT"] = o2[:, 2560:3072].rearrange("p (k t) -> p k t", t=HID)
            S.append(d)

        w_loaded = sem("w_loaded")
        w_loaded2 = sem("w_loaded2")
        x_loaded = [sem(f"x_loaded{f}") for f in range(2)]
        wn_loaded = sem("wn_loaded")
        consts_ready = sem("consts_ready")
        psum_full = sem("psum_full")
        drained = {"act": sem("act_drained"), "dve": sem("dve_drained")}
        dve_link = sem("dve_link")
        act_link = sem("act_link")
        pool_link = sem("pool_link")
        conv_started = sem("conv_started")
        feat_ready = sem("feat_ready")
        squares_ready = sem("squares_ready")
        ab_abs = sem("ab_abs")
        ab_exp = sem("ab_exp")
        ab_plus = sem("ab_plus")
        ab_ln = sem("ab_ln")
        norms_ready = sem("norms_ready")
        roots_ready = sem("roots_ready")
        GU_ready = sem("GU_ready")
        E_masked = sem("E_masked")
        u_ready = sem("u_ready")
        diag_copied = sem("diag_copied")
        diag_zeroed = sem("diag_zeroed")
        inverse_out = sem("inverse_out")
        inverse_ready = sem("inverse_ready")
        o_squared = sem("o_squared")
        ms_ready = sem("ms_ready")
        rms_ready = sem("rms_ready")
        gatew_ready = sem("gatew_ready")
        og_ready = sem("og_ready")
        var_ready = sem("var_ready")
        rstd_ready = sem("rstd_ready")
        x1_ready = sem("x1_ready")
        expA_ready = sem("expA_ready")
        wamax = sem("wamax")
        wscaled = sem("wscaled")
        wmagic = sem("wmagic")
        wquant = sem("wquant")
        xw_ready = sem("xw_ready")
        stage1_done = sem("stage1_done")

        def sems2(name):
            return [sem(f"{name}{s}") for s in range(2)]
        c_ctx, c_full = sems2("c_ctx"), sems2("c_full")
        c_drained = {"act": sems2("c_act_drained"), "dve": sems2("c_dve_drained")}
        c_xb, c_xc = sems2("c_xb"), sems2("c_xc")
        c_max, c_exp, c_pn = sems2("c_max"), sems2("c_exp"), sems2("c_pn")
        c_mean, c_dev, c_rstd = sems2("c_mean"), sems2("c_dev"), sems2("c_rstd")
        c_aff, c_relu = sems2("c_aff"), sems2("c_relu")
        c_v2, c_r2, c_x2 = sems2("c_v2"), sems2("c_r2"), sems2("c_x2")
        c_dq = sems2("c_dq")
        c_tanh, c_magic, c_hq, c_hdq = sems2("c_tanh"), sems2("c_magic"), sems2("c_hq"), sems2("c_hdq")
        c_v3, c_r3, c_x3, c_out = sems2("c_v3"), sems2("c_r3"), sems2("c_x3"), sems2("c_out")

        block = stack.enter_context(nc.Block())

        def bank_of(key):
            return bank[tiles.at[key] % NBANK]

        def wait_free(pe, key):
            n = tiles.at[key] - NBANK
            if n >= 0:
                reader, count = tiles.drain[n]
                pe.wait_ge(drained[reader], count)

        def wait_full(eng, key):
            eng.wait_ge(psum_full, tiles.at[key] + 1)

        def wait_drained(eng, key):
            reader, count = tiles.drain[tiles.at[key]]
            eng.wait_ge(drained[reader], count)

        def wait_slot_free(pe, s, it, name):
            i = ST_AT[name]
            if i >= 4:
                prev = ST[i - 4]
                pe.wait_ge(c_drained[ST_READER[prev]][s], it * ST_N[ST_READER[prev]] + ST_DRAIN[prev])

        def slot_bank(s, name):
            return bank[4 * s + ST_AT[name] % 4]

        def full_at(it, name):
            return it * len(ST) + ST_AT[name] + 1

        def drained_at(it, name):
            return it * ST_N[ST_READER[name]] + ST_DRAIN[name]

        NW1, NW2 = 0, 0
        def v256(w):
            return w.rearrange("(c p) n -> p c n", p=P)
        loads1 = [
            (W_f[:, :, 0:128], v256(Wk)[:, :, 0:128]), (W_f[:, :, 128:256], v256(Wq)[:, :, 0:128]),
            (W_f[:, :, 256:320], v256(Wk)[:, :, 128:192]), (W_f[:, :, 320:384], v256(Wq)[:, :, 128:192]),
            (W_f[:, :, 384:768], v256(Wv)), (W_g[:, :, :], v256(Wg)),
            (W_ab[:, :, 0:NH], v256(Wa)), (W_ab[:, :, NH:2 * NH], v256(Wb)),
            (W_o[:, :, :], Wo.rearrange("(c p) n -> p c n", p=P)),
            (conv_w[:, 0, :], conv_wk[0:128, :]), (conv_w[:, 1, :], conv_wq[0:128, :]),
            (conv_w[0:64, 2, :], conv_wk[128:192, :]), (conv_w[0:64, 3, :], conv_wq[128:192, :]),
            (conv_w[:, 4:7, :], conv_wv.rearrange("(c p) n -> p c n", p=P)),
            (ab_bias[:, 0:NH], dt_bias.rearrange("(a n) -> a n", a=1).broadcast_to([P, NH])),
            (expA[:, :], A_log.rearrange("(a n) -> a n", a=1).broadcast_to([P, NH])),
            (norm_w[:, :], norm_weight.rearrange("(a n) -> a n", a=1).broadcast_to([P, DV])),
        ]
        loads2 = [
            (xw_in[:, 0, :], theta_w), (xw_in[:, 1, :], phi_w), (xw_in[:, 2, :], g_w),
            (ow_in[:, :], out_w), (th_b[:, :], theta_b.rearrange("(n a) -> n a", a=1)),
            (ph_b[:, :], phi_b.rearrange("(n a) -> n a", a=1)),
            (g_bb[:, :], g_b.rearrange("(a n) -> a n", a=1).broadcast_to([P, LAT])),
            (gamma[:, :], ln_gamma), (beta_ln[:, :], ln_beta),
            (o_b[:, :], out_b.rearrange("(n a) -> n a", a=1)),
        ]
        W1_ALL, W2_ALL = 16 * len(loads1), 16 * len(loads2)

        @block.sync
        def _(sp):
            sp.dma_start(x_h[:, :, :], x[0:HALF].rearrange("b p n -> p b n")).then_inc(x_loaded[0], 16)
            for dst, src in loads1:
                sp.dma_start(dst, src).then_inc(w_loaded, 16)
            for dst, src in loads2:
                sp.dma_start(dst, src).then_inc(w_loaded2, 16)
            sp.dma_start(wn.rearrange("p (t n) -> p t n", t=8),
                         gate_w.rearrange("(t p) n -> p t n", p=P)).then_inc(wn_loaded, 16)
            sp.wait_ge(wscaled, 1)
            sp.dma_start(wn.rearrange("p (t n) -> p t n", t=8),
                         up_w.rearrange("(t p) n -> p t n", p=P)).then_inc(wn_loaded, 16)
            sp.wait_ge(wscaled, 2)
            sp.dma_start(wn.rearrange("p (t n) -> p t n", t=2),
                         down_w.rearrange("(t p) n -> p t n", p=P)).then_inc(wn_loaded, 16)
            sp.wait_ge(x1_ready, HALF)
            sp.dma_start(x_h[:, :, :], x[HALF:SEQ].rearrange("b p n -> p b n")).then_inc(x_loaded[1], 16)
            sp.wait_ge(stage1_done, 1)
            with sp.Fori(0, SEQ // 2) as it:
                for s in range(2):
                    sp.dma_start(S[s]["ctx"][:, :], ctxt[2 * it + s, :, :]).then_inc(c_ctx[s], 16)
                for s in range(2):
                    sp.wait_ge(c_x3[s], it + 1)
                    sp.dma_start(out[2 * it + s, :, :], S[s]["th"][:, 0:HID]).then_inc(c_out[s], 16)
            for s in range(2):
                sp.wait_ge(c_out[s], 16 * (SEQ // 2))

        @block.gpsimd
        def _(pool):
            link = [0]

            def linked(ins):
                link[0] += 1
                ins.then_inc(pool_link, 1)
                pool.wait_ge(pool_link, link[0])

            linked(nc.gpsimd.memset(ident[:, :], 0.0))
            linked(nc.gpsimd.affine_select(out=ident[:, :], in_=ident[:, :], compare_op=ALU.not_equal, fill=1.0,
                                           base=0, pattern=[[-1, P]], channel_multiplier=1))
            linked(nc.gpsimd.memset(upto[:, :], 1.0))
            linked(nc.gpsimd.affine_select(out=upto[:, :], in_=upto[:, :], compare_op=ALU.is_ge, fill=0.0,
                                           base=0, pattern=[[1, P]], channel_multiplier=-1))
            linked(nc.gpsimd.memset(after[:, :], 1.0))
            linked(nc.gpsimd.affine_select(out=after[:, :], in_=after[:, :], compare_op=ALU.is_gt, fill=0.0,
                                           base=0, pattern=[[-1, P]], channel_multiplier=1))
            linked(nc.gpsimd.memset(headsel[:, :], 1.0))
            linked(nc.gpsimd.affine_select(out=headsel[:, :], in_=headsel[:, :], compare_op=ALU.is_ge, fill=0.0,
                                           base=0, pattern=[[-DK, 4]], channel_multiplier=1))
            linked(nc.gpsimd.affine_select(out=headsel[:, :], in_=headsel[:, :], compare_op=ALU.is_ge, fill=0.0,
                                           base=DK - 1, pattern=[[DK, 4]], channel_multiplier=-1))
            linked(nc.gpsimd.memset(mean64[:, :], 1.0 / LAT))
            linked(nc.gpsimd.memset(powers[:, :, 0:NH], 0.5))
            linked(nc.gpsimd.memset(powers[:, :, NH:2 * NH], -0.5))
            linked(nc.gpsimd.memset(mhalf[:, :], -0.5))
            linked(nc.gpsimd.memset(ab_bias[:, NH:2 * NH], 0.0))
            linked(nc.gpsimd.memset(sq[:, 2:4, :], 0.0))
            linked(nc.gpsimd.memset(TTe[:, :, :], 0.0))
            linked(nc.gpsimd.memset(CD[:, :, :], 0.0))
            linked(nc.gpsimd.memset(T[:, :, :], 0.0))
            nc.gpsimd.affine_select(out=T[:, :, :], in_=T[:, :, :], compare_op=ALU.not_equal, fill=1.0,
                                    base=0, pattern=[[1, BLK], [-1, BLK]], channel_multiplier=0).then_inc(consts_ready, 1)

            def weight_prep(n):
                def v(a):
                    return a.rearrange("p (k m) -> p k m", m=BLK)

                pool.wait_ge(wn_loaded, 16 * (n + 1))
                pool.wait_ge(wamax, n + 1)
                if n:
                    name, parts = WPREP[n - 1]
                    pool.wait_ge(psum_full, tiles.at[(name, parts - 1)] + 1)
                nc.gpsimd.tensor_tensor(v(wx), v(wn), wsc[:, 2, :].unsqueeze(2).broadcast_to([P, 64, BLK]), ALU.mult).then_inc(wscaled, 1)
                pool.wait_ge(wscaled, n + 1)
                pool.wait_ge(wmagic, n + 1)
                linked(nc.gpsimd.tensor_tensor(wx, wx, ww, ALU.add))
                linked(nc.gpsimd.tensor_tensor(wx, wx, ww, ALU.subtract))
                nc.gpsimd.tensor_tensor(v(wx), v(wx), wsc[:, 1, :].unsqueeze(2).broadcast_to([P, 64, BLK]), ALU.mult).then_inc(wquant, 1)

            for f in range(2):
                for i in range(4):
                    n = FT[i][1]
                    pool.wait_ge(feat_ready, NFT * f + i + 1)
                    if f:
                        pool.wait_ge(psum_full, tiles.at[(f - 1, "norm")] + 1)
                    nc.gpsimd.tensor_tensor(sq[0:n, i, :], F[0:n, i, :], F[0:n, i, :], ALU.mult).then_inc(squares_ready, 1)
                pool.wait_ge(norms_ready, f + 1)
                nc.gpsimd.tensor_tensor(small[:, 6], small[:, 5], powers[:, :, :], ALU.pow).then_inc(roots_ready, 1)
                for g in range(NQ // 4):
                    wait_drained(pool, (f, "decay", g))
                    nc.gpsimd.tensor_tensor(E[:, 4 * g:4 * g + 4, :], E[:, 4 * g:4 * g + 4, :],
                                            upto[:, :].unsqueeze(1).broadcast_to([P, 4, P]), ALU.mult).then_inc(E_masked, 1)
                wait_drained(pool, (f, "gate", HALF - 1))
                nc.gpsimd.tensor_tensor(SG[:, :, :], SG[:, :, :], norm_w[:, :].unsqueeze(1).broadcast_to([P, NQ, DV]),
                                        ALU.mult).then_inc(gatew_ready, 1)
                pool.wait_ge(gatew_ready, f + 1)
                pool.wait_ge(diag_copied, 4 * (f + 1))
                for g in range(4):
                    r = slice(BLK * g, BLK * g + BLK)
                    if g:
                        pool.wait_ge(diag_zeroed, 4 * f + g)
                    nc.gpsimd.memset(MP[r, :, 0, BLK * g:BLK * g + BLK], 0.0).then_inc(diag_zeroed, 1)
                pool.wait_ge(diag_zeroed, 4 * (f + 1))
                if f == 0:
                    weight_prep(0)
                pool.wait_ge(ms_ready, f + 1)
                nc.gpsimd.tensor_tensor(small[:, 9, :, 0:NH], small[:, 8, :, 0:NH],
                                        mhalf[:, :].rearrange("p (b h) -> p b h", b=HALF), ALU.pow).then_inc(rms_ready, 1)
                pool.wait_ge(var_ready, f + 1)
                nc.gpsimd.tensor_tensor(mv[:, :, 1], mv[:, :, 1], mhalf[:, 0:HALF], ALU.pow).then_inc(rstd_ready, 1)
                if f == 0:
                    weight_prep(1)
                    weight_prep(2)
            pool.wait_ge(stage1_done, 1)

            with pool.Fori(0, SEQ // 2) as it:
                for s in range(2):
                    pool.wait_ge(x1_ready, SEQ)
                    nc.gpsimd.tensor_copy(S[s]["xb"][:, :], x1[:, bass.ds(2 * it + s, 1), :].rearrange("p a n -> p (a n)")).then_inc(c_xb[s], 1)
                    pool.wait_ge(c_xb[s], it + 1)
                    pool.wait_ge(c_ctx[s], 16 * (it + 1))
                    nc.gpsimd.tensor_tensor(S[s]["xc"][:, :], S[s]["xb"][:, :], S[s]["ctx"][:, :], ALU.add).then_inc(c_xc[s], 1)
                for s in range(2):
                    pool.wait_ge(c_drained["dve"][s], drained_at(it, "var"))
                    nc.gpsimd.tensor_tensor(S[s]["st"][0:LAT, 3:4], S[s]["st"][0:LAT, 2:3], mhalf[0:LAT, 0:1], ALU.pow).then_inc(c_rstd[s], 1)
                for s in range(2):
                    pool.wait_ge(c_v2[s], it + 1)
                    nc.gpsimd.tensor_tensor(S[s]["st"][:, 5:6], S[s]["st"][:, 5:6], mhalf[:, 0:1], ALU.pow).then_inc(c_r2[s], 1)
                for s in range(2):
                    d = S[s]
                    pool.wait_ge(c_magic[s], it + 1)
                    nc.gpsimd.tensor_tensor(d["xq"], d["xq"], d["w"], ALU.add).then_inc(c_hq[s], 1)
                    pool.wait_ge(c_hq[s], 2 * it + 1)
                    nc.gpsimd.tensor_tensor(d["xq"], d["xq"], d["w"], ALU.subtract).then_inc(c_hq[s], 1)
                for s in range(2):
                    pool.wait_ge(c_v3[s], it + 1)
                    nc.gpsimd.tensor_tensor(S[s]["st"][:, 5:6], S[s]["st"][:, 5:6], mhalf[:, 0:1], ALU.pow).then_inc(c_r3[s], 1)

        @block.scalar
        def _(act):
            act.wait_ge(w_loaded, W1_ALL)
            nc.scalar.activation(expA[:, :], expA[:, :], ACT.Exp).then_inc(expA_ready, 1)
            for f in range(2):
                if f:
                    wait_full(act, (f - 1, "gate", HALF - 1))
                wait_full(act, (f, "xT", 0))
                nc.scalar.activation(xT[:, 0, :], bank_of((f, "xT", 0))[:, :], ACT.Copy).then_inc(drained["act"], 1)
                if f:
                    wait_full(act, (f - 1, "kq", 1, NH - 1))
                for i, (_, n) in enumerate(FT):
                    wait_full(act, (f, "feat", i))
                    nc.scalar.activation(F[0:n, i, :], bank_of((f, "feat", i))[0:n, :], ACT.Copy,
                                         scale=conv_w[0:n, i, TAPS - 1:TAPS]).then_inc(conv_started, 1)
                act.wait_ge(ab_abs, f + 1)
                nc.scalar.activation(small[:, 2, :, 0:NH], small[:, 1, :, 0:NH], ACT.Exp).then_inc(ab_exp, 1)
                nc.scalar.activation(small[:, 2, :, NH:2 * NH], small[:, 0, :, NH:2 * NH], ACT.Exp, scale=-1.0).then_inc(ab_exp, 1)
                act.wait_ge(ab_plus, f + 1)
                nc.scalar.activation(small[:, 3, :, 0:NH], small[:, 3, :, 0:NH], ACT.Ln).then_inc(ab_ln, 1)
                for i, (_, n) in enumerate(FT):
                    wait_drained(act, (f, "feat", i))
                    nc.scalar.activation(F[0:n, i, :], F[0:n, i, :], ACT.Silu).then_inc(feat_ready, 1)
                for b in range(HALF):
                    wait_full(act, (f, "gate", b))
                    if f and b == 0:
                        act.wait_ge(og_ready, f)
                    nc.scalar.activation(SG[:, NH * b:NH * b + NH, :].rearrange("p h d -> p (h d)"),
                                         bank_of((f, "gate", b))[:, 0:NH * DV], ACT.Silu).then_inc(drained["act"], 1)
                for g in range(NQ // 4):
                    wait_full(act, (f, "decay", g))
                    if f and g == 0:
                        act.wait_ge(inverse_out, f)
                    nc.scalar.activation(E[:, 4 * g:4 * g + 4, :].rearrange("p q t -> p (q t)"),
                                         bank_of((f, "decay", g))[:, :], ACT.Exp).then_inc(drained["act"], 1)
                wait_drained(act, (f, "kq", 1, NH - 1))
                for g in range(4):
                    r = slice(BLK * g, BLK * g + BLK)
                    nc.scalar.activation(CD[r, :, 0:NQ].rearrange("p c q -> p q c"), MP[r, :, 0, BLK * g:BLK * g + BLK],
                                         ACT.Copy).then_inc(diag_copied, 1)
                act.wait_ge(inverse_out, f + 1)
                for g in range(4):
                    r = slice(BLK * g, BLK * g + BLK)
                    nc.scalar.activation(TTe[r, :, BLK * g:BLK * g + BLK], CT[r, :, 0:NQ].rearrange("p c q -> p q c"),
                                         ACT.Copy).then_inc(inverse_ready, 1)

                def rows(a, g):
                    return a[:, 8 * g:8 * g + 8, :].rearrange("p q d -> p (q d)")
                for g in range(NQ // 8):
                    wait_full(act, (f, "y0", g))
                    if f and g == 0:
                        act.wait_ge(og_ready, f)
                    nc.scalar.activation(rows(Y0, g), bank_of((f, "y0", g))[:, :], ACT.Copy).then_inc(drained["act"], 1)
                for k in range(1, P // BLK):
                    for g in range(NQ // 8):
                        wait_full(act, (f, "r", k, g))
                        if k > 1:
                            wait_full(act, (f, "z", k - 1, g))
                        nc.scalar.activation(rows(R, g), bank_of((f, "r", k, g))[:, :], ACT.Copy).then_inc(drained["act"], 1)
                wait_drained(act, (f, "z", P // BLK - 1, NQ // 8 - 1))
                for g in range(NQ // 8):
                    wait_full(act, (f, "o", g))
                    nc.scalar.activation(rows(osq, g), bank_of((f, "o", g))[:, :], ACT.Square).then_inc(o_squared, 1)
                    nc.scalar.activation(rows(osb, g), bank_of((f, "o", g))[:, :], ACT.Copy).then_inc(drained["act"], 1)
                for b in range(HALF):
                    wait_full(act, (f, "ogT", b))
                    if f and b == 0:
                        wait_full(act, (f - 1, "y", HALF - 1))
                    nc.scalar.activation(ogT[:, b, :, :].rearrange("p c t -> p (c t)"),
                                         bank_of((f, "ogT", b))[:, 0:3 * P], ACT.Copy).then_inc(drained["act"], 1)
                if f == 0:
                    for name, parts in WPREP:
                        for i in range(parts):
                            wait_full(act, (name, i))
                            src = bank_of((name, i))
                            if name == "dw":
                                dst = downT[:, 2 * i:2 * i + 2, :].rearrange("p k n -> p (k n)")
                            else:
                                dst = (gateT if name == "gw" else upT)[:, i % 2, 512 * (i // 2):512 * (i // 2) + 512]
                            nc.scalar.activation(dst, src[:, :], ACT.Copy).then_inc(drained["act"], 1)

            with act.Fori(0, SEQ // 2) as it:
                for s in range(2):
                    d = S[s]
                    act.wait_ge(c_max[s], it + 1)
                    for t in range(2):
                        ins = nc.scalar.activation(d["p"][:, t, :], slot_bank(s, "sc")[:, HID * t:HID * t + HID], ACT.Exp,
                                                   bias=d["sm"][:, t:t + 1], accum_out=d["sm"][:, 2 + t:3 + t])
                        ins.then_inc(c_exp[s] if t == 0 else c_drained["act"][s], 1)
                for s in range(2):
                    act.wait_ge(c_full[s], full_at(it, "pT"))
                    nc.scalar.activation(S[s]["pT"].rearrange("p k t -> p (k t)"), slot_bank(s, "pT")[:, :],
                                         ACT.Copy).then_inc(c_drained["act"][s], 1)
                for s in range(2):
                    act.wait_ge(c_aff[s], it + 1)
                    nc.scalar.activation(S[s]["h1"][:, :], S[s]["h1"][:, :], ACT.Relu).then_inc(c_relu[s], 1)
                for s in range(2):
                    act.wait_ge(c_full[s], full_at(it, "x2T"))
                    nc.scalar.activation(S[s]["x2T"].rearrange("p k t -> p (k t)"), slot_bank(s, "x2T")[:, 0:HID],
                                         ACT.Copy).then_inc(c_drained["act"][s], 1)
                for j in range(2):
                    for s in range(2):
                        act.wait_ge(c_full[s], full_at(it, f"gate{j}"))
                        nc.scalar.activation(S[s]["th"][:, 512 * j:512 * j + 512], slot_bank(s, f"gate{j}")[:, :],
                                             ACT.Tanh, scale=0.5).then_inc(c_tanh[s], 1)
                for j in range(2):
                    for s in range(2):
                        act.wait_ge(c_full[s], full_at(it, f"hT{j}"))
                        nc.scalar.activation(S[s]["hT"][:, 4 * j:4 * j + 4, :].rearrange("p k t -> p (k t)"),
                                             slot_bank(s, f"hT{j}")[:, :], ACT.Copy).then_inc(c_drained["act"][s], 1)
                for s in range(2):
                    act.wait_ge(c_out[s], 16 * (it + 1))

        @block.vector
        def _(dve):
            link = [0]

            def linked(ins):
                link[0] += 1
                ins.then_inc(dve_link, 1)
                dve.wait_ge(dve_link, link[0])

            def weight_scales(n):
                dve.wait_ge(wn_loaded, 16 * (n + 1))
                if n:
                    dve.wait_ge(wquant, n)
                linked(nc.vector.tensor_reduce(wsc[:, 0, :], wn.rearrange("p (k m) -> p k m", m=BLK), X, ALU.max,
                                               apply_absolute_value=True))
                linked(nc.vector.tensor_scalar(wsc[:, 1, :], wsc[:, 0, :], 1.0 / FP8_MAX, SCALE_MIN, ALU.mult, ALU.max))
                nc.vector.reciprocal(wsc[:, 2, :], wsc[:, 1, :]).then_inc(wamax, 1)

            def weight_magic(n):
                dve.wait_ge(wscaled, n + 1)
                linked(nc.vector.tensor_scalar(ww.bitcast(I32), wx.bitcast(I32), EXP_MASK, HALF_BIT,
                                               ALU.bitwise_and, ALU.bitwise_or))
                nc.vector.tensor_scalar(ww, ww, 1.5 * MIN_NORMAL, MAGIC_SHIFT, ALU.max, ALU.mult).then_inc(wmagic, 1)

            dve.wait_ge(w_loaded, W1_ALL)
            dve.wait_ge(consts_ready, 1)
            for f in range(2):
                if f:
                    wait_full(dve, (f - 1, "gate", HALF - 1))
                wait_full(dve, (f, "xT", 1))
                nc.vector.tensor_copy(xT[:, 1, :], bank_of((f, "xT", 1))[:, :]).then_inc(drained["dve"], 1)
                wait_full(dve, (f, "ab"))
                nc.vector.tensor_tensor(small[:, 0], bank_of((f, "ab"))[:, 0:HALF * 2 * NH].rearrange("p (b n) -> p b n", b=HALF),
                                        ab_bias[:, :].unsqueeze(1).broadcast_to([P, HALF, 2 * NH]), ALU.add).then_inc(drained["dve"], 1)
                wait_drained(dve, (f, "ab"))
                nc.vector.scalar_tensor_tensor(small[:, 1], small[:, 0], -1.0, small[:, 0], ALU.mult, ALU.min).then_inc(ab_abs, 1)
                for i, (_, n) in enumerate(FT):
                    src = bank_of((f, "feat", i))[0:n, :].rearrange("p (b t) -> p b t", b=HALF)
                    dst = F[0:n, i, :].rearrange("p (b t) -> p b t", b=HALF)
                    dve.wait_ge(conv_started, NFT * f + i + 1)
                    for tap in range(TAPS - 2, -1, -1):
                        d = TAPS - 1 - tap
                        ins = nc.vector.scalar_tensor_tensor(dst[:, :, d:P], src[:, :, 0:P - d], conv_w[0:n, i, tap:tap + 1],
                                                             dst[:, :, d:P], ALU.mult, ALU.add)
                        if tap:
                            linked(ins)
                    ins.then_inc(drained["dve"], 1)
                    if i == 0:
                        dve.wait_ge(ab_exp, 2 * (f + 1))
                        nc.vector.tensor_scalar(small[:, 3], small[:, 2], 1.0, None, ALU.add).then_inc(ab_plus, 1)
                dve.wait_ge(ab_plus, f + 1)
                linked(nc.vector.reciprocal(small[:, 4, :, NH:2 * NH], small[:, 3, :, NH:2 * NH]))
                dve.wait_ge(ab_ln, f + 1)
                linked(nc.vector.scalar_tensor_tensor(small[:, 4, :, 0:NH], small[:, 0, :, 0:NH], 0.0, small[:, 3, :, 0:NH],
                                                      ALU.max, ALU.add))
                dve.wait_ge(expA_ready, 1)
                linked(nc.vector.scalar_tensor_tensor(small[:, 4, :, 0:NH], small[:, 4, :, 0:NH], -1.0,
                                                      expA[:, :].unsqueeze(1).broadcast_to([P, HALF, NH]), ALU.mult, ALU.mult))
                if f:
                    wait_full(dve, (f - 1, "o", NQ // 8 - 1))
                for q in range(NQ):
                    ins = nc.vector.tensor_scalar(GU[:, q, :], upto[:, :], small[:, 4, q // NH, q % NH:q % NH + 1], None, ALU.mult)
                ins.then_inc(GU_ready, 1)
                wait_full(dve, (f, "norm"))
                nc.vector.tensor_copy(small[:, 5], bank_of((f, "norm"))[:, 0:HALF * 2 * NH].rearrange("p (b n) -> p b n", b=HALF)).then_inc(drained["dve"], 1)
                wait_drained(dve, (f, "norm"))
                nc.vector.reciprocal(small[:, 7, :, 0:NH], small[:, 5, :, 0:NH]).then_inc(norms_ready, 1)
                dve.wait_ge(norms_ready, f + 1)
                linked(nc.vector.tensor_tensor(small[:, 7, :, 0:NH], small[:, 7, :, 0:NH], small[:, 4, :, NH:2 * NH], ALU.mult))
                dve.wait_ge(roots_ready, f + 1)
                if f:
                    wait_full(dve, (f - 1, "y", HALF - 1))
                for b in range(HALF):
                    wait_full(dve, (f, "vT", b))
                    nc.vector.tensor_tensor(u[:, NH * b:NH * b + NH, :], bank_of((f, "vT", b))[:, 0:NH * DV].rearrange("p (h d) -> p h d", h=NH),
                                            small[:, 6, b, 0:NH].unsqueeze(2).broadcast_to([P, NH, DV]), ALU.mult).then_inc(drained["dve"], 1)
                wait_full(dve, (f, "decay", NQ // 4 - 1))
                dve.wait_ge(E_masked, 6 * (f + 1))
                for j in range(HALF // 2):
                    for h in range(NH):
                        wait_full(dve, (f, "kq", j, h))
                        for k in range(2):
                            b = 2 * j + k
                            q = NH * b + h
                            src = bank_of((f, "kq", j, h))[:, 256 * k:256 * k + 256].rearrange("p (a t) -> p a t", a=2)
                            ins = nc.vector.scalar_tensor_tensor(MP[:, q], src, small[:, 7, b, h:h + 1],
                                                                 E[:, q, :].unsqueeze(1).broadcast_to([P, 2, P]), ALU.mult, ALU.mult)
                        ins.then_inc(drained["dve"], 1)
                if f == 0:
                    weight_scales(0)
                dve.wait_ge(diag_copied, 4 * (f + 1))
                linked(nc.vector.transpose(L[:, :, :].rearrange("p c j -> p (c j)"), CD[:, :, :].rearrange("p c q -> p (c q)")))
                M2 = L[:, :, :].rearrange("p (a t) (b j) -> p a b t j", a=2, b=2)
                T2 = T[:, :, :].rearrange("p (a t) (b j) -> p a b t j", a=2, b=2)
                for t in range(1, 16):
                    pr = prod[:, 0:2 * t * t].rearrange("p (a c j) -> p a c j", a=2, c=t)
                    for a in range(2):
                        ins = nc.vector.tensor_tensor(pr[:, a], M2[:, a, a, t, 0:t].unsqueeze(1).broadcast_to([P, t, t]),
                                                      T2[:, a, a, 0:t, 0:t].rearrange("p j c -> p c j"), ALU.mult)
                    linked(ins)
                    for a in range(2):
                        ins = nc.vector.tensor_reduce(T2[:, a, a, t, 0:t], pr[:, a], X, ALU.add, negate=True)
                    linked(ins)
                for dst, lhs, rhs, neg in [(Wl[:, :, :], M2[:, 1, 0], T2[:, 0, 0], False), (T2[:, 1, 0], T2[:, 1, 1], Wl[:, :, :], True)]:
                    for t0 in range(0, 16, 8):
                        pr = prod[:, 0:2048].rearrange("p (t c j) -> p t c j", t=8, c=16)
                        for t in range(8):
                            ins = nc.vector.tensor_tensor(pr[:, t], lhs[:, t0 + t, :].unsqueeze(1).broadcast_to([P, 16, 16]),
                                                          rhs.rearrange("p j c -> p c j"), ALU.mult)
                        linked(ins)
                        linked(nc.vector.tensor_reduce(dst[:, t0:t0 + 8, :], pr, X, ALU.add, negate=neg))
                if f:
                    dve.wait_ge(inverse_ready, 4 * f)
                nc.vector.transpose(CT[:, :, :].rearrange("p c q -> p (c q)"), T[:, :, :].rearrange("p t j -> p (t j)")).then_inc(inverse_out, 1)
                if f == 0:
                    weight_magic(0)
                for k in range(1, P // BLK):
                    for g in range(NQ // 8):
                        wait_full(dve, (f, "z", k, g))
                        sl = slice(8 * g, 8 * g + 8)
                        nc.vector.tensor_tensor(om[:, sl, :], Y0[:, sl, :], bank_of((f, "z", k, g))[:, :].rearrange("p (q d) -> p q d", q=8),
                                                ALU.subtract).then_inc(drained["dve"], 1)
                dve.wait_ge(o_squared, 3 * (f + 1))
                s8 = small[:, 8, :, 0:NH]
                rq = small[:, 6, :, NH:2 * NH]
                linked(nc.vector.tensor_reduce(s8, osq[:, :, :].rearrange("p (b h) d -> p b h d", b=HALF), X, ALU.add))
                linked(nc.vector.tensor_tensor(s8, s8, rq, ALU.mult))
                linked(nc.vector.scalar_tensor_tensor(s8, s8, 1.0 / (DV * DK), rq, ALU.mult, ALU.mult))
                nc.vector.tensor_scalar(s8, s8, EPS, None, ALU.add).then_inc(ms_ready, 1)
                dve.wait_ge(rms_ready, f + 1)
                s9 = small[:, 9, :, 0:NH]
                linked(nc.vector.scalar_tensor_tensor(s9, s9, float(DK) ** -0.5, rq, ALU.mult, ALU.mult))
                wait_drained(dve, (f, "o", NQ // 8 - 1))
                dve.wait_ge(gatew_ready, f + 1)
                linked(nc.vector.tensor_tensor(osq[:, :, :].rearrange("p (b h) d -> p b h d", b=HALF), osb[:, :, :].rearrange("p (b h) d -> p b h d", b=HALF),
                                               s9.unsqueeze(3).broadcast_to([P, HALF, NH, DV]), ALU.mult))
                nc.vector.tensor_tensor(osb[:, :, :], osq[:, :, :], SG[:, :, :], ALU.mult).then_inc(og_ready, 1)
                for b in range(HALF):
                    wait_full(dve, (f, "y", b))
                    nc.vector.tensor_tensor(x_h[:, b, :], x_h[:, b, :], bank_of((f, "y", b))[:, 0:HID], ALU.add).then_inc(drained["dve"], 1)
                    wait_drained(dve, (f, "y", b))
                    linked(nc.vector.bn_stats(stats[:, b, :], x_h[:, b, :]))
                    linked(nc.vector.bn_aggr(mv[:, b, :], stats[:, b, :]))
                nc.vector.tensor_scalar(mv[:, :, 1], mv[:, :, 1], EPS, None, ALU.add).then_inc(var_ready, 1)
                dve.wait_ge(rstd_ready, f + 1)
                for b in range(HALF):
                    nc.vector.tensor_scalar(x1[:, HALF * f + b, :], x_h[:, b, :], mv[:, b, 0:1], mv[:, b, 1:2], ALU.subtract, ALU.mult).then_inc(x1_ready, 1)
                if f == 0:
                    for n in range(1, 3):
                        weight_scales(n)
                        weight_magic(n)

            dve.wait_ge(stage1_done, 1)
            nc.vector.tensor_copy(xw[:, :, :], bank[0][:, 0:3 * LAT].rearrange("p (i l) -> p i l", i=3)).then_inc(xw_ready, 1)
            nc.vector.tensor_copy(owT[:, :], bank[1][0:LAT, 0:P]).then_inc(xw_ready, 1)
            base = link[0]
            LINKS = 2 * 23

            with dve.Fori(0, SEQ // 2) as it:
                link[0] = 0

                def clinked(ins):
                    link[0] += 1
                    ins.then_inc(dve_link, 1)
                    dve.wait_ge(dve_link, it * LINKS + (base + link[0]))

                for s in range(2):
                    d = S[s]
                    dve.wait_ge(w_loaded2, W2_ALL)
                    dve.wait_ge(c_full[s], full_at(it, "thph"))
                    ps = slot_bank(s, "thph")
                    clinked(nc.vector.tensor_scalar(d["thph"][:, 0, :], ps[0:LAT, 0:HID], th_b[:, 0:1], None, ALU.add))
                    nc.vector.tensor_scalar(d["thph"][:, 1, :], ps[0:LAT, HID:2 * HID], ph_b[:, 0:1], None, ALU.add).then_inc(c_drained["dve"][s], 1)
                    dve.wait_ge(c_full[s], full_at(it, "g"))
                    nc.vector.tensor_tensor(d["g"][:, :, :], slot_bank(s, "g")[:, 0:2 * LAT].rearrange("p (k l) -> p k l", k=2),
                                            g_bb[:, :].unsqueeze(1).broadcast_to([P, 2, LAT]), ALU.add).then_inc(c_drained["dve"][s], 1)
                for s in range(2):
                    dve.wait_ge(c_full[s], full_at(it, "sc"))
                    nc.vector.tensor_reduce(S[s]["sm"][:, 0:2], slot_bank(s, "sc")[:, :].rearrange("p (t s) -> p t s", t=2), X, ALU.max,
                                            negate=True).then_inc(c_max[s], 1)
                for s in range(2):
                    d = S[s]
                    dve.wait_ge(c_drained["act"][s], drained_at(it, "sc"))
                    clinked(nc.vector.reciprocal(d["sm"][:, 4:6], d["sm"][:, 2:4]))
                    for t in range(2):
                        ins = nc.vector.tensor_scalar(d["p"][:, t, :], d["p"][:, t, :], d["sm"][:, 4 + t:5 + t], None, ALU.mult)
                        ins.then_inc(c_pn[s], 1)
                for s in range(2):
                    d = S[s]
                    dve.wait_ge(c_full[s], full_at(it, "tx"))
                    clinked(nc.vector.bn_stats(d["bs"][0:LAT, :], slot_bank(s, "tx")[0:LAT, 0:HID]))
                    nc.vector.memset(d["sm"][:, 8:9], 0.0)
                    nc.vector.bn_aggr(d["st"][0:LAT, 0:2], d["bs"][0:LAT, :]).then_inc(c_mean[s], 1)
                for s in range(2):
                    d = S[s]
                    dve.wait_ge(c_mean[s], it + 1)
                    dve.wait_ge(c_full[s], full_at(it, "mu"))
                    clinked(nc.vector.tensor_copy(d["st"][0:LAT, 4:5], slot_bank(s, "mu")[0:LAT, 0:1]))
                    nc.vector.scalar_tensor_tensor(d["h1"], slot_bank(s, "tx")[0:LAT, 0:HID], d["st"][0:LAT, 4:5], gamma[:, :],
                                                   ALU.subtract, ALU.mult).then_inc(c_drained["dve"][s], 1)
                    nc.vector.tensor_tensor(d["st"][0:LAT, 6:7], d["st"][0:LAT, 0:1], slot_bank(s, "mu")[0:LAT, 0:1], ALU.subtract).then_inc(c_drained["dve"][s], 1)
                    dve.wait_ge(c_drained["dve"][s], drained_at(it, "mu"))
                    clinked(nc.vector.tensor_tensor(d["st"][0:LAT, 6:7], d["st"][0:LAT, 6:7], d["st"][0:LAT, 6:7], ALU.mult))
                    nc.vector.tensor_tensor(d["st"][0:LAT, 1:2], d["st"][0:LAT, 1:2], d["st"][0:LAT, 6:7], ALU.add).then_inc(c_dev[s], 1)
                for s in range(2):
                    d = S[s]
                    dve.wait_ge(c_full[s], full_at(it, "var"))
                    nc.vector.tensor_scalar(d["st"][0:LAT, 2:3], slot_bank(s, "var")[0:LAT, 0:1], EPS, None, ALU.add).then_inc(c_drained["dve"][s], 1)
                    dve.wait_ge(c_rstd[s], it + 1)
                    nc.vector.scalar_tensor_tensor(d["h1"][:, :], d["h1"][:, :], d["st"][0:LAT, 3:4], beta_ln[:, :], ALU.mult, ALU.add).then_inc(c_aff[s], 1)
                for s in range(2):
                    d = S[s]
                    dve.wait_ge(c_xc[s], it + 1)
                    dve.wait_ge(c_full[s], full_at(it, "ow"))
                    nc.vector.scalar_tensor_tensor(d["x2"][:, :], slot_bank(s, "ow")[:, 0:HID], o_b[:, 0:1], d["xc"][:, :], ALU.add, ALU.add).then_inc(c_drained["dve"][s], 1)
                    dve.wait_ge(c_drained["dve"][s], drained_at(it, "ow"))
                    clinked(nc.vector.bn_stats(d["bs"][:, :], d["x2"][:, :]))
                    nc.vector.memset(d["sm"][:, 8:9], 0.0)
                    clinked(nc.vector.bn_aggr(d["st"][:, 4:6], d["bs"][:, :]))
                    nc.vector.tensor_scalar(d["st"][:, 5:6], d["st"][:, 5:6], EPS, None, ALU.add).then_inc(c_v2[s], 1)

                def quantise(s, src, xq, w, nb, scaled=None):
                    d = S[s]
                    v = src.rearrange("p (k m) -> p k m", m=BLK)
                    qs = d["qs"]
                    clinked(nc.vector.tensor_reduce(qs[:, 0, 0:nb], v, X, ALU.max, apply_absolute_value=True))
                    clinked(nc.vector.tensor_scalar(qs[:, 1, 0:nb], qs[:, 0, 0:nb], 1.0 / FP8_MAX, SCALE_MIN, ALU.mult, ALU.max))
                    clinked(nc.vector.reciprocal(qs[:, 2, 0:nb], qs[:, 1, 0:nb]))
                    clinked(nc.vector.tensor_tensor(xq.rearrange("p (k m) -> p k m", m=BLK), v,
                                                    qs[:, 2, 0:nb].unsqueeze(2).broadcast_to([P, nb, BLK]), ALU.mult))
                    clinked(nc.vector.tensor_scalar(w.bitcast(I32), xq.bitcast(I32), EXP_MASK, HALF_BIT, ALU.bitwise_and, ALU.bitwise_or))
                    return nc.vector.tensor_scalar(w, w, 1.5 * MIN_NORMAL, MAGIC_SHIFT, ALU.max, ALU.mult)

                def dequantise(s, xq, nb):
                    v = xq.rearrange("p (k m) -> p k m", m=BLK)
                    return nc.vector.tensor_tensor(v, v, S[s]["qs"][:, 1, 0:nb].unsqueeze(2).broadcast_to([P, nb, BLK]), ALU.mult)

                for s in range(2):
                    d = S[s]
                    dve.wait_ge(c_r2[s], it + 1)
                    nc.vector.tensor_scalar(d["x2"][:, :], d["x2"][:, :], d["st"][:, 4:5], d["st"][:, 5:6], ALU.subtract, ALU.mult).then_inc(c_x2[s], 1)
                    dve.wait_ge(c_x2[s], it + 1)
                    clinked(quantise(s, d["x2"][:, :], d["xq"][:, 0:HID], d["xw"], HID // BLK))
                    clinked(nc.vector.tensor_tensor(d["xq"][:, 0:HID], d["xq"][:, 0:HID], d["xw"], ALU.add))
                    clinked(nc.vector.tensor_tensor(d["xq"][:, 0:HID], d["xq"][:, 0:HID], d["xw"], ALU.subtract))
                    dequantise(s, d["xq"][:, 0:HID], HID // BLK).then_inc(c_dq[s], 1)
                for s in range(2):
                    d = S[s]
                    for j in range(2):
                        c = slice(512 * j, 512 * j + 512)
                        dve.wait_ge(c_tanh[s], 2 * it + j + 1)
                        nc.vector.scalar_tensor_tensor(d["hh"][:, c], d["th"][:, c], 1.0, slot_bank(s, f"gate{j}")[:, :], ALU.add, ALU.mult).then_inc(c_drained["dve"][s], 1)
                        dve.wait_ge(c_drained["dve"][s], drained_at(it, f"gate{j}"))
                        dve.wait_ge(c_full[s], full_at(it, f"up{j}"))
                        nc.vector.tensor_tensor(d["hh"][:, c], d["hh"][:, c], slot_bank(s, f"up{j}")[:, :], ALU.mult).then_inc(c_drained["dve"][s], 1)
                    dve.wait_ge(c_drained["dve"][s], drained_at(it, "up1"))
                    clinked(nc.vector.tensor_scalar(d["hh"], d["hh"], 0.5, None, ALU.mult))
                    quantise(s, d["hh"], d["xq"], d["w"], INTER // BLK).then_inc(c_magic[s], 1)
                for s in range(2):
                    d = S[s]
                    dve.wait_ge(c_hq[s], 2 * it + 2)
                    dequantise(s, d["xq"], INTER // BLK).then_inc(c_hdq[s], 1)
                for s in range(2):
                    d = S[s]
                    dve.wait_ge(c_full[s], full_at(it, "dn"))
                    nc.vector.tensor_tensor(d["x2"][:, :], d["x2"][:, :], slot_bank(s, "dn")[:, 0:HID], ALU.add).then_inc(c_drained["dve"][s], 1)
                    dve.wait_ge(c_drained["dve"][s], drained_at(it, "dn"))
                    clinked(nc.vector.bn_stats(d["bs"][:, :], d["x2"][:, :]))
                    nc.vector.memset(d["sm"][:, 8:9], 0.0)
                    clinked(nc.vector.bn_aggr(d["st"][:, 4:6], d["bs"][:, :]))
                    nc.vector.tensor_scalar(d["st"][:, 5:6], d["st"][:, 5:6], EPS, None, ALU.add).then_inc(c_v3[s], 1)
                for s in range(2):
                    d = S[s]
                    dve.wait_ge(c_r3[s], it + 1)
                    nc.vector.tensor_scalar(d["th"][:, 0:HID], d["x2"][:, :], d["st"][:, 4:5], d["st"][:, 5:6], ALU.subtract, ALU.mult).then_inc(c_x3[s], 1)
                assert link[0] == LINKS, link[0]

        @block.tensor
        def _(pe):
            mm, tr = nc.tensor.matmul, nc.tensor.transpose
            pe.wait_ge(w_loaded, W1_ALL)
            pe.wait_ge(consts_ready, 1)
            for f in range(2):
                pe.wait_ge(x_loaded[f], 16)
                for c in range(2):
                    wait_free(pe, (f, "xT", c))
                    for b in range(HALF):
                        ins = tr(bank_of((f, "xT", c))[:, P * b:P * b + P], x_h[:, b, P * c:P * c + P], ident[:, :])
                    ins.then_inc(psum_full, 1)
                for c in range(2):
                    wait_drained(pe, (f, "xT", c))
                wait_free(pe, (f, "ab"))
                for b in range(HALF):
                    for c in range(2):
                        ins = mm(bank_of((f, "ab"))[:, 2 * NH * b:2 * NH * (b + 1)], xT[:, c, P * b:P * b + P], W_ab[:, c, :],
                                 start=(c == 0), stop=(c == 1))
                ins.then_inc(psum_full, 1)
                for i, (at, n) in enumerate(FT):
                    wait_free(pe, (f, "feat", i))
                    for c in range(2):
                        ins = mm(bank_of((f, "feat", i))[0:n, :], W_f[:, c, at:at + n], xT[:, c, :], start=(c == 0), stop=(c == 1))
                    ins.then_inc(psum_full, 1)
                for b in range(HALF):
                    wait_free(pe, (f, "gate", b))
                    for c in range(2):
                        ins = mm(bank_of((f, "gate", b))[:, 0:NH * DV], xT[:, c, P * b:P * b + P], W_g[:, c, :], start=(c == 0), stop=(c == 1))
                    ins.then_inc(psum_full, 1)
                pe.wait_ge(squares_ready, 4 * (f + 1))
                wait_free(pe, (f, "norm"))
                for b in range(HALF):
                    for i, (c0, m) in enumerate([(0, 4), (6, 4), (4, 2), (10, 2)]):
                        c0 += 2 * NH * b
                        ins = mm(bank_of((f, "norm"))[:, c0:c0 + m], sq[:, i, P * b:P * b + P], headsel[:, 0:m], start=True, stop=True)
                ins.then_inc(psum_full, 1)
                pe.wait_ge(GU_ready, f + 1)
                for g in range(NQ // 4):
                    wait_free(pe, (f, "decay", g))
                    ins = mm(bank_of((f, "decay", g))[:, :], after[:, :], GU[:, 4 * g:4 * g + 4, :], start=True, stop=True)
                    ins.then_inc(psum_full, 1)
                pe.wait_ge(feat_ready, NFT * (f + 1))
                for b in range(HALF):
                    wait_free(pe, (f, "vT", b))
                    for c in range(3):
                        ins = tr(bank_of((f, "vT", b))[:, P * c:P * c + P], F[:, 4 + c, P * b:P * b + P], ident[:, :])
                    ins.then_inc(psum_full, 1)
                for j in range(HALF // 2):
                    for h in range(NH):
                        wait_free(pe, (f, "kq", j, h))
                        r = slice(DK * (h % 4), DK * (h % 4) + DK)
                        i = 2 * (h // 4)
                        for k in range(2):
                            t = slice(P * (2 * j + k), P * (2 * j + k) + P)
                            ins = mm(bank_of((f, "kq", j, h))[:, 256 * k:256 * k + 256], F[r, i, t], F[r, i:i + 2, t], start=True, stop=True)
                        ins.then_inc(psum_full, 1)

                def products(key, lhs, rhs, g):
                    wait_free(pe, key)
                    for q in range(8 * g, 8 * g + 8):
                        ins = mm(bank_of(key)[:, DV * (q % 8):DV * (q % 8) + DV], lhs(q), rhs[:, q, :], start=True, stop=True)
                    ins.then_inc(psum_full, 1)
                wait_drained(pe, (f, "vT", HALF - 1))
                pe.wait_ge(inverse_ready, 4 * (f + 1))
                for g in range(NQ // 8):
                    products((f, "y0", g), lambda q: TTe[:, q, :], u, g)
                pe.wait_ge(diag_zeroed, 4 * (f + 1))
                for k in range(1, P // BLK):
                    for g in range(NQ // 8):
                        wait_drained(pe, (f, "y0", g) if k == 1 else (f, "z", k - 1, g))
                        products((f, "r", k, g), lambda q: MP[:, q, 0, :], Y0 if k == 1 else om, g)
                    for g in range(NQ // 8):
                        wait_drained(pe, (f, "r", k, g))
                        products((f, "z", k, g), lambda q: TTe[:, q, :], R, g)
                for g in range(NQ // 8):
                    wait_drained(pe, (f, "z", P // BLK - 1, g))
                    products((f, "o", g), lambda q: MP[:, q, 1, :], om, g)
                pe.wait_ge(og_ready, f + 1)
                for b in range(HALF):
                    wait_free(pe, (f, "ogT", b))
                    og = osb[:, NH * b:NH * b + NH, :].rearrange("p h d -> p (h d)")
                    for c in range(3):
                        ins = tr(bank_of((f, "ogT", b))[:, P * c:P * c + P], og[:, P * c:P * c + P], ident[:, :])
                    ins.then_inc(psum_full, 1)
                for b in range(HALF):
                    wait_drained(pe, (f, "ogT", b))
                    wait_free(pe, (f, "y", b))
                    for c in range(3):
                        ins = mm(bank_of((f, "y", b))[:, 0:HID], ogT[:, b, c, :], W_o[:, c, :], start=(c == 0), stop=(c == 2))
                    ins.then_inc(psum_full, 1)
                if f == 0:
                    for n, (name, parts) in enumerate(WPREP):
                        pe.wait_ge(wquant, n + 1)
                        for i in range(parts):
                            wait_free(pe, (name, i))
                            for m in range(4):
                                if name == "dw":
                                    k, t = 2 * i + m // 2, m % 2
                                    src = wx[:, INTER * t + P * k:INTER * t + P * k + P]
                                else:
                                    c, t = i % 2, 4 * (i // 2) + m
                                    src = wx[:, HID * t + P * c:HID * t + P * c + P]
                                ins = tr(bank_of((name, i))[:, P * m:P * m + P], src, ident[:, :])
                            ins.then_inc(psum_full, 1)
            pe.wait_ge(w_loaded2, W2_ALL)
            pe.wait_ge(drained["dve"], tiles.count["dve"])
            pe.wait_ge(drained["act"], tiles.count["act"])
            for i in range(3):
                tr(bank[0][:, LAT * i:LAT * i + LAT], xw_in[:, i, :], ident[0:LAT, 0:LAT])
            tr(bank[1][0:LAT, 0:P], ow_in[:, :], ident[:, :]).then_inc(stage1_done, 1)
            pe.wait_ge(xw_ready, 2)
            with pe.Fori(0, SEQ // 2) as it:
                for s in range(2):
                    d = S[s]
                    wait_slot_free(pe, s, it, "thph")
                    pe.wait_ge(c_ctx[s], 16 * (it + 1))
                    pe.wait_ge(c_xb[s], it + 1)
                    ps = slot_bank(s, "thph")
                    mm(ps[0:LAT, 0:HID], xw[:, 0, :], d["ctx"][:, :], start=True, stop=True)
                    mm(ps[0:LAT, HID:2 * HID], xw[:, 1, :], d["xb"][:, :], start=True, stop=True).then_inc(c_full[s], 1)
                    wait_slot_free(pe, s, it, "g")
                    for t in range(2):
                        ins = mm(slot_bank(s, "g")[:, LAT * t:LAT * t + LAT], d["xb"][:, P * t:P * t + P], xw[:, 2, :], start=True, stop=True)
                    ins.then_inc(c_full[s], 1)
                for s in range(2):
                    d = S[s]
                    wait_slot_free(pe, s, it, "sc")
                    pe.wait_ge(c_drained["dve"][s], drained_at(it, "thph"))
                    for t in range(2):
                        ins = mm(slot_bank(s, "sc")[:, HID * t:HID * t + HID], d["thph"][:, 0, P * t:P * t + P], d["thph"][:, 1, :], start=True, stop=True)
                    ins.then_inc(c_full[s], 1)
                for s in range(2):
                    wait_slot_free(pe, s, it, "pT")
                    pe.wait_ge(c_pn[s], 2 * (it + 1))
                    for k in range(2):
                        for t in range(2):
                            ins = tr(slot_bank(s, "pT")[:, HID * k + P * t:HID * k + P * t + P], S[s]["p"][:, t, P * k:P * k + P], ident[:, :])
                    ins.then_inc(c_full[s], 1)
                for s in range(2):
                    wait_slot_free(pe, s, it, "tx")
                    pe.wait_ge(c_drained["act"][s], drained_at(it, "pT"))
                    pe.wait_ge(c_drained["dve"][s], drained_at(it, "g"))
                    for k in range(2):
                        ins = mm(slot_bank(s, "tx")[0:LAT, 0:HID], S[s]["g"][:, k, :], S[s]["pT"][:, k, :], start=(k == 0), stop=(k == 1))
                    ins.then_inc(c_full[s], 1)
                for s in range(2):
                    wait_slot_free(pe, s, it, "mu")
                    pe.wait_ge(c_mean[s], it + 1)
                    mm(slot_bank(s, "mu")[:, 0:1], mean64[:, :], S[s]["st"][0:LAT, 0:1], start=True, stop=True).then_inc(c_full[s], 1)
                for s in range(2):
                    wait_slot_free(pe, s, it, "var")
                    pe.wait_ge(c_dev[s], it + 1)
                    mm(slot_bank(s, "var")[:, 0:1], mean64[:, :], S[s]["st"][0:LAT, 1:2], start=True, stop=True).then_inc(c_full[s], 1)
                for s in range(2):
                    wait_slot_free(pe, s, it, "ow")
                    pe.wait_ge(c_relu[s], it + 1)
                    mm(slot_bank(s, "ow")[:, 0:HID], owT[:, :], S[s]["h1"][:, :], start=True, stop=True).then_inc(c_full[s], 1)
                for s in range(2):
                    wait_slot_free(pe, s, it, "x2T")
                    pe.wait_ge(c_dq[s], it + 1)
                    for k in range(2):
                        ins = tr(slot_bank(s, "x2T")[:, P * k:P * k + P], S[s]["xq"][:, P * k:P * k + P], ident[:, :])
                    ins.then_inc(c_full[s], 1)
                for j in range(2):
                    for s in range(2):
                        if j == 0:
                            pe.wait_ge(c_drained["act"][s], drained_at(it, "x2T"))
                        for name, wt in (("gate", gateT), ("up", upT)):
                            wait_slot_free(pe, s, it, f"{name}{j}")
                            for k in range(2):
                                ins = mm(slot_bank(s, f"{name}{j}")[:, :], S[s]["x2T"][:, k, :], wt[:, k, 512 * j:512 * j + 512],
                                         start=(k == 0), stop=(k == 1))
                            ins.then_inc(c_full[s], 1)
                for j in range(2):
                    for s in range(2):
                        wait_slot_free(pe, s, it, f"hT{j}")
                        pe.wait_ge(c_hdq[s], it + 1)
                        for m in range(4):
                            k = 4 * j + m
                            ins = tr(slot_bank(s, f"hT{j}")[:, P * m:P * m + P], S[s]["xq"][:, P * k:P * k + P], ident[:, :])
                        ins.then_inc(c_full[s], 1)
                for s in range(2):
                    wait_slot_free(pe, s, it, "dn")
                    pe.wait_ge(c_drained["act"][s], drained_at(it, "hT1"))
                    for k in range(INTER // P):
                        ins = mm(slot_bank(s, "dn")[:, 0:HID], S[s]["hT"][:, k, :], downT[:, k, :], start=(k == 0), stop=(k == INTER // P - 1))
                    ins.then_inc(c_full[s], 1)
                for s in range(2):
                    pe.wait_ge(c_drained["act"][s], (it + 1) * ST_N["act"])
                    pe.wait_ge(c_drained["dve"][s], (it + 1) * ST_N["dve"])


_INS = ["x", "ctx_2048", "L0_attn_Wq", "L0_attn_Wk", "L0_attn_Wv", "L0_attn_Wa", "L0_attn_Wb", "L0_attn_Wg", "L0_attn_Wo",
        "L0_attn_conv_wq", "L0_attn_conv_wk", "L0_attn_conv_wv", "L0_attn_A_log", "L0_attn_dt_bias",
        "L0_attn_norm_weight", "L0_xattn_theta_w", "L0_xattn_theta_b", "L0_xattn_phi_w", "L0_xattn_phi_b",
        "L0_xattn_g_w", "L0_xattn_g_b", "L0_xattn_ln_gamma", "L0_xattn_ln_beta", "L0_xattn_out_w",
        "L0_xattn_out_b", "L0_ffn_gate_w", "L0_ffn_up_w", "L0_ffn_down_w"]


def kernel(**inputs):
    import numpy as np
    import concourse.bacc as bacc
    from concourse.bass_utils import run_bass_kernel_spmd

    nc = bacc.Bacc("TRN2", target_bir_lowering=False, num_devices=1)
    arrays, args = {}, []
    for name in _INS:
        a = np.ascontiguousarray(inputs[name])
        arrays[f"in_{name}"] = a
        args.append(nc.dram_tensor(f"in_{name}", a.shape, mybir.dt.from_np(a.dtype), kind="ExternalInput").ap())
    args.append(nc.dram_tensor("out", (SEQ, P, HID), F32, kind="ExternalOutput").ap())
    program(nc, *args)
    r = run_bass_kernel_spmd(nc, [arrays], core_ids=[0])
    return r.results[0]["out"]
```

```python
from contextlib import ExitStack

import concourse.bass as bass
from concourse import mybir

F32 = mybir.dt.float32
I32 = mybir.dt.int32
ALU = mybir.AluOpType
ACT = mybir.ActivationFunctionType
X = mybir.AxisListType.X

P = 128
SEQ = 8
HALF = 4
HID = 256
NH, DK, DV = 6, 32, 64
TAPS = 4
NQ = HALF * NH
GQ = 8
LAT, INTER = 64, 1024
BLK = 32
SUB = 16
NBANK = 8
EPS = 1e-5
FP8_MAX, SCALE_MIN = 448.0, 1e-30
MIN_NORMAL = 2.0 ** -6
MAGIC_SHIFT = 2.0 ** 20
EXP_MASK, HALF_BIT = 0x7F800000, 0x00400000
DIAG = SUB * BLK + SUB

FT = [(0, 128), (128, 128), (256, 64), (320, 64), (384, 128), (512, 128), (640, 128)]
NFT = len(FT)
ROWS = [(1, 6), (6, 10), (10, 13), (13, 16)]

SEQ_STAGES = ["project", "scores", "attend", "mix", "stats", "centre", "spread", "affine", "residual",
              "quantise", "gate_up", "quantise_h", "transpose_h", "down", "final"]


def chains():
    c = {"w": [(k, n) for n in range(3) for k in ("w_scale", "w_magic", "w_T")] + [("xw",)]}
    for f in range(2):
        c["AB"[f]] = ([("xT", f)] + [("feat", f, i) for i in range(NFT)] + [("feat_end", f), ("norm", f)]
                      + [("kq", f, j, h) for j in range(HALF // 2) for h in range(NH)]
                      + [("diag", f)] + [("rows", f, i) for i in range(len(ROWS))]
                      + [("below", f, i) for i in range(2)] + [("inverse", f)]
                      + [("solve", f, k) for k in range(P // BLK)]
                      + [("o", f), ("og", f), ("y", f), ("x1", f)])
        c["ab"[f]] = ([("gate", f, b) for b in range(HALF)] + [("ab", f), ("decay_in", f)]
                      + [("decay", f, g) for g in range(NQ // 4)])
        c["uv"[f]] = [("vT", f, b) for b in range(HALF)]
    for n in range(SEQ):
        c[str(n)] = [(k, n) for k in SEQ_STAGES]
    return c


INTERLEAVE = (
    "AwAaaaaawaAAAAaaaaaaAAwAwAAAAAAAAAwAAAAuuuuAwBAAAAAwAAwBAAAAAwBwBABABbAB0101bb0101001b0110"
    "1bBb0B10bb1B001bb010bb101B12BB2B323BB23B2B323B22B3BBvv3v2B23BB3BBvB23BB23BBB2B3B2B3B2B3345"
    "6475647456457544564656457646756745674757564764756745675767")


def order():
    left = chains()
    stages = [left[c].pop(0) for c in INTERLEAVE]
    assert not any(left.values())
    return stages


def tiles_of(stage):
    k, a = stage[0], stage[1:]
    if k == "xT":
        return [(stage + (c,), "act") for c in range(2)]
    if k == "solve":
        r = [("r",) + a + (g,) for g in range(NQ // GQ)] if a[1] else []
        return [(t, "dve") for t in r] + [(("w",) + a + (g,), "act") for g in range(NQ // GQ)]
    if k == "o":
        return [(stage + (g,), "act") for g in range(NQ // GQ)]
    if k == "og":
        return [(stage + (b,), "act") for b in range(HALF)]
    if k == "y":
        return [(stage + (b,), "dve") for b in range(HALF)]
    if k == "w_T":
        return [(stage + (i,), "act") for i in range(4)]
    if k == "xw":
        return [(("xw", 0), "dve"), (("xw", 1), "dve")]
    if k == "project":
        return [(("thph",) + a, "act"), (("g",) + a, "dve")]
    if k == "gate_up":
        return [((n,) + a + (j,), r) for j in range(2) for n, r in (("gate_h", "act"), ("up_h", "dve"))]
    if k == "transpose_h":
        return [(stage + (j,), "act") for j in range(2)]
    reader = {"gate": "act", "feat": "dve", "decay": "act", "norm": "dve", "vT": "dve", "kq": "dve",
              "scores": "act", "attend": "act", "mix": "act", "centre": "dve", "spread": "dve",
              "residual": "dve", "quantise": "act",
              "down": "dve"}.get(k)
    return [(stage, reader)] if reader else []


class Tiles:

    def __init__(self, stages):
        self.at, self.drain, self.count = {}, [], {"act": 0, "dve": 0}
        for stage in stages:
            for key, reader in tiles_of(stage):
                self.at[key] = len(self.drain)
                self.count[reader] += 1
                self.drain.append((reader, self.count[reader]))


def program(nc, x, ctxt, Wq, Wk, Wv, Wa, Wb, Wg, Wo, conv_wq, conv_wk, conv_wv, A_log, dt_bias,
            norm_weight, theta_w, theta_b, phi_w, phi_b, g_w, g_b, ln_gamma, ln_beta, out_w,
            out_b, gate_w, up_w, down_w, out):
    STAGES = order()
    tiles = Tiles(STAGES)
    slot_of = [0, 1, 0, 1, 0, 1, 2, 3]

    with ExitStack() as stack:
        def sb(name, shape, dt=F32):
            return stack.enter_context(nc.sbuf_tensor(name, shape, dt))

        def sem(name):
            return stack.enter_context(nc.semaphore(name))

        bank = [stack.enter_context(nc.psum_tensor(f"bank{i}", [P, 512], F32)) for i in range(NBANK)]

        ident = sb("ident", [P, P])
        upto = sb("upto", [P, P])
        after = sb("after", [P, P])
        headsel = sb("headsel", [P, 4])
        mean64 = sb("mean64", [LAT, LAT])
        powers = sb("powers", [P, HALF, 2 * NH])
        mhalf = sb("mhalf", [P, NQ])
        W_f = sb("W_f", [P, 2, 768])
        W_g = sb("W_g", [P, 2, NH * DV + 2 * NH])
        W_o = sb("W_o", [P, 3, HID])
        conv_w = sb("conv_w", [P, NFT, TAPS])
        dt_b = sb("dt_b", [P, NH])
        expA = sb("expA", [P, NH])
        norm_w = sb("norm_w", [P, DV])
        gateT = sb("gateT", [P, 2, INTER])
        upT = sb("upT", [P, 2, INTER])
        downT = sb("downT", [P, INTER // P, HID])
        xw_in = sb("xw_in", [LAT, 3, P])
        xw = sb("xw", [P, 3, LAT])
        ow_in = sb("ow_in", [P, LAT])
        owT = sb("owT", [LAT, P])
        th_b = sb("th_b", [LAT, 1])
        ph_b = sb("ph_b", [LAT, 1])
        g_bb = sb("g_bb", [P, LAT])
        gamma = sb("gamma", [LAT, HID])
        beta_ln = sb("beta_ln", [LAT, HID])
        o_b = sb("o_b", [P, 1])

        xs = sb("xs", [P, SEQ, HID])
        ctx = sb("ctx", [P, SEQ, HID])
        xT = sb("xT", [P, 2, 512])
        Fm = sb("Fm", [P, 3584])
        F = Fm[:, :].rearrange("p (i t) -> p i t", i=NFT)
        SG = sb("SG", [P, NQ, DV])
        MPm = sb("MPm", [P, NQ * 2 * P])
        MP = MPm[:, :].rearrange("p (q a t) -> p q a t", q=NQ, a=2)
        Em = sb("Em", [P, NQ * P])
        E = Em[:, :].rearrange("p (q t) -> p q t", q=NQ)
        CD = sb("CD", [P, BLK, BLK])
        L = sb("L", [P, 2 * DIAG])
        T = sb("T", [P, 2 * DIAG])
        CT = CD
        TT = sb("TT", [P, NQ, BLK])
        Wl = sb("Wl", [P, SUB, SUB])
        u = sb("u", [P, NQ, DV])
        Rom = sb("Rom", [P, 2, NQ * DV])
        R, om = (Rom[:, i, :].rearrange("p (q d) -> p q d", q=NQ) for i in range(2))
        small = sb("small", [P, 10, HALF, 2 * NH])
        stats = sb("stats", [P, HALF, 6])
        mv = sb("mv", [P, HALF, 2])
        sq = Rom[:, :, :].rearrange("p a n -> p (a n)")[:, 0:4 * 512].rearrange("p (i t) -> p i t", i=4)
        GU = MPm[:, 0:NQ * P].rearrange("p (q t) -> p q t", q=NQ)
        prod = Em
        osb = R
        ogT = u[:, :, :].rearrange("p q d -> p (q d)").rearrange("p (b c t) -> p b c t", b=HALF, c=3)
        osq = om

        arena = sb("arena", [P, 3 * 2048])
        wn, wx, ww = (arena[:, 2048 * i:2048 * i + 2048] for i in range(3))
        wsc = sb("wsc", [P, 3, 64])
        ffn = sb("ffn", [P, 2 * 3072])

        S = []
        for s, (a, b) in enumerate([(arena[:, 0:3072], ffn[:, 0:3072]), (arena[:, 3072:6144], ffn[:, 3072:6144]),
                                    (MPm[:, 0:3072], MPm[:, 3072:6144]), (Fm[:, 0:3072], Em[:, :])]):
            d = {n: sb(f"{n}{s}", shape) for n, shape in [("sm", [P, 8]), ("st", [P, 8]), ("bs", [P, 6]), ("qs", [P, 3, 32])]}
            d["xc"], d["x2"] = a[:, 0:256], a[:, 256:512]
            d["thph"] = a[0:LAT, 512:1024].rearrange("p (k t) -> p k t", k=2)
            d["p"] = a[:, 1024:1536].rearrange("p (k t) -> p k t", k=2)
            d["pT"] = a[:, 1536:2048].rearrange("p (k t) -> p k t", k=2)
            d["g"] = a[:, 2048:2176].rearrange("p (k t) -> p k t", k=2)
            d["h1"] = a[0:LAT, 2176:2432]
            d["x2T"] = a[:, 2432:2688].rearrange("p (k t) -> p k t", k=2)
            d["hh"], d["xq"], d["w"] = b[:, 0:1024], b[:, 1024:2048], b[:, 2048:3072]
            d["hT"] = d["w"].rearrange("p (k t) -> p k t", k=INTER // P)
            S.append(d)

        x_loaded = [sem(f"x_loaded{f}") for f in range(2)]
        wf_loaded, wg_loaded, conv_loaded, wo_loaded = (sem(n) for n in ("wf_loaded", "wg_loaded", "conv_loaded", "wo_loaded"))
        small_loaded, cross_loaded, ctx_loaded, wn_loaded = (sem(n) for n in ("small_loaded", "cross_loaded", "ctx_loaded", "wn_loaded"))
        consts_ready = sem("consts_ready")
        psum_full = sem("psum_full")
        drained = {"act": sem("act_drained"), "dve": sem("dve_drained")}
        dve_link, pool_link = sem("dve_link"), sem("pool_link")
        (expA_ready, ab_raw, ab_biased, ab_abs, ab_exp, ab_plus, ab_ln, g_ready, conv_started, feat_ready, squares_ready, norms_ready,
         roots_ready, GU_ready, E_masked, gatew_ready, diag_copied, inverse_out, inverse_ready, o_squared,
         ms_ready, rms_ready, og_ready, var_ready, rstd_ready, x1_ready, wamax, wscaled, wmagic, wquant) = (sem(n) for n in (
             "expA_ready", "ab_raw", "ab_biased", "ab_abs", "ab_exp", "ab_plus", "ab_ln", "g_ready", "conv_started", "feat_ready",
             "squares_ready", "norms_ready", "roots_ready", "GU_ready", "E_masked", "gatew_ready",
             "diag_copied", "inverse_out", "inverse_ready", "o_squared", "ms_ready", "rms_ready", "og_ready",
             "var_ready", "rstd_ready", "x1_ready", "wamax", "wscaled", "wmagic", "wquant"))
        (xc_ready, max_ready, sum_ready, p_ready, mean_ready, dev_ready, spread_rstd, affine_ready, relu_ready,
         var2_ready, rstd2_ready, x2_ready, xdq_ready, magic_ready, hrounded, hdq_ready,
         var3_ready, rstd3_ready, final_ready) = (sem(n) for n in (
             "xc_ready", "max_ready", "sum_ready", "p_ready", "mean_ready", "dev_ready", "spread_rstd", "affine_ready",
             "relu_ready", "var2_ready", "rstd2_ready", "x2_ready", "xdq_ready", "magic_ready",
             "hrounded", "hdq_ready", "var3_ready", "rstd3_ready", "final_ready"))
        out_stored = [sem(f"out_stored{s}") for s in range(4)]

        block = stack.enter_context(nc.Block())

        def bank_of(key):
            return bank[tiles.at[key] % NBANK]

        def wait_free(pe, key):
            n = tiles.at[key] - NBANK
            if n >= 0:
                reader, count = tiles.drain[n]
                pe.wait_ge(drained[reader], count)

        def wait_full(eng, key):
            eng.wait_ge(psum_full, tiles.at[key] + 1)

        def wait_drained(eng, key):
            reader, count = tiles.drain[tiles.at[key]]
            eng.wait_ge(drained[reader], count)

        def wait_out_stored(eng, n):
            before = [m for m in range(n) if slot_of[m] == slot_of[n]]
            if before:
                eng.wait_ge(out_stored[slot_of[n]], 16 * len(before))

        def group(a, g, rows=slice(0, P)):
            return a[rows, GQ * g:GQ * g + GQ, :].rearrange("p q d -> p (q d)")

        def run(parts):
            for stage in STAGES:
                if stage[0] in parts:
                    parts[stage[0]](*stage[1:])

        def rows_p(w):
            return w.rearrange("(c p) n -> p c n", p=P)

        def row_everywhere(w, n):
            return w.rearrange("(a n) -> a n", a=1).broadcast_to([P, n])

        loads = {
            wf_loaded: [(W_f[:, :, 0:128], rows_p(Wk)[:, :, 0:128]), (W_f[:, :, 128:256], rows_p(Wq)[:, :, 0:128]),
                        (W_f[:, :, 256:320], rows_p(Wk)[:, :, 128:192]), (W_f[:, :, 320:384], rows_p(Wq)[:, :, 128:192]),
                        (W_f[:, :, 384:768], rows_p(Wv))],
            wg_loaded: [(W_g[:, :, 0:NH * DV], rows_p(Wg)), (W_g[:, :, NH * DV:NH * DV + NH], rows_p(Wa)),
                        (W_g[:, :, NH * DV + NH:], rows_p(Wb))],
            conv_loaded: [(conv_w[:, 0, :], conv_wk[0:128, :]), (conv_w[:, 1, :], conv_wq[0:128, :]),
                          (conv_w[0:64, 2, :], conv_wk[128:192, :]), (conv_w[0:64, 3, :], conv_wq[128:192, :]),
                          (conv_w[:, 4:7, :], rows_p(conv_wv))],
            small_loaded: [(dt_b[:, :], row_everywhere(dt_bias, NH)), (expA[:, :], row_everywhere(A_log, NH)),
                           (norm_w[:, :], row_everywhere(norm_weight, DV))],
            wo_loaded: [(W_o[:, :, :], rows_p(Wo))],
            cross_loaded: [(xw_in[:, 0, :], theta_w), (xw_in[:, 1, :], phi_w), (xw_in[:, 2, :], g_w), (ow_in[:, :], out_w),
                           (th_b[:, :], theta_b.rearrange("(n a) -> n a", a=1)),
                           (ph_b[:, :], phi_b.rearrange("(n a) -> n a", a=1)),
                           (g_bb[:, :], row_everywhere(g_b, LAT)), (gamma[:, :], ln_gamma), (beta_ln[:, :], ln_beta),
                           (o_b[:, :], out_b.rearrange("(n a) -> n a", a=1))],
        }
        loaded = {k: 16 * len(v) for k, v in loads.items()}

        @block.sync
        def _(sp):
            def x_half(f):
                b = slice(HALF * f, HALF * f + HALF)
                sp.dma_start(xs[:, b, :], x[b].rearrange("b p n -> p b n")).then_inc(x_loaded[f], 16)
            x_half(0)
            for dst, src in loads[wf_loaded]:
                sp.dma_start(dst, src).then_inc(wf_loaded, 16)
            for k in (small_loaded, wo_loaded):
                for dst, src in loads[k]:
                    sp.dma_start(dst, src).then_inc(k, 16)
            sp.dma_start(wn.rearrange("p (t n) -> p t n", t=8), rows_p(gate_w)).then_inc(wn_loaded, 16)
            x_half(1)
            sp.dma_start(ctx[:, :, :], ctxt.rearrange("b p n -> p b n")).then_inc(ctx_loaded, 16)
            for dst, src in loads[cross_loaded]:
                sp.dma_start(dst, src).then_inc(cross_loaded, 16)
            sp.wait_ge(wscaled, 1)
            sp.dma_start(wn.rearrange("p (t n) -> p t n", t=8), rows_p(up_w)).then_inc(wn_loaded, 16)
            sp.wait_ge(wscaled, 2)
            sp.dma_start(wn.rearrange("p (t n) -> p t n", t=2), rows_p(down_w)).then_inc(wn_loaded, 16)

            def final(n):
                sp.wait_ge(final_ready, n + 1)
                sp.dma_start(out[n, :, :], S[slot_of[n]]["x2"]).then_inc(out_stored[slot_of[n]], 16)
            run({"final": final})
            for s in range(4):
                sp.wait_ge(out_stored[s], 16 * slot_of.count(s))

        @block.gpsimd
        def _(pool):
            link = [0]

            def linked(ins):
                link[0] += 1
                ins.then_inc(pool_link, 1)
                pool.wait_ge(pool_link, link[0])

            linked(nc.gpsimd.memset(ident[:, :], 0.0))
            linked(nc.gpsimd.affine_select(out=ident[:, :], in_=ident[:, :], compare_op=ALU.not_equal, fill=1.0,
                                           base=0, pattern=[[-1, P]], channel_multiplier=1))
            linked(nc.gpsimd.memset(upto[:, :], 1.0))
            linked(nc.gpsimd.affine_select(out=upto[:, :], in_=upto[:, :], compare_op=ALU.is_ge, fill=0.0,
                                           base=0, pattern=[[1, P]], channel_multiplier=-1))
            linked(nc.gpsimd.memset(after[:, :], 1.0))
            linked(nc.gpsimd.affine_select(out=after[:, :], in_=after[:, :], compare_op=ALU.is_gt, fill=0.0,
                                           base=0, pattern=[[-1, P]], channel_multiplier=1))
            linked(nc.gpsimd.memset(headsel[:, :], 1.0))
            linked(nc.gpsimd.affine_select(out=headsel[:, :], in_=headsel[:, :], compare_op=ALU.is_ge, fill=0.0,
                                           base=0, pattern=[[-DK, 4]], channel_multiplier=1))
            linked(nc.gpsimd.affine_select(out=headsel[:, :], in_=headsel[:, :], compare_op=ALU.is_ge, fill=0.0,
                                           base=DK - 1, pattern=[[DK, 4]], channel_multiplier=-1))
            linked(nc.gpsimd.memset(mean64[:, :], 1.0 / LAT))
            linked(nc.gpsimd.memset(powers[:, :, 0:NH], 0.5))
            linked(nc.gpsimd.memset(powers[:, :, NH:2 * NH], -0.5))
            linked(nc.gpsimd.memset(mhalf[:, :], -0.5))
            linked(nc.gpsimd.memset(CD[:, :, :], 0.0))
            linked(nc.gpsimd.memset(T[:, :], 0.0))
            Tm = T[:, 0:BLK * BLK].rearrange("p (t j) -> p t j", t=BLK)
            nc.gpsimd.affine_select(out=Tm, in_=Tm, compare_op=ALU.not_equal, fill=1.0,
                                    base=0, pattern=[[1, BLK], [-1, BLK]], channel_multiplier=0).then_inc(consts_ready, 1)

            def blocks(a):
                return a.rearrange("p (k m) -> p k m", m=BLK)

            def w_scale(n):
                pool.wait_ge(wn_loaded, 16 * (n + 1))
                pool.wait_ge(wamax, n + 1)
                if n:
                    wait_full(pool, ("w_T", n - 1, 3))
                nc.gpsimd.tensor_tensor(blocks(wx), blocks(wn), wsc[:, 2, :].unsqueeze(2).broadcast_to([P, 64, BLK]), ALU.mult).then_inc(wscaled, 1)

            def w_magic(n):
                pool.wait_ge(wscaled, n + 1)
                pool.wait_ge(wmagic, n + 1)
                linked(nc.gpsimd.tensor_tensor(wx, wx, ww, ALU.add))
                linked(nc.gpsimd.tensor_tensor(wx, wx, ww, ALU.subtract))
                nc.gpsimd.tensor_tensor(blocks(wx), blocks(wx), wsc[:, 1, :].unsqueeze(2).broadcast_to([P, 64, BLK]), ALU.mult).then_inc(wquant, 1)

            def feat(f, i):
                if 1 <= i <= 4:
                    n = FT[i - 1][1]
                    pool.wait_ge(feat_ready, NFT * f + i)
                    if f:
                        wait_full(pool, ("og", f - 1, HALF - 1))
                    nc.gpsimd.tensor_tensor(sq[0:n, i - 1, :], F[0:n, i - 1, :], F[0:n, i - 1, :], ALU.mult).then_inc(squares_ready, 1)

            def decay(f, g):
                wait_drained(pool, ("decay", f, g))
                nc.gpsimd.tensor_tensor(E[:, 4 * g:4 * g + 4, :], E[:, 4 * g:4 * g + 4, :],
                                        upto[:, :].unsqueeze(1).broadcast_to([P, 4, P]), ALU.mult).then_inc(E_masked, 1)

            def norm(f):
                pool.wait_ge(norms_ready, f + 1)
                nc.gpsimd.tensor_tensor(small[:, 6], small[:, 5], powers[:, :, :], ALU.pow).then_inc(roots_ready, 1)

            def diag(f):
                pool.wait_ge(small_loaded, loaded[small_loaded])
                wait_drained(pool, ("gate", f, HALF - 1))
                nc.gpsimd.tensor_tensor(SG[:, :, :], SG[:, :, :], norm_w[:, :].unsqueeze(1).broadcast_to([P, NQ, DV]),
                                        ALU.mult).then_inc(gatew_ready, 1)

            def o(f):
                pool.wait_ge(ms_ready, f + 1)
                nc.gpsimd.tensor_tensor(small[:, 9, :, 0:NH], small[:, 8, :, 0:NH],
                                        mhalf[:, :].rearrange("p (b h) -> p b h", b=HALF), ALU.pow).then_inc(rms_ready, 1)

            def y(f):
                pool.wait_ge(var_ready, f + 1)
                nc.gpsimd.tensor_tensor(mv[:, :, 1], mv[:, :, 1], mhalf[:, 0:HALF], ALU.pow).then_inc(rstd_ready, 1)

            def project(n):
                pool.wait_ge(x1_ready, n + 1)
                pool.wait_ge(ctx_loaded, 16)
                wait_out_stored(pool, n)
                wait_full(pool, ("w_T", 2, 3))
                nc.gpsimd.tensor_tensor(S[slot_of[n]]["xc"], xs[:, n, :], ctx[:, n, :], ALU.add).then_inc(xc_ready, 1)

            def spread(n):
                st = S[slot_of[n]]["st"]
                wait_drained(pool, ("spread", n))
                nc.gpsimd.tensor_tensor(st[0:LAT, 3:4], st[0:LAT, 2:3], mhalf[0:LAT, 0:1], ALU.pow).then_inc(spread_rstd, 1)

            def residual(n):
                st = S[slot_of[n]]["st"]
                pool.wait_ge(var2_ready, n + 1)
                nc.gpsimd.tensor_tensor(st[:, 5:6], st[:, 5:6], mhalf[:, 0:1], ALU.pow).then_inc(rstd2_ready, 1)

            def quantise_h(n):
                d = S[slot_of[n]]
                pool.wait_ge(magic_ready, n + 1)
                nc.gpsimd.tensor_tensor(d["xq"], d["xq"], d["w"], ALU.add).then_inc(hrounded, 1)
                pool.wait_ge(hrounded, 2 * n + 1)
                nc.gpsimd.tensor_tensor(d["xq"], d["xq"], d["w"], ALU.subtract).then_inc(hrounded, 1)

            def down(n):
                st = S[slot_of[n]]["st"]
                pool.wait_ge(var3_ready, n + 1)
                nc.gpsimd.tensor_tensor(st[:, 5:6], st[:, 5:6], mhalf[:, 0:1], ALU.pow).then_inc(rstd3_ready, 1)

            run({"w_scale": w_scale, "w_magic": w_magic, "feat": feat, "decay": decay, "norm": norm, "diag": diag,
                 "o": o, "y": y, "project": project, "spread": spread, "residual": residual,
                 "quantise_h": quantise_h, "down": down})

        @block.scalar
        def _(act):
            for k in (wg_loaded, conv_loaded):
                for dst, src in loads[k]:
                    act.dma_start(dst, src).then_inc(k, 16)

            def copy(dst, src):
                return nc.scalar.activation(dst, src, ACT.Copy)

            def x_T(f):
                if f:
                    wait_full(act, ("feat", f - 1, NFT - 1))
                    wait_full(act, ("gate", f - 1, HALF - 1))
                for c in range(2):
                    wait_full(act, ("xT", f, c))
                    copy(xT[:, c, :], bank_of(("xT", f, c))[:, :]).then_inc(drained["act"], 1)

            def gate(f, b):
                wait_full(act, ("gate", f, b))
                if f and b == 0:
                    act.wait_ge(og_ready, f)
                src = bank_of(("gate", f, b))
                copy(small[:, 0, b, :], src[:, NH * DV:NH * DV + 2 * NH]).then_inc(ab_raw, 1)
                nc.scalar.activation(SG[:, NH * b:NH * b + NH, :].rearrange("p h d -> p (h d)"), src[:, 0:NH * DV],
                                     ACT.Silu).then_inc(drained["act"], 1)

            def ab(f):
                if f == 0:
                    act.wait_ge(small_loaded, loaded[small_loaded])
                    nc.scalar.activation(expA[:, :], expA[:, :], ACT.Exp).then_inc(expA_ready, 1)
                act.wait_ge(ab_abs, f + 1)
                nc.scalar.activation(small[:, 2, :, 0:NH], small[:, 1, :, 0:NH], ACT.Exp).then_inc(ab_exp, 1)
                nc.scalar.activation(small[:, 2, :, NH:2 * NH], small[:, 0, :, NH:2 * NH], ACT.Exp, scale=-1.0).then_inc(ab_exp, 1)
                act.wait_ge(ab_plus, f + 1)
                nc.scalar.activation(small[:, 3, :, 0:NH], small[:, 3, :, 0:NH], ACT.Ln).then_inc(ab_ln, 1)

            def silu_feat(f, i):
                n = FT[i][1]
                wait_drained(act, ("feat", f, i))
                nc.scalar.activation(F[0:n, i, :], F[0:n, i, :], ACT.Silu).then_inc(feat_ready, 1)

            def feat(f, i):
                n = FT[i][1]
                if i == 0:
                    act.wait_ge(conv_loaded, loaded[conv_loaded])
                    if f:
                        wait_full(act, ("kq", f - 1, 1, NH - 1))
                        wait_full(act, ("vT", f - 1, HALF - 1))
                wait_full(act, ("feat", f, i))
                nc.scalar.activation(F[0:n, i, :], bank_of(("feat", f, i))[0:n, :], ACT.Copy,
                                     scale=conv_w[0:n, i, TAPS - 1:TAPS]).then_inc(conv_started, 1)
                if i:
                    silu_feat(f, i - 1)

            def feat_end(f):
                silu_feat(f, NFT - 1)

            def decay_in(f):
                act.wait_ge(consts_ready, 1)
                act.wait_ge(g_ready, f + 1)
                if f:
                    wait_full(act, ("o", f - 1, NQ // GQ - 1))
                for q in range(NQ):
                    ins = nc.scalar.activation(GU[:, q, :], upto[:, :], ACT.Copy, scale=small[:, 4, q // NH, q % NH:q % NH + 1])
                ins.then_inc(GU_ready, 1)

            def decay(f, g):
                wait_full(act, ("decay", f, g))
                if f and g == 0:
                    act.wait_ge(inverse_out, f)
                nc.scalar.activation(E[:, 4 * g:4 * g + 4, :].rearrange("p q t -> p (q t)"),
                                     bank_of(("decay", f, g))[:, :], ACT.Exp).then_inc(drained["act"], 1)

            def diag(f):
                if f:
                    act.wait_ge(inverse_ready, f)
                wait_drained(act, ("kq", f, 1, NH - 1))
                for g in range(P // BLK):
                    r = slice(BLK * g, BLK * g + BLK)
                    copy(CD[r, :, 0:NQ].rearrange("p c q -> p q c"), MP[r, :, 0, r]).then_inc(diag_copied, 1)

            def inverse(f):
                act.wait_ge(inverse_out, f + 1)
                copy(TT[:, :, :], CT[:, :, 0:NQ].rearrange("p c q -> p q c")).then_inc(inverse_ready, 1)

            def solve(f, k):
                r = slice(BLK * k, BLK * k + BLK)
                for g in range(NQ // GQ):
                    wait_full(act, ("w", f, k, g))
                    copy(group(om, g, r), bank_of(("w", f, k, g))[r, :]).then_inc(drained["act"], 1)

            def o(f):
                for g in range(NQ // GQ):
                    wait_full(act, ("o", f, NQ // GQ - 1))
                    nc.scalar.activation(group(osq, g), bank_of(("o", f, g))[:, :], ACT.Square).then_inc(o_squared, 1)
                    copy(group(osb, g), bank_of(("o", f, g))[:, :]).then_inc(drained["act"], 1)

            def og(f):
                for b in range(HALF):
                    wait_full(act, ("og", f, b))
                    copy(ogT[:, b, :, :].rearrange("p c t -> p (c t)"), bank_of(("og", f, b))[:, 0:3 * P]).then_inc(drained["act"], 1)

            def w_T(n):
                for i in range(4):
                    key = ("w_T", n, i)
                    wait_full(act, key)
                    if n == 2:
                        dst = downT[:, 2 * i:2 * i + 2, :].rearrange("p k n -> p (k n)")
                    else:
                        dst = (gateT, upT)[n][:, i % 2, 512 * (i // 2):512 * (i // 2) + 512]
                    copy(dst, bank_of(key)[:, :]).then_inc(drained["act"], 1)

            def project(n):
                act.wait_ge(cross_loaded, loaded[cross_loaded])
                act.wait_ge(xc_ready, n + 1)
                wait_full(act, ("thph", n))
                ps, th = bank_of(("thph", n)), S[slot_of[n]]["thph"]
                nc.scalar.activation(th[:, 0, :], ps[0:LAT, 0:HID], ACT.Identity, bias=th_b[:, 0:1])
                nc.scalar.activation(th[:, 1, :], ps[0:LAT, HID:2 * HID], ACT.Identity, bias=ph_b[:, 0:1]).then_inc(drained["act"], 1)

            def scores(n):
                d = S[slot_of[n]]
                act.wait_ge(max_ready, n + 1)
                for t in range(2):
                    ins = nc.scalar.activation(d["p"][:, t, :], bank_of(("scores", n))[:, HID * t:HID * t + HID], ACT.Exp,
                                               bias=d["sm"][:, t:t + 1], accum_out=d["sm"][:, 2 + t:3 + t])
                    ins.then_inc(sum_ready if t == 0 else drained["act"], 1)

            def attend(n):
                wait_full(act, ("attend", n))
                copy(S[slot_of[n]]["pT"].rearrange("p k t -> p (k t)"), bank_of(("attend", n))[:, :]).then_inc(drained["act"], 1)

            def mix(n):
                wait_full(act, ("mix", n))
                copy(S[slot_of[n]]["h1"], bank_of(("mix", n))[0:LAT, 0:HID]).then_inc(drained["act"], 1)

            def affine(n):
                h1 = S[slot_of[n]]["h1"]
                act.wait_ge(affine_ready, n + 1)
                nc.scalar.activation(h1, h1, ACT.Relu).then_inc(relu_ready, 1)

            def quantise(n):
                wait_full(act, ("quantise", n))
                copy(S[slot_of[n]]["x2T"].rearrange("p k t -> p (k t)"), bank_of(("quantise", n))[:, 0:HID]).then_inc(drained["act"], 1)

            def gate_up(n):
                for j in range(2):
                    wait_full(act, ("gate_h", n, j))
                    nc.scalar.activation(S[slot_of[n]]["hh"][:, 512 * j:512 * j + 512], bank_of(("gate_h", n, j))[:, :],
                                         ACT.Silu).then_inc(drained["act"], 1)

            def transpose_h(n):
                for j in range(2):
                    wait_full(act, ("transpose_h", n, j))
                    copy(S[slot_of[n]]["hT"][:, 4 * j:4 * j + 4, :].rearrange("p k t -> p (k t)"),
                         bank_of(("transpose_h", n, j))[:, :]).then_inc(drained["act"], 1)

            run({"xT": x_T, "gate": gate, "ab": ab, "feat": feat, "feat_end": feat_end, "decay_in": decay_in, "decay": decay, "diag": diag,
                 "inverse": inverse, "solve": solve, "o": o, "og": og, "w_T": w_T, "project": project, "scores": scores,
                 "attend": attend, "mix": mix, "affine": affine, "quantise": quantise, "gate_up": gate_up,
                 "transpose_h": transpose_h})

        @block.vector
        def _(dve):
            link = [0]

            def linked(ins):
                link[0] += 1
                ins.then_inc(dve_link, 1)
                dve.wait_ge(dve_link, link[0])

            def blocks(a):
                return a.rearrange("p (k m) -> p k m", m=BLK)

            def w_scale(n):
                dve.wait_ge(wn_loaded, 16 * (n + 1))
                if n:
                    dve.wait_ge(wquant, n)
                linked(nc.vector.tensor_reduce(wsc[:, 0, :], blocks(wn), X, ALU.max, apply_absolute_value=True))
                linked(nc.vector.tensor_scalar(wsc[:, 1, :], wsc[:, 0, :], 1.0 / FP8_MAX, SCALE_MIN, ALU.mult, ALU.max))
                nc.vector.reciprocal(wsc[:, 2, :], wsc[:, 1, :]).then_inc(wamax, 1)

            def round_to(w, xq):
                linked(nc.vector.tensor_scalar(w.bitcast(I32), xq.bitcast(I32), EXP_MASK, HALF_BIT,
                                               ALU.bitwise_and, ALU.bitwise_or))
                return nc.vector.tensor_scalar(w, w, 1.5 * MIN_NORMAL, MAGIC_SHIFT, ALU.max, ALU.mult)

            def w_magic(n):
                dve.wait_ge(wscaled, n + 1)
                round_to(ww, wx).then_inc(wmagic, 1)

            def ab(f):
                a, b = slice(0, NH), slice(NH, 2 * NH)
                dve.wait_ge(ab_raw, HALF * (f + 1))
                dve.wait_ge(small_loaded, loaded[small_loaded])
                nc.vector.tensor_tensor(small[:, 0, :, a], small[:, 0, :, a], dt_b[:, :].unsqueeze(1).broadcast_to([P, HALF, NH]),
                                        ALU.add).then_inc(ab_biased, 1)
                dve.wait_ge(ab_biased, f + 1)
                nc.vector.scalar_tensor_tensor(small[:, 1, :, a], small[:, 0, :, a], -1.0, small[:, 0, :, a], ALU.mult, ALU.min).then_inc(ab_abs, 1)
                dve.wait_ge(ab_exp, 2 * (f + 1))
                nc.vector.tensor_scalar(small[:, 3], small[:, 2], 1.0, None, ALU.add).then_inc(ab_plus, 1)
                dve.wait_ge(ab_plus, f + 1)
                linked(nc.vector.reciprocal(small[:, 4, :, b], small[:, 3, :, b]))
                dve.wait_ge(ab_ln, f + 1)
                linked(nc.vector.scalar_tensor_tensor(small[:, 4, :, a], small[:, 0, :, a], 0.0, small[:, 3, :, a], ALU.max, ALU.add))
                dve.wait_ge(expA_ready, 1)
                nc.vector.scalar_tensor_tensor(small[:, 4, :, a], small[:, 4, :, a], -1.0,
                                               expA[:, :].unsqueeze(1).broadcast_to([P, HALF, NH]), ALU.mult, ALU.mult).then_inc(g_ready, 1)

            def feat(f, i):
                n = FT[i][1]
                src = bank_of(("feat", f, i))[0:n, :].rearrange("p (b t) -> p b t", b=HALF)
                dst = F[0:n, i, :].rearrange("p (b t) -> p b t", b=HALF)
                dve.wait_ge(conv_started, NFT * f + i + 1)
                for tap in range(TAPS - 2, -1, -1):
                    d = TAPS - 1 - tap
                    ins = nc.vector.scalar_tensor_tensor(dst[:, :, d:P], src[:, :, 0:P - d], conv_w[0:n, i, tap:tap + 1],
                                                         dst[:, :, d:P], ALU.mult, ALU.add)
                    if tap:
                        linked(ins)
                ins.then_inc(drained["dve"], 1)

            def norm(f):
                wait_full(dve, ("norm", f))
                nc.vector.tensor_copy(small[:, 5], bank_of(("norm", f))[:, 0:HALF * 2 * NH].rearrange("p (b n) -> p b n", b=HALF)).then_inc(drained["dve"], 1)
                wait_drained(dve, ("norm", f))
                dve.wait_ge(g_ready, f + 1)
                c = small[:, 7, :, 0:NH]
                nc.vector.reciprocal(c, small[:, 5, :, 0:NH]).then_inc(norms_ready, 1)
                dve.wait_ge(norms_ready, f + 1)
                linked(nc.vector.tensor_tensor(c, c, small[:, 4, :, NH:2 * NH], ALU.mult))

            def vT(f, b):
                dve.wait_ge(roots_ready, f + 1)
                if f and b == 0:
                    wait_full(dve, ("y", f - 1, HALF - 1))
                wait_full(dve, ("vT", f, b))
                nc.vector.tensor_tensor(u[:, NH * b:NH * b + NH, :], bank_of(("vT", f, b))[:, 0:NH * DV].rearrange("p (h d) -> p h d", h=NH),
                                        small[:, 6, b, 0:NH].unsqueeze(2).broadcast_to([P, NH, DV]), ALU.mult).then_inc(drained["dve"], 1)

            def kq(f, j, h):
                if (j, h) == (0, 0):
                    wait_full(dve, ("decay", f, NQ // 4 - 1))
                    dve.wait_ge(E_masked, NQ // 4 * (f + 1))
                wait_full(dve, ("kq", f, j, h))
                for k in range(2):
                    b = 2 * j + k
                    q = NH * b + h
                    src = bank_of(("kq", f, j, h))[:, 2 * P * k:2 * P * k + 2 * P].rearrange("p (a t) -> p a t", a=2)
                    ins = nc.vector.scalar_tensor_tensor(MP[:, q], src, small[:, 7, b, h:h + 1],
                                                         E[:, q, :].unsqueeze(1).broadcast_to([P, 2, P]), ALU.mult, ALU.mult)
                ins.then_inc(drained["dve"], 1)

            def square(a):
                return a[:, 0:BLK * BLK].rearrange("p (t j) -> p t j", t=BLK)

            def diag(f):
                dve.wait_ge(diag_copied, P // BLK * (f + 1))
                linked(nc.vector.transpose(L[:, 0:BLK * BLK], CD[:, :, :].rearrange("p c q -> p (c q)")))

            def rows(f, i):
                M2, T2 = (a[:, :].rearrange("p (a m) -> p a m", a=2) for a in (L, T))
                for t in range(*ROWS[i]):
                    pr = prod[:, 0:2 * t * t].rearrange("p (a c j) -> p a c j", a=2, c=t)
                    above = T2[:, :, 0:BLK * t].rearrange("p a (j c) -> p a c j", c=BLK)[:, :, 0:t, :]
                    linked(nc.vector.tensor_tensor(pr, M2[:, :, BLK * t:BLK * t + t].unsqueeze(2).broadcast_to([P, 2, t, t]),
                                                   above, ALU.mult))
                    linked(nc.vector.tensor_reduce(T2[:, :, BLK * t:BLK * t + t], pr, X, ALU.add, negate=True))

            def product(dst, lhs, rhs, negate):
                (m, k), n = lhs.shape[1:], rhs.shape[2]
                pr = prod[:, 0:m * n * k].rearrange("p (t c j) -> p t c j", t=m, c=n)
                linked(nc.vector.tensor_tensor(pr, lhs.unsqueeze(2).broadcast_to([P, m, n, k]),
                                               rhs.rearrange("p j c -> p c j").unsqueeze(1).broadcast_to([P, m, n, k]), ALU.mult))
                linked(nc.vector.tensor_reduce(dst, pr, X, ALU.add, negate=negate))

            def below(f, i):
                M, Tm, h = square(L), square(T), SUB // 2
                if i == 0:
                    product(Wl[:, :, 0:h], M[:, SUB:, 0:SUB], Tm[:, 0:SUB, 0:h], False)
                    product(Wl[:, :, h:], M[:, SUB:, h:SUB], Tm[:, h:SUB, h:SUB], False)
                else:
                    product(Tm[:, SUB:SUB + h, 0:SUB], Tm[:, SUB:SUB + h, SUB:SUB + h], Wl[:, 0:h, :], True)
                    product(Tm[:, SUB + h:, 0:SUB], Tm[:, SUB + h:, SUB:], Wl[:, :, :], True)

            def inverse(f):
                if f:
                    dve.wait_ge(inverse_ready, f)
                nc.vector.transpose(CT[:, :, :].rearrange("p c q -> p (c q)"), T[:, 0:BLK * BLK]).then_inc(inverse_out, 1)

            def solve(f, k):
                r = slice(BLK * k, BLK * k + BLK)
                if k:
                    for g in range(NQ // GQ):
                        wait_full(dve, ("r", f, k, g))
                        nc.vector.tensor_tensor(group(R, g, r), group(u, g, r), bank_of(("r", f, k, g))[r, :], ALU.subtract).then_inc(drained["dve"], 1)

            def o(f):
                dve.wait_ge(o_squared, NQ // GQ * (f + 1))
                s8, s9, rq = small[:, 8, :, 0:NH], small[:, 9, :, 0:NH], small[:, 6, :, NH:2 * NH]
                linked(nc.vector.tensor_reduce(s8, osq[:, :, :].rearrange("p (b h) d -> p b h d", b=HALF), X, ALU.add))
                linked(nc.vector.tensor_tensor(s8, s8, rq, ALU.mult))
                linked(nc.vector.scalar_tensor_tensor(s8, s8, 1.0 / (DV * DK), rq, ALU.mult, ALU.mult))
                nc.vector.tensor_scalar(s8, s8, EPS, None, ALU.add).then_inc(ms_ready, 1)
                dve.wait_ge(rms_ready, f + 1)
                linked(nc.vector.scalar_tensor_tensor(s9, s9, float(DK) ** -0.5, rq, ALU.mult, ALU.mult))
                wait_drained(dve, ("o", f, NQ // GQ - 1))
                dve.wait_ge(gatew_ready, f + 1)
                linked(nc.vector.tensor_tensor(osq[:, :, :].rearrange("p (b h) d -> p b h d", b=HALF),
                                               osb[:, :, :].rearrange("p (b h) d -> p b h d", b=HALF),
                                               s9.unsqueeze(3).broadcast_to([P, HALF, NH, DV]), ALU.mult))
                nc.vector.tensor_tensor(osb[:, :, :], osq[:, :, :], SG[:, :, :], ALU.mult).then_inc(og_ready, 1)

            def y(f):
                dve.wait_ge(x_loaded[f], 16)
                for b in range(HALF):
                    wait_full(dve, ("y", f, b))
                    xb = xs[:, HALF * f + b, :]
                    nc.vector.tensor_tensor(xb, xb, bank_of(("y", f, b))[:, 0:HID], ALU.add).then_inc(drained["dve"], 1)
                for b in range(HALF):
                    wait_drained(dve, ("y", f, b))
                    ins = nc.vector.bn_stats(stats[:, b, :], xs[:, HALF * f + b, :])
                linked(ins)
                for b in range(HALF):
                    ins = nc.vector.bn_aggr(mv[:, b, :], stats[:, b, :])
                linked(ins)
                nc.vector.tensor_scalar(mv[:, :, 1], mv[:, :, 1], EPS, None, ALU.add).then_inc(var_ready, 1)

            def x1(f):
                dve.wait_ge(rstd_ready, f + 1)
                for b in range(HALF):
                    xb = xs[:, HALF * f + b, :]
                    nc.vector.tensor_scalar(xb, xb, mv[:, b, 0:1], mv[:, b, 1:2], ALU.subtract, ALU.mult).then_inc(x1_ready, 1)

            def xw_T():
                wait_full(dve, ("xw", 1))
                nc.vector.tensor_copy(xw[:, :, :], bank_of(("xw", 0))[:, 0:3 * LAT].rearrange("p (i l) -> p i l", i=3)).then_inc(drained["dve"], 1)
                nc.vector.tensor_copy(owT[:, :], bank_of(("xw", 1))[0:LAT, 0:P]).then_inc(drained["dve"], 1)

            def project(n):
                d = S[slot_of[n]]
                dve.wait_ge(cross_loaded, loaded[cross_loaded])
                dve.wait_ge(xc_ready, n + 1)
                wait_full(dve, ("g", n))
                nc.vector.tensor_tensor(d["g"], bank_of(("g", n))[:, 0:2 * LAT].rearrange("p (k l) -> p k l", k=2),
                                        g_bb[:, :].unsqueeze(1).broadcast_to([P, 2, LAT]), ALU.add).then_inc(drained["dve"], 1)

            def scores(n):
                wait_full(dve, ("scores", n))
                nc.vector.tensor_reduce(S[slot_of[n]]["sm"][:, 0:2], bank_of(("scores", n))[:, :].rearrange("p (t s) -> p t s", t=2), X, ALU.max,
                                        negate=True).then_inc(max_ready, 1)

            def attend(n):
                d = S[slot_of[n]]
                wait_drained(dve, ("scores", n))
                linked(nc.vector.reciprocal(d["sm"][:, 4:6], d["sm"][:, 2:4]))
                for t in range(2):
                    nc.vector.tensor_scalar(d["p"][:, t, :], d["p"][:, t, :], d["sm"][:, 4 + t:5 + t], None, ALU.mult).then_inc(p_ready, 1)

            def stats_of(n):
                d = S[slot_of[n]]
                wait_drained(dve, ("mix", n))
                linked(nc.vector.bn_stats(d["bs"][0:LAT, :], d["h1"]))
                nc.vector.bn_aggr(d["st"][0:LAT, 0:2], d["bs"][0:LAT, :]).then_inc(mean_ready, 1)

            def centre(n):
                d = S[slot_of[n]]
                st = d["st"]
                dve.wait_ge(mean_ready, n + 1)
                wait_full(dve, ("centre", n))
                mu = bank_of(("centre", n))[0:LAT, 0:1]
                linked(nc.vector.tensor_tensor(st[0:LAT, 6:7], st[0:LAT, 0:1], mu, ALU.subtract))
                linked(nc.vector.tensor_tensor(st[0:LAT, 6:7], st[0:LAT, 6:7], st[0:LAT, 6:7], ALU.mult))
                nc.vector.tensor_tensor(st[0:LAT, 1:2], st[0:LAT, 1:2], st[0:LAT, 6:7], ALU.add).then_inc(dev_ready, 1)
                nc.vector.scalar_tensor_tensor(d["h1"], d["h1"], mu, gamma[:, :], ALU.subtract, ALU.mult).then_inc(drained["dve"], 1)

            def spread(n):
                wait_full(dve, ("spread", n))
                nc.vector.tensor_scalar(S[slot_of[n]]["st"][0:LAT, 2:3], bank_of(("spread", n))[0:LAT, 0:1], EPS, None, ALU.add).then_inc(drained["dve"], 1)

            def affine(n):
                d = S[slot_of[n]]
                dve.wait_ge(spread_rstd, n + 1)
                wait_drained(dve, ("centre", n))
                nc.vector.scalar_tensor_tensor(d["h1"], d["h1"], d["st"][0:LAT, 3:4], beta_ln[:, :], ALU.mult, ALU.add).then_inc(affine_ready, 1)

            def layer_stats(d, done):
                linked(nc.vector.bn_stats(d["bs"][:, :], d["x2"]))
                linked(nc.vector.bn_aggr(d["st"][:, 4:6], d["bs"][:, :]))
                nc.vector.tensor_scalar(d["st"][:, 5:6], d["st"][:, 5:6], EPS, None, ALU.add).then_inc(done, 1)

            def residual(n):
                d = S[slot_of[n]]
                wait_full(dve, ("residual", n))
                nc.vector.scalar_tensor_tensor(d["x2"], bank_of(("residual", n))[:, 0:HID], o_b[:, 0:1], d["xc"], ALU.add, ALU.add).then_inc(drained["dve"], 1)
                wait_drained(dve, ("residual", n))
                layer_stats(d, var2_ready)

            def scaled(d, src, xq, nb):
                v, qs = blocks(src), d["qs"]
                linked(nc.vector.tensor_reduce(qs[:, 0, 0:nb], v, X, ALU.max, apply_absolute_value=True))
                linked(nc.vector.tensor_scalar(qs[:, 1, 0:nb], qs[:, 0, 0:nb], 1.0 / FP8_MAX, SCALE_MIN, ALU.mult, ALU.max))
                linked(nc.vector.reciprocal(qs[:, 2, 0:nb], qs[:, 1, 0:nb]))
                linked(nc.vector.tensor_tensor(blocks(xq), v, qs[:, 2, 0:nb].unsqueeze(2).broadcast_to([P, nb, BLK]), ALU.mult))

            def times_scale(d, xq, nb):
                v = blocks(xq)
                return nc.vector.tensor_tensor(v, v, d["qs"][:, 1, 0:nb].unsqueeze(2).broadcast_to([P, nb, BLK]), ALU.mult)

            def quantise(n):
                d = S[slot_of[n]]
                dve.wait_ge(rstd2_ready, n + 1)
                nc.vector.tensor_scalar(d["x2"], d["x2"], d["st"][:, 4:5], d["st"][:, 5:6], ALU.subtract, ALU.mult).then_inc(x2_ready, 1)
                dve.wait_ge(x2_ready, n + 1)
                xq, w = d["xq"][:, 0:HID], d["w"][:, 0:HID]
                scaled(d, d["x2"], xq, HID // BLK)
                linked(round_to(w, xq))
                linked(nc.vector.tensor_tensor(xq, xq, w, ALU.add))
                linked(nc.vector.tensor_tensor(xq, xq, w, ALU.subtract))
                times_scale(d, xq, HID // BLK).then_inc(xdq_ready, 1)

            def gate_up(n):
                d = S[slot_of[n]]
                for j in range(2):
                    h = d["hh"][:, 512 * j:512 * j + 512]
                    wait_drained(dve, ("gate_h", n, j))
                    wait_full(dve, ("up_h", n, j))
                    nc.vector.tensor_tensor(h, h, bank_of(("up_h", n, j))[:, :], ALU.mult).then_inc(drained["dve"], 1)

            def quantise_h(n):
                d = S[slot_of[n]]
                wait_drained(dve, ("up_h", n, 1))
                scaled(d, d["hh"], d["xq"], INTER // BLK)
                round_to(d["w"], d["xq"]).then_inc(magic_ready, 1)

            def transpose_h(n):
                d = S[slot_of[n]]
                dve.wait_ge(hrounded, 2 * n + 2)
                times_scale(d, d["xq"], INTER // BLK).then_inc(hdq_ready, 1)

            def down(n):
                d = S[slot_of[n]]
                wait_full(dve, ("down", n))
                nc.vector.tensor_tensor(d["x2"], d["x2"], bank_of(("down", n))[:, 0:HID], ALU.add).then_inc(drained["dve"], 1)
                wait_drained(dve, ("down", n))
                layer_stats(d, var3_ready)

            def final(n):
                d = S[slot_of[n]]
                dve.wait_ge(rstd3_ready, n + 1)
                nc.vector.tensor_scalar(d["x2"], d["x2"], d["st"][:, 4:5], d["st"][:, 5:6], ALU.subtract, ALU.mult).then_inc(final_ready, 1)

            dve.wait_ge(consts_ready, 1)
            run({"w_scale": w_scale, "w_magic": w_magic, "ab": ab, "feat": feat, "norm": norm,
                 "vT": vT, "kq": kq, "diag": diag, "rows": rows, "below": below, "inverse": inverse, "solve": solve,
                 "o": o, "y": y, "x1": x1, "xw": xw_T, "project": project, "scores": scores, "attend": attend,
                 "stats": stats_of, "centre": centre, "spread": spread, "affine": affine, "residual": residual,
                 "quantise": quantise, "gate_up": gate_up, "quantise_h": quantise_h,
                 "transpose_h": transpose_h, "down": down, "final": final})

        @block.tensor
        def _(pe):
            mm, tr = nc.tensor.matmul, nc.tensor.transpose

            def x_T(f):
                pe.wait_ge(x_loaded[f], 16)
                for c in range(2):
                    wait_free(pe, ("xT", f, c))
                    for b in range(HALF):
                        ins = tr(bank_of(("xT", f, c))[:, P * b:P * b + P], xs[:, HALF * f + b, P * c:P * c + P], ident[:, :])
                    ins.then_inc(psum_full, 1)

            def gate(f, b):
                key = ("gate", f, b)
                if b == 0:
                    pe.wait_ge(wg_loaded, loaded[wg_loaded])
                    for c in range(2):
                        wait_drained(pe, ("xT", f, c))
                wait_free(pe, key)
                for c in range(2):
                    ins = mm(bank_of(key)[:, 0:NH * DV + 2 * NH], xT[:, c, P * b:P * b + P], W_g[:, c, :], start=(c == 0), stop=(c == 1))
                ins.then_inc(psum_full, 1)

            def feat(f, i):
                key = ("feat", f, i)
                at, n = FT[i]
                if i == 0:
                    pe.wait_ge(wf_loaded, loaded[wf_loaded])
                    for c in range(2):
                        wait_drained(pe, ("xT", f, c))
                wait_free(pe, key)
                for c in range(2):
                    ins = mm(bank_of(key)[0:n, :], W_f[:, c, at:at + n], xT[:, c, :], start=(c == 0), stop=(c == 1))
                ins.then_inc(psum_full, 1)

            def decay(f, g):
                pe.wait_ge(GU_ready, f + 1)
                wait_free(pe, ("decay", f, g))
                mm(bank_of(("decay", f, g))[:, :], after[:, :], GU[:, 4 * g:4 * g + 4, :], start=True, stop=True).then_inc(psum_full, 1)

            def norm(f):
                pe.wait_ge(squares_ready, 4 * (f + 1))
                wait_free(pe, ("norm", f))
                for b in range(HALF):
                    for i, (c0, m) in enumerate([(0, 4), (NH, 4), (4, 2), (NH + 4, 2)]):
                        c0 += 2 * NH * b
                        n = DK * m
                        ins = mm(bank_of(("norm", f))[:, c0:c0 + m], sq[0:n, i, P * b:P * b + P], headsel[0:n, 0:m], start=True, stop=True)
                ins.then_inc(psum_full, 1)

            def vT(f, b):
                pe.wait_ge(feat_ready, NFT * (f + 1))
                wait_free(pe, ("vT", f, b))
                for c in range(3):
                    ins = tr(bank_of(("vT", f, b))[:, P * c:P * c + P], F[:, 4 + c, P * b:P * b + P], ident[:, :])
                ins.then_inc(psum_full, 1)

            def kq(f, j, h):
                key = ("kq", f, j, h)
                wait_free(pe, key)
                r = slice(DK * (h % 4), DK * (h % 4) + DK)
                i = 2 * (h // 4)
                for k in range(2):
                    t = slice(P * (2 * j + k), P * (2 * j + k) + P)
                    ins = mm(bank_of(key)[:, 2 * P * k:2 * P * k + 2 * P], F[r, i, t], F[r, i:i + 2, t], start=True, stop=True)
                ins.then_inc(psum_full, 1)

            def products(key, rows, lhs, rhs, g):
                wait_free(pe, key)
                for q in range(GQ * g, GQ * g + GQ):
                    ins = mm(bank_of(key)[rows, DV * (q % GQ):DV * (q % GQ) + DV], lhs(q), rhs(q), start=True, stop=True)
                ins.then_inc(psum_full, 1)

            def solve(f, k):
                r, up = slice(BLK * k, BLK * k + BLK), slice(0, BLK * k)
                if k == 0:
                    wait_drained(pe, ("vT", f, HALF - 1))
                    pe.wait_ge(inverse_ready, f + 1)
                else:
                    for g in range(NQ // GQ):
                        wait_drained(pe, ("w", f, k - 1, g))
                        products(("r", f, k, g), r, lambda q: MP[up, q, 0, r], lambda q: om[up, q, :], g)
                for g in range(NQ // GQ):
                    if k:
                        wait_drained(pe, ("r", f, k, g))
                    products(("w", f, k, g), r, lambda q: TT[r, q, :], lambda q: (R if k else u)[r, q, :], g)

            def o(f):
                for g in range(NQ // GQ):
                    wait_drained(pe, ("w", f, P // BLK - 1, g))
                    products(("o", f, g), slice(0, P), lambda q: MP[:, q, 1, :], lambda q: om[:, q, :], g)

            def og(f):
                pe.wait_ge(og_ready, f + 1)
                for b in range(HALF):
                    key = ("og", f, b)
                    wait_free(pe, key)
                    src = osb[:, NH * b:NH * b + NH, :].rearrange("p h d -> p (h d)")
                    for c in range(3):
                        ins = tr(bank_of(key)[:, P * c:P * c + P], src[:, P * c:P * c + P], ident[:, :])
                    ins.then_inc(psum_full, 1)

            def y(f):
                pe.wait_ge(wo_loaded, loaded[wo_loaded])
                for b in range(HALF):
                    key = ("y", f, b)
                    wait_drained(pe, ("og", f, b))
                    wait_free(pe, key)
                    for c in range(3):
                        ins = mm(bank_of(key)[:, 0:HID], ogT[:, b, c, :], W_o[:, c, :], start=(c == 0), stop=(c == 2))
                    ins.then_inc(psum_full, 1)

            def w_T(n):
                pe.wait_ge(wquant, n + 1)
                for i in range(4):
                    key = ("w_T", n, i)
                    wait_free(pe, key)
                    for m in range(4):
                        if n == 2:
                            k, t = 2 * i + m // 2, m % 2
                            src = wx[:, INTER * t + P * k:INTER * t + P * k + P]
                        else:
                            t = 4 * (i // 2) + m
                            src = wx[:, HID * t + P * (i % 2):HID * t + P * (i % 2) + P]
                        ins = tr(bank_of(key)[:, P * m:P * m + P], src, ident[:, :])
                    ins.then_inc(psum_full, 1)

            def xw_T():
                pe.wait_ge(cross_loaded, loaded[cross_loaded])
                wait_free(pe, ("xw", 0))
                for i in range(3):
                    ins = tr(bank_of(("xw", 0))[:, LAT * i:LAT * i + LAT], xw_in[:, i, :], ident[0:LAT, 0:LAT])
                ins.then_inc(psum_full, 1)
                wait_free(pe, ("xw", 1))
                tr(bank_of(("xw", 1))[0:LAT, 0:P], ow_in[:, :], ident[:, :]).then_inc(psum_full, 1)

            def project(n):
                wait_drained(pe, ("xw", 1))
                wait_free(pe, ("thph", n))
                pe.wait_ge(ctx_loaded, 16)
                pe.wait_ge(x1_ready, n + 1)
                ps = bank_of(("thph", n))
                mm(ps[0:LAT, 0:HID], xw[:, 0, :], ctx[:, n, :], start=True, stop=True)
                mm(ps[0:LAT, HID:2 * HID], xw[:, 1, :], xs[:, n, :], start=True, stop=True).then_inc(psum_full, 1)
                wait_free(pe, ("g", n))
                for t in range(2):
                    ins = mm(bank_of(("g", n))[:, LAT * t:LAT * t + LAT], xs[:, n, P * t:P * t + P], xw[:, 2, :], start=True, stop=True)
                ins.then_inc(psum_full, 1)

            def scores(n):
                th = S[slot_of[n]]["thph"]
                wait_free(pe, ("scores", n))
                wait_drained(pe, ("thph", n))
                for t in range(2):
                    ins = mm(bank_of(("scores", n))[:, HID * t:HID * t + HID], th[:, 0, P * t:P * t + P], th[:, 1, :], start=True, stop=True)
                ins.then_inc(psum_full, 1)

            def attend(n):
                wait_free(pe, ("attend", n))
                pe.wait_ge(p_ready, 2 * (n + 1))
                for k in range(2):
                    for t in range(2):
                        ins = tr(bank_of(("attend", n))[:, HID * k + P * t:HID * k + P * t + P],
                                 S[slot_of[n]]["p"][:, t, P * k:P * k + P], ident[:, :])
                ins.then_inc(psum_full, 1)

            def mix(n):
                d = S[slot_of[n]]
                wait_free(pe, ("mix", n))
                wait_drained(pe, ("attend", n))
                wait_drained(pe, ("g", n))
                for k in range(2):
                    ins = mm(bank_of(("mix", n))[0:LAT, 0:HID], d["g"][:, k, :], d["pT"][:, k, :], start=(k == 0), stop=(k == 1))
                ins.then_inc(psum_full, 1)

            def centre(n):
                wait_free(pe, ("centre", n))
                pe.wait_ge(mean_ready, n + 1)
                mm(bank_of(("centre", n))[0:LAT, 0:1], mean64[:, :], S[slot_of[n]]["st"][0:LAT, 0:1], start=True, stop=True).then_inc(psum_full, 1)

            def spread(n):
                wait_free(pe, ("spread", n))
                pe.wait_ge(dev_ready, n + 1)
                mm(bank_of(("spread", n))[0:LAT, 0:1], mean64[:, :], S[slot_of[n]]["st"][0:LAT, 1:2], start=True, stop=True).then_inc(psum_full, 1)

            def residual(n):
                wait_free(pe, ("residual", n))
                pe.wait_ge(relu_ready, n + 1)
                mm(bank_of(("residual", n))[:, 0:HID], owT[:, :], S[slot_of[n]]["h1"], start=True, stop=True).then_inc(psum_full, 1)

            def quantise(n):
                wait_free(pe, ("quantise", n))
                pe.wait_ge(xdq_ready, n + 1)
                for k in range(2):
                    ins = tr(bank_of(("quantise", n))[:, P * k:P * k + P], S[slot_of[n]]["xq"][:, P * k:P * k + P], ident[:, :])
                ins.then_inc(psum_full, 1)

            def gate_up(n):
                wait_drained(pe, ("quantise", n))
                for j in range(2):
                    for name, wt in (("gate_h", gateT), ("up_h", upT)):
                        key = (name, n, j)
                        wait_free(pe, key)
                        for k in range(2):
                            ins = mm(bank_of(key)[:, :], S[slot_of[n]]["x2T"][:, k, :], wt[:, k, 512 * j:512 * j + 512], start=(k == 0), stop=(k == 1))
                        ins.then_inc(psum_full, 1)

            def transpose_h(n):
                pe.wait_ge(hdq_ready, n + 1)
                for j in range(2):
                    key = ("transpose_h", n, j)
                    wait_free(pe, key)
                    for m in range(4):
                        k = 4 * j + m
                        ins = tr(bank_of(key)[:, P * m:P * m + P], S[slot_of[n]]["xq"][:, P * k:P * k + P], ident[:, :])
                    ins.then_inc(psum_full, 1)

            def down(n):
                wait_free(pe, ("down", n))
                for k in range(INTER // P):
                    if k % 4 == 0:
                        wait_drained(pe, ("transpose_h", n, k // 4))
                    ins = mm(bank_of(("down", n))[:, 0:HID], S[slot_of[n]]["hT"][:, k, :], downT[:, k, :], start=(k == 0), stop=(k == INTER // P - 1))
                ins.then_inc(psum_full, 1)

            pe.wait_ge(consts_ready, 1)
            run({"xT": x_T, "gate": gate, "feat": feat, "decay": decay, "norm": norm, "vT": vT, "kq": kq, "solve": solve,
                 "o": o, "og": og, "y": y, "w_T": w_T, "xw": xw_T, "project": project, "scores": scores,
                 "attend": attend, "mix": mix, "centre": centre, "spread": spread, "residual": residual,
                 "quantise": quantise, "gate_up": gate_up, "transpose_h": transpose_h, "down": down})


_INS = ["x", "ctx_2048", "L0_attn_Wq", "L0_attn_Wk", "L0_attn_Wv", "L0_attn_Wa", "L0_attn_Wb", "L0_attn_Wg", "L0_attn_Wo",
        "L0_attn_conv_wq", "L0_attn_conv_wk", "L0_attn_conv_wv", "L0_attn_A_log", "L0_attn_dt_bias",
        "L0_attn_norm_weight", "L0_xattn_theta_w", "L0_xattn_theta_b", "L0_xattn_phi_w", "L0_xattn_phi_b",
        "L0_xattn_g_w", "L0_xattn_g_b", "L0_xattn_ln_gamma", "L0_xattn_ln_beta", "L0_xattn_out_w",
        "L0_xattn_out_b", "L0_ffn_gate_w", "L0_ffn_up_w", "L0_ffn_down_w"]


def kernel(**inputs):
    import numpy as np
    import concourse.bacc as bacc
    from concourse.bass_utils import run_bass_kernel_spmd

    nc = bacc.Bacc("TRN2", target_bir_lowering=False, num_devices=1)
    arrays, args = {}, []
    for name in _INS:
        a = np.ascontiguousarray(inputs[name])
        arrays[f"in_{name}"] = a
        args.append(nc.dram_tensor(f"in_{name}", a.shape, mybir.dt.from_np(a.dtype), kind="ExternalInput").ap())
    args.append(nc.dram_tensor("out", (SEQ, P, HID), F32, kind="ExternalOutput").ap())
    program(nc, *args)
    r = run_bass_kernel_spmd(nc, [arrays], core_ids=[0])
    return r.results[0]["out"]
```

```python
from contextlib import ExitStack

import concourse.bass as bass
from concourse import mybir

F32 = mybir.dt.float32
I32 = mybir.dt.int32
ALU = mybir.AluOpType
ACT = mybir.ActivationFunctionType
X = mybir.AxisListType.X

P = 128
SEQ = 8
HALF = 4
HID = 256
NH, DK, DV = 6, 32, 64
TAPS = 4
NQ = HALF * NH
GQ = 8
LAT, INTER = 64, 1024
BLK = 32
SUB = 16
NBANK = 8
EPS = 1e-5
FP8_MAX, SCALE_MIN = 448.0, 1e-30
MIN_NORMAL = 2.0 ** -6
MAGIC_SHIFT = 2.0 ** 20
EXP_MASK, HALF_BIT = 0x7F800000, 0x00400000
DIAG = SUB * BLK + SUB

FT = [(0, 128), (192, 128), (128, 64), (320, 64), (384, 128), (512, 128), (640, 128)]
NFT = len(FT)
ROWS = [(1, 6), (6, 10), (10, 13), (13, 16)]

SEQ_STAGES = ["project", "scores", "attend", "mix", "stats", "centre", "spread", "affine", "residual",
              "quantise", "gate_up", "quantise_h", "transpose_h", "down", "final"]


def chains():
    c = {"w": [(k, n) for n in range(3) for k in ("w_scale", "w_magic", "w_T")] + [("xw",)]}
    for f in range(2):
        c["AB"[f]] = ([("xT", f)] + [("feat", f, i) for i in range(NFT)] + [("feat_end", f), ("norm", f)]
                      + [s for j in range(HALF // 2) for s in [("kq", f, j, h) for h in range(NH)] + [("diag_in", f, j)]]
                      + [("diag", f)] + [("rows", f, i) for i in range(len(ROWS))]
                      + [("below", f, i) for i in range(4)] + [("inverse", f)]
                      + [("solve", f, k) for k in range(P // BLK)]
                      + [(k, f, b) for b in range(HALF) for k in ("o", "o_scale")]
                      + [(k, f, b) for b in range(HALF) for k in ("og", "y", "x1")])
        c["ab"[f]] = ([("gate", f, b) for b in range(HALF)] + [("ab", f)] + [("decay_in", f, b) for b in range(HALF)]
                      + [("decay", f, g) for g in range(NQ // 4)])
        c["uv"[f]] = [("vT", f, b) for b in range(HALF)]
    for n in range(SEQ):
        c[str(n)] = [(k, n) for k in SEQ_STAGES]
    return c


INTERLEAVE = (
    "AAAAaAaAaaaAABaaAAbaaaaabubwbaaubawAAAAAAAAAAAbAuAAAbbAAubAwAAAAAAwbBbbbbBBBBAwBBBBAAAbwwA"
    "AAAAwAABBBBBBBBBBBBBBBBBBBBwABwAAAAABAA0ABAA10A10Bv010vvv10B0B1101B101B010011BBBBB0BBA0B01"
    "B1B1BB2BBB32B3423BB2252323243563245345246543226635B246455B22457636747765776773474563475667"
    "57343657645767")


def order():
    left = chains()
    stages = [left[c].pop(0) for c in INTERLEAVE]
    assert not any(left.values())
    return stages


def tiles_of(stage):
    k, a = stage[0], stage[1:]
    if k == "xT":
        return [(stage + (c,), "act") for c in range(2)]
    if k == "solve":
        r = [("r",) + a + (g,) for g in range(NQ // GQ)] if a[1] else []
        return [(t, "dve") for t in r] + [(("w",) + a + (g,), "act") for g in range(NQ // GQ)]
    if k == "w_T":
        return [(stage + (i,), "act") for i in range(4)]
    if k == "xw":
        return [(("xw", 0), "dve"), (("xw", 1), "dve")]
    if k == "project":
        return [(("thph",) + a, "act"), (("g",) + a, "dve")]
    if k == "gate_up":
        return [((n,) + a + (j,), r) for j in range(2) for n, r in (("gate_h", "act"), ("up_h", "dve"))]
    if k == "transpose_h":
        return [(stage + (j,), "act") for j in range(2)]
    reader = {"gate": "act", "feat": "dve", "decay": "act", "norm": "dve", "vT": "dve", "kq": "dve",
              "o": "act", "og": "act", "y": "dve", "scores": "act", "attend": "act", "mix": "act", "centre": "dve",
              "spread": "dve", "residual": "dve", "quantise": "act", "down": "dve"}.get(k)
    return [(stage, reader)] if reader else []


class Tiles:

    def __init__(self, stages):
        self.at, self.drain, self.count = {}, [], {"act": 0, "dve": 0}
        for stage in stages:
            for key, reader in tiles_of(stage):
                self.at[key] = len(self.drain)
                self.count[reader] += 1
                self.drain.append((reader, self.count[reader]))


def program(nc, x, ctxt, Wq, Wk, Wv, Wa, Wb, Wg, Wo, conv_wq, conv_wk, conv_wv, A_log, dt_bias,
            norm_weight, theta_w, theta_b, phi_w, phi_b, g_w, g_b, ln_gamma, ln_beta, out_w,
            out_b, gate_w, up_w, down_w, out):
    STAGES = order()
    tiles = Tiles(STAGES)
    slot_of = [0, 1, 0, 1, 2, 3, 4, 0]
    NSLOT = 5

    with ExitStack() as stack:
        def sb(name, shape, dt=F32):
            return stack.enter_context(nc.sbuf_tensor(name, shape, dt))

        def sem(name):
            return stack.enter_context(nc.semaphore(name))

        bank = [stack.enter_context(nc.psum_tensor(f"bank{i}", [P, 512], F32)) for i in range(NBANK)]

        ident = sb("ident", [P, P])
        upto = sb("upto", [P, P])
        after = sb("after", [P, P])
        headsel = sb("headsel", [P, 4])
        mean64 = sb("mean64", [LAT, LAT])
        powers = sb("powers", [P, HALF, 2 * NH])
        mhalf = sb("mhalf", [P, NQ])
        W_f = sb("W_f", [P, 2, 768])
        W_g = sb("W_g", [P, 2, NH * DV + 2 * NH])
        W_o = sb("W_o", [P, 3, HID])
        conv_w = sb("conv_w", [P, NFT, TAPS])
        dt_b = sb("dt_b", [P, NH])
        expA = sb("expA", [P, NH])
        norm_w = sb("norm_w", [P, DV])
        gateT = sb("gateT", [P, 2, INTER])
        upT = sb("upT", [P, 2, INTER])
        downT = sb("downT", [P, INTER // P, HID])
        xw_in = sb("xw_in", [LAT, 3, P])
        xw = sb("xw", [P, 3, LAT])
        ow_in = sb("ow_in", [P, LAT])
        owT = sb("owT", [LAT, P])
        th_b = sb("th_b", [LAT, 1])
        ph_b = sb("ph_b", [LAT, 1])
        g_bb = sb("g_bb", [P, LAT])
        gamma = sb("gamma", [LAT, HID])
        beta_ln = sb("beta_ln", [LAT, HID])
        o_b = sb("o_b", [P, 1])

        xs = sb("xs", [P, SEQ, HID])
        xT = sb("xT", [P, 2, 512])
        Fm = sb("Fm", [P, 3584])
        F = Fm[:, :].rearrange("p (i t) -> p i t", i=NFT)
        SGs = [sb(f"SG{f}", [P, NQ, DV]) for f in range(2)]
        MPm = sb("MPm", [P, NQ * 2 * P])
        MP = MPm[:, :].rearrange("p (q a t) -> p q a t", q=NQ, a=2)
        Em = sb("Em", [P, NQ * P])
        E = Em[:, :].rearrange("p (q t) -> p q t", q=NQ)
        CD = sb("CD", [P, BLK, BLK])
        L = sb("L", [P, 2 * DIAG])
        T = sb("T", [P, 2 * DIAG])
        CT = CD
        TT = sb("TT", [P, NQ, BLK])
        Wl = sb("Wl", [P, SUB, SUB])
        u = sb("u", [P, NQ, DV])
        Rom = sb("Rom", [P, 2, NQ * DV])
        R, om = (Rom[:, i, :].rearrange("p (q d) -> p q d", q=NQ) for i in range(2))
        smalls = [sb(f"small{f}", [P, 10, HALF, 2 * NH]) for f in range(2)]
        stats = sb("stats", [P, HALF, 6])
        mv = sb("mv", [P, HALF, 2])
        prod = Em
        osb = R
        ogT = u[:, :, :].rearrange("p q d -> p (q d)").rearrange("p (b c t) -> p b c t", b=HALF, c=3)
        osq = om

        arena = sb("arena", [P, 3 * 2048])
        wn, wx, ww = (arena[:, 2048 * i:2048 * i + 2048] for i in range(3))
        wsc = sb("wsc", [P, 3, 64])
        ffn = sb("ffn", [P, 2 * 3072])
        GU = ffn[:, 0:NQ * P].rearrange("p (q t) -> p q t", q=NQ)
        sq = ffn[:, NQ * P:NQ * P + 4 * 512].rearrange("p (i t) -> p i t", i=4)

        S = []
        for s, (a, b) in enumerate([(arena[:, 0:3072], ffn[:, 0:3072]), (arena[:, 3072:6144], ffn[:, 3072:6144]),
                                    (MPm[:, 0:3072], MPm[:, 3072:6144]), (Fm[:, 0:3072], Em[:, :]),
                                    (Rom[:, :, :].rearrange("p a n -> p (a n)"), None)]):
            d = {n: sb(f"{n}{s}", shape) for n, shape in [("sm", [P, 8]), ("st", [P, 8]), ("bs", [P, 6]), ("qs", [P, 3, 32])]}
            d["xc"], d["x2"] = a[:, 0:256], a[:, 256:512]
            d["thph"] = a[0:LAT, 512:1024].rearrange("p (k t) -> p k t", k=2)
            d["p"] = a[:, 1024:1536].rearrange("p (k t) -> p k t", k=2)
            d["pT"] = a[:, 1536:2048].rearrange("p (k t) -> p k t", k=2)
            d["g"] = a[:, 2048:2176].rearrange("p (k t) -> p k t", k=2)
            d["h1"] = a[0:LAT, 2176:2432]
            d["x2T"] = a[:, 2432:2688].rearrange("p (k t) -> p k t", k=2)
            d["ctx"] = a[:, 2688:2944]
            if b is None:
                d["hh"], d["xq"], d["w"] = (v[:, :, :].rearrange("p q d -> p (q d)")[:, 0:1024] for v in (SGs[0], SGs[1], u))
            else:
                d["hh"], d["xq"], d["w"] = b[:, 0:1024], b[:, 1024:2048], b[:, 2048:3072]
            d["hT"] = d["w"].rearrange("p (k t) -> p k t", k=INTER // P)
            S.append(d)

        x_loaded = [sem(f"x_loaded{f}") for f in range(2)]
        wf_loaded, wg_loaded, conv_loaded, wo_loaded = (sem(n) for n in ("wf_loaded", "wg_loaded", "conv_loaded", "wo_loaded"))
        small_loaded, cross_loaded, wn_loaded = (sem(n) for n in ("small_loaded", "cross_loaded", "wn_loaded"))
        ctx_loaded = [sem(f"ctx_loaded{s}") for s in range(NSLOT)]
        ident_ready, consts_ready = sem("ident_ready"), sem("consts_ready")
        psum_full = sem("psum_full")
        drained = {"act": sem("act_drained"), "dve": sem("dve_drained")}
        dve_link, pool_link = sem("dve_link"), sem("pool_link")
        (expA_ready, ab_raw, ab_biased, ab_abs, ab_exp, ab_plus, ab_ln, g_ready, conv_started, feat_ready, squares_ready, norms_ready,
         roots_ready, GU_ready, E_masked, gatew_ready, diag_copied, rows_ready, lane_product, Wl_ready, inverse_out, inverse_ready, o_squared,
         ms_ready, rms_ready, og_ready, var_ready, rstd_ready, x1_ready, wamax, wscaled, wmagic, wquant) = (sem(n) for n in (
             "expA_ready", "ab_raw", "ab_biased", "ab_abs", "ab_exp", "ab_plus", "ab_ln", "g_ready", "conv_started", "feat_ready",
             "squares_ready", "norms_ready", "roots_ready", "GU_ready", "E_masked", "gatew_ready",
             "diag_copied", "rows_ready", "lane_product", "Wl_ready", "inverse_out", "inverse_ready", "o_squared", "ms_ready", "rms_ready", "og_ready",
             "var_ready", "rstd_ready", "x1_ready", "wamax", "wscaled", "wmagic", "wquant"))
        (xc_ready, max_ready, p_ready, mean_ready, dev_ready, spread_rstd, affine_ready, relu_ready,
         var2_ready, rstd2_ready, x2_ready, xdq_ready, magic_ready, hrounded, hdq_ready, last_hdq_ready,
         var3_ready, rstd3_ready, final_ready) = (sem(n) for n in (
             "xc_ready", "max_ready", "p_ready", "mean_ready", "dev_ready", "spread_rstd", "affine_ready",
             "relu_ready", "var2_ready", "rstd2_ready", "x2_ready", "xdq_ready", "magic_ready",
             "hrounded", "hdq_ready", "last_hdq_ready", "var3_ready", "rstd3_ready", "final_ready"))
        out_stored = [sem(f"out_stored{s}") for s in range(NSLOT)]

        block = stack.enter_context(nc.Block())

        def bank_of(key):
            return bank[tiles.at[key] % NBANK]

        def wait_free(pe, key):
            n = tiles.at[key] - NBANK
            if n >= 0:
                reader, count = tiles.drain[n]
                pe.wait_ge(drained[reader], count)

        def wait_full(eng, key):
            eng.wait_ge(psum_full, tiles.at[key] + 1)

        def wait_drained(eng, key):
            reader, count = tiles.drain[tiles.at[key]]
            eng.wait_ge(drained[reader], count)

        def wait_ctx(eng, n):
            eng.wait_ge(ctx_loaded[slot_of[n]], 16 * (1 + slot_of[:n].count(slot_of[n])))

        def wait_out_stored(eng, n):
            before = [m for m in range(n) if slot_of[m] == slot_of[n]]
            if before:
                eng.wait_ge(out_stored[slot_of[n]], 16 * len(before))

        def group(a, g, rows=slice(0, P)):
            return a[rows, GQ * g:GQ * g + GQ, :].rearrange("p q d -> p (q d)")

        def run(parts):
            for stage in STAGES:
                if stage[0] in parts:
                    parts[stage[0]](*stage[1:])

        def rows_p(w):
            return w.rearrange("(c p) n -> p c n", p=P)

        def row_everywhere(w, n):
            return w.rearrange("(a n) -> a n", a=1).broadcast_to([P, n])

        loads = {
            wf_loaded: [(W_f[:, :, 0:192], rows_p(Wk)), (W_f[:, :, 192:384], rows_p(Wq)), (W_f[:, :, 384:768], rows_p(Wv))],
            wg_loaded: [(W_g[:, :, 0:NH * DV], rows_p(Wg)), (W_g[:, :, NH * DV:NH * DV + NH], rows_p(Wa)),
                        (W_g[:, :, NH * DV + NH:], rows_p(Wb))],
            conv_loaded: [(conv_w[:, 0, :], conv_wk[0:128, :]), (conv_w[:, 1, :], conv_wq[0:128, :]),
                          (conv_w[0:64, 2, :], conv_wk[128:192, :]), (conv_w[0:64, 3, :], conv_wq[128:192, :]),
                          (conv_w[:, 4:7, :], rows_p(conv_wv))],
            small_loaded: [(dt_b[:, :], row_everywhere(dt_bias, NH)), (expA[:, :], row_everywhere(A_log, NH)),
                           (norm_w[:, :], row_everywhere(norm_weight, DV))],
            wo_loaded: [(W_o[:, :, :], rows_p(Wo))],
            cross_loaded: [(xw_in[:, 0, :], theta_w), (xw_in[:, 1, :], phi_w), (xw_in[:, 2, :], g_w), (ow_in[:, :], out_w),
                           (th_b[:, :], theta_b.rearrange("(n a) -> n a", a=1)),
                           (ph_b[:, :], phi_b.rearrange("(n a) -> n a", a=1)),
                           (g_bb[:, :], row_everywhere(g_b, LAT)), (gamma[:, :], ln_gamma), (beta_ln[:, :], ln_beta),
                           (o_b[:, :], out_b.rearrange("(n a) -> n a", a=1))],
        }
        loaded = {k: 16 * len(v) for k, v in loads.items()}

        def lane_products():
            M, Tm = (v[:, 0:BLK * BLK].rearrange("p (t j) -> p t j", t=BLK) for v in (L, T))
            h = SUB // 2
            return [(Wl[:, :, 0:h], M[:, SUB:, 0:SUB], Tm[:, 0:SUB, 0:h], False, False),
                    (Wl[:, :, h:], M[:, SUB:, h:SUB], Tm[:, h:SUB, h:SUB], False, True),
                    (Tm[:, SUB + h:, 0:SUB], Tm[:, SUB + h:, SUB:], Wl[:, :, :], True, False),
                    (Tm[:, SUB:SUB + h, 0:SUB], Tm[:, SUB:SUB + h, SUB:SUB + h], Wl[:, 0:h, :], True, True)]

        def product_terms(i, lhs, rhs):
            (m, k), n = lhs.shape[1:], rhs.shape[2]
            at = 2048 if i % 2 else 0
            return prod[:, at:at + m * n * k].rearrange("p (t c j) -> p t c j", t=m, c=n)

        def factors(lhs, rhs):
            (m, k), n = lhs.shape[1:], rhs.shape[2]
            return (lhs.unsqueeze(2).broadcast_to([P, m, n, k]),
                    rhs.rearrange("p j c -> p c j").unsqueeze(1).broadcast_to([P, m, n, k]))

        @block.sync
        def _(sp):
            def x_half(f):
                b = slice(HALF * f, HALF * f + HALF)
                sp.dma_start(xs[:, b, :], x[b].rearrange("b p n -> p b n")).then_inc(x_loaded[f], 16)
            x_half(0)
            for k in (wf_loaded, conv_loaded, wg_loaded, small_loaded, wo_loaded):
                for dst, src in loads[k]:
                    sp.dma_start(dst, src).then_inc(k, 16)
            sp.dma_start(wn.rearrange("p (t n) -> p t n", t=8), rows_p(gate_w)).then_inc(wn_loaded, 16)
            x_half(1)
            for dst, src in loads[cross_loaded]:
                sp.dma_start(dst, src).then_inc(cross_loaded, 16)
            sp.wait_ge(wscaled, 1)
            sp.dma_start(wn.rearrange("p (t n) -> p t n", t=8), rows_p(up_w)).then_inc(wn_loaded, 16)
            sp.wait_ge(wscaled, 2)
            sp.dma_start(wn.rearrange("p (t n) -> p t n", t=2), rows_p(down_w)).then_inc(wn_loaded, 16)

            def load_ctx(n):
                sp.dma_start(S[slot_of[n]]["ctx"], ctxt[n, :, :]).then_inc(ctx_loaded[slot_of[n]], 16)

            wait_full(sp, ("w_T", 2, 3))
            load_ctx(0)
            load_ctx(1)

            def mix(n):
                after_n = [m for m in range(n + 1, SEQ) if slot_of[m] == slot_of[n]]
                if after_n:
                    wait_full(sp, ("thph", n))
                    sp.wait_ge(xc_ready, n + 1)
                    load_ctx(after_n[0])

            def og(f, b):
                if (f, b) == (1, HALF - 1):
                    for n, key in ((4, ("o", 1, HALF - 1)), (5, ("vT", 1, HALF - 1)), (6, ("og", 1, HALF - 1))):
                        wait_full(sp, key)
                        load_ctx(n)

            def final(n):
                sp.wait_ge(final_ready, n + 1)
                sp.dma_start(out[n, :, :], S[slot_of[n]]["x2"]).then_inc(out_stored[slot_of[n]], 16)
            run({"mix": mix, "og": og, "final": final})
            for s in range(NSLOT):
                sp.wait_ge(out_stored[s], 16 * slot_of.count(s))

        @block.gpsimd
        def _(pool):
            link = [0]

            def linked(ins):
                link[0] += 1
                ins.then_inc(pool_link, 1)
                pool.wait_ge(pool_link, link[0])

            linked(nc.gpsimd.memset(ident[:, :], 0.0))
            nc.gpsimd.affine_select(out=ident[:, :], in_=ident[:, :], compare_op=ALU.not_equal, fill=1.0,
                                    base=0, pattern=[[-1, P]], channel_multiplier=1).then_inc(ident_ready, 1)
            linked(nc.gpsimd.memset(upto[:, :], 1.0))
            linked(nc.gpsimd.affine_select(out=upto[:, :], in_=upto[:, :], compare_op=ALU.is_ge, fill=0.0,
                                           base=0, pattern=[[1, P]], channel_multiplier=-1))
            linked(nc.gpsimd.memset(after[:, :], 1.0))
            linked(nc.gpsimd.affine_select(out=after[:, :], in_=after[:, :], compare_op=ALU.is_gt, fill=0.0,
                                           base=0, pattern=[[-1, P]], channel_multiplier=1))
            linked(nc.gpsimd.memset(headsel[:, :], 1.0))
            linked(nc.gpsimd.affine_select(out=headsel[:, :], in_=headsel[:, :], compare_op=ALU.is_ge, fill=0.0,
                                           base=0, pattern=[[-DK, 4]], channel_multiplier=1))
            linked(nc.gpsimd.affine_select(out=headsel[:, :], in_=headsel[:, :], compare_op=ALU.is_ge, fill=0.0,
                                           base=DK - 1, pattern=[[DK, 4]], channel_multiplier=-1))
            linked(nc.gpsimd.memset(mean64[:, :], 1.0 / LAT))
            linked(nc.gpsimd.memset(powers[:, :, 0:NH], 0.5))
            linked(nc.gpsimd.memset(powers[:, :, NH:2 * NH], -0.5))
            linked(nc.gpsimd.memset(mhalf[:, :], -0.5))
            linked(nc.gpsimd.memset(CD[:, :, :], 0.0))
            linked(nc.gpsimd.memset(T[:, :], 0.0))
            Tm = T[:, 0:BLK * BLK].rearrange("p (t j) -> p t j", t=BLK)
            nc.gpsimd.affine_select(out=Tm, in_=Tm, compare_op=ALU.not_equal, fill=1.0,
                                    base=0, pattern=[[1, BLK], [-1, BLK]], channel_multiplier=0).then_inc(consts_ready, 1)

            def blocks(a):
                return a.rearrange("p (k m) -> p k m", m=BLK)

            def w_scale(n):
                pool.wait_ge(wn_loaded, 16 * (n + 1))
                pool.wait_ge(wamax, n + 1)
                if n:
                    wait_full(pool, ("w_T", n - 1, 3))
                nc.gpsimd.tensor_tensor(blocks(wx), blocks(wn), wsc[:, 2, :].unsqueeze(2).broadcast_to([P, 64, BLK]), ALU.mult).then_inc(wscaled, 1)

            def w_magic(n):
                pool.wait_ge(wscaled, n + 1)
                pool.wait_ge(wmagic, n + 1)
                linked(nc.gpsimd.tensor_tensor(wx, wx, ww, ALU.add))
                linked(nc.gpsimd.tensor_tensor(wx, wx, ww, ALU.subtract))
                nc.gpsimd.tensor_tensor(blocks(wx), blocks(wx), wsc[:, 1, :].unsqueeze(2).broadcast_to([P, 64, BLK]), ALU.mult).then_inc(wquant, 1)

            def feat(f, i):
                if 1 <= i <= 4:
                    n = FT[i - 1][1]
                    pool.wait_ge(feat_ready, NFT * f + i)
                    if f:
                        wait_full(pool, ("norm", f - 1))
                    nc.gpsimd.tensor_tensor(sq[0:n, i - 1, :], F[0:n, i - 1, :], F[0:n, i - 1, :], ALU.mult).then_inc(squares_ready, 1)

            def decay(f, g):
                wait_drained(pool, ("decay", f, g))
                nc.gpsimd.tensor_tensor(E[:, 4 * g:4 * g + 4, :], E[:, 4 * g:4 * g + 4, :],
                                        upto[:, :].unsqueeze(1).broadcast_to([P, 4, P]), ALU.mult).then_inc(E_masked, 1)

            def norm(f):
                pool.wait_ge(norms_ready, f + 1)
                for n in (slice(0, NH), slice(NH, 2 * NH)):
                    nc.gpsimd.tensor_tensor(smalls[f][:, 6, :, n], smalls[f][:, 5, :, n], powers[:, :, n], ALU.pow).then_inc(roots_ready, 1)

            def diag(f):
                pool.wait_ge(small_loaded, loaded[small_loaded])
                wait_drained(pool, ("gate", f, HALF - 1))
                nc.gpsimd.tensor_tensor(SGs[f][:, :, :], SGs[f][:, :, :], norm_w[:, :].unsqueeze(1).broadcast_to([P, NQ, DV]),
                                        ALU.mult).then_inc(gatew_ready, 1)

            def below(f, i):
                if i in (0, 2):
                    pool.wait_ge(rows_ready if i == 0 else Wl_ready, f + 1)
                    _, lhs, rhs, _, _ = lane_products()[i + 1]
                    nc.gpsimd.tensor_tensor(product_terms(i + 1, lhs, rhs), *factors(lhs, rhs), ALU.mult).then_inc(lane_product, 1)

            def o(f, b):
                pool.wait_ge(ms_ready, HALF * f + b + 1)
                nc.gpsimd.tensor_tensor(smalls[f][:, 9, b, 0:NH], smalls[f][:, 8, b, 0:NH], mhalf[:, 0:NH], ALU.pow).then_inc(rms_ready, 1)

            def y(f, b):
                pool.wait_ge(var_ready, HALF * f + b + 1)
                nc.gpsimd.tensor_tensor(mv[:, b, 1:2], mv[:, b, 1:2], mhalf[:, 0:1], ALU.pow).then_inc(rstd_ready, 1)

            def project(n):
                pool.wait_ge(x1_ready, n + 1)
                wait_ctx(pool, n)
                wait_out_stored(pool, n)
                wait_full(pool, ("w_T", 2, 3))
                nc.gpsimd.tensor_tensor(S[slot_of[n]]["xc"], xs[:, n, :], S[slot_of[n]]["ctx"], ALU.add).then_inc(xc_ready, 1)

            def spread(n):
                st = S[slot_of[n]]["st"]
                wait_drained(pool, ("spread", n))
                nc.gpsimd.tensor_tensor(st[0:LAT, 3:4], st[0:LAT, 2:3], mhalf[0:LAT, 0:1], ALU.pow).then_inc(spread_rstd, 1)

            def residual(n):
                st = S[slot_of[n]]["st"]
                pool.wait_ge(var2_ready, n + 1)
                nc.gpsimd.tensor_tensor(st[:, 5:6], st[:, 5:6], mhalf[:, 0:1], ALU.pow).then_inc(rstd2_ready, 1)

            def quantise_h(n):
                if n == SEQ - 1:
                    return
                d = S[slot_of[n]]
                pool.wait_ge(magic_ready, n + 1)
                nc.gpsimd.tensor_tensor(d["xq"], d["xq"], d["w"], ALU.add).then_inc(hrounded, 1)
                pool.wait_ge(hrounded, 2 * n + 1)
                nc.gpsimd.tensor_tensor(d["xq"], d["xq"], d["w"], ALU.subtract).then_inc(hrounded, 1)
                pool.wait_ge(hrounded, 2 * n + 2)
                nc.gpsimd.tensor_tensor(blocks(d["xq"]), blocks(d["xq"]), d["qs"][:, 1, :].unsqueeze(2).broadcast_to([P, INTER // BLK, BLK]),
                                        ALU.mult).then_inc(hdq_ready, 1)

            def down(n):
                st = S[slot_of[n]]["st"]
                pool.wait_ge(var3_ready, n + 1)
                nc.gpsimd.tensor_tensor(st[:, 5:6], st[:, 5:6], mhalf[:, 0:1], ALU.pow).then_inc(rstd3_ready, 1)

            run({"w_scale": w_scale, "w_magic": w_magic, "feat": feat, "decay": decay, "norm": norm, "diag": diag,
                 "below": below, "o": o, "y": y, "project": project, "spread": spread, "residual": residual,
                 "quantise_h": quantise_h, "down": down})

        @block.scalar
        def _(act):
            def copy(dst, src):
                return nc.scalar.activation(dst, src, ACT.Copy)

            def x_T(f):
                if f:
                    wait_full(act, ("feat", f - 1, NFT - 1))
                    wait_full(act, ("gate", f - 1, HALF - 1))
                for c in range(2):
                    wait_full(act, ("xT", f, c))
                    copy(xT[:, c, :], bank_of(("xT", f, c))[:, :]).then_inc(drained["act"], 1)

            def gate(f, b):
                wait_full(act, ("gate", f, b))
                src = bank_of(("gate", f, b))
                copy(smalls[f][:, 0, b, :], src[:, NH * DV:NH * DV + 2 * NH]).then_inc(ab_raw, 1)
                nc.scalar.activation(SGs[f][:, NH * b:NH * b + NH, :].rearrange("p h d -> p (h d)"), src[:, 0:NH * DV],
                                     ACT.Silu).then_inc(drained["act"], 1)

            def ab(f):
                if f == 0:
                    act.wait_ge(small_loaded, loaded[small_loaded])
                    nc.scalar.activation(expA[:, :], expA[:, :], ACT.Exp).then_inc(expA_ready, 1)
                act.wait_ge(ab_abs, f + 1)
                nc.scalar.activation(smalls[f][:, 2, :, 0:NH], smalls[f][:, 1, :, 0:NH], ACT.Exp).then_inc(ab_exp, 1)
                nc.scalar.activation(smalls[f][:, 2, :, NH:2 * NH], smalls[f][:, 0, :, NH:2 * NH], ACT.Exp, scale=-1.0).then_inc(ab_exp, 1)
                act.wait_ge(ab_plus, f + 1)
                nc.scalar.activation(smalls[f][:, 3, :, 0:NH], smalls[f][:, 3, :, 0:NH], ACT.Ln).then_inc(ab_ln, 1)

            def silu_feat(f, i):
                n = FT[i][1]
                wait_drained(act, ("feat", f, i))
                nc.scalar.activation(F[0:n, i, :], F[0:n, i, :], ACT.Silu).then_inc(feat_ready, 1)

            def feat(f, i):
                n = FT[i][1]
                if i == 0:
                    act.wait_ge(conv_loaded, loaded[conv_loaded])
                    if f:
                        wait_full(act, ("kq", f - 1, 1, NH - 1))
                        wait_full(act, ("vT", f - 1, HALF - 1))
                wait_full(act, ("feat", f, i))
                nc.scalar.activation(F[0:n, i, :], bank_of(("feat", f, i))[0:n, :], ACT.Copy,
                                     scale=conv_w[0:n, i, TAPS - 1:TAPS]).then_inc(conv_started, 1)
                if i:
                    silu_feat(f, i - 1)

            def feat_end(f):
                silu_feat(f, NFT - 1)

            def decay_in(f, b):
                act.wait_ge(consts_ready, 1)
                act.wait_ge(g_ready, f + 1)
                if f and b == 0:
                    wait_full(act, ("decay", f - 1, NQ // 4 - 1))
                for h in range(NH):
                    ins = nc.scalar.activation(GU[:, NH * b + h, :], upto[:, :], ACT.Copy, scale=smalls[f][:, 4, b, h:h + 1])
                ins.then_inc(GU_ready, 1)

            def decay(f, g):
                wait_full(act, ("decay", f, g))
                if f and g == 0:
                    act.wait_ge(inverse_out, f)
                nc.scalar.activation(E[:, 4 * g:4 * g + 4, :].rearrange("p q t -> p (q t)"),
                                     bank_of(("decay", f, g))[:, :], ACT.Exp).then_inc(drained["act"], 1)

            def diag_in(f, j):
                if f:
                    act.wait_ge(inverse_ready, f)
                wait_drained(act, ("kq", f, j, NH - 1))
                qs = slice(2 * NH * j, 2 * NH * j + 2 * NH)
                for g in range(P // BLK):
                    r = slice(BLK * g, BLK * g + BLK)
                    copy(CD[r, :, qs].rearrange("p c q -> p q c"), MP[r, qs, 0, r]).then_inc(diag_copied, 1)

            def inverse(f):
                act.wait_ge(inverse_out, f + 1)
                if f:
                    wait_full(act, ("w", f - 1, P // BLK - 1, NQ // GQ - 1))
                copy(TT[:, :, :], CT[:, :, 0:NQ].rearrange("p c q -> p q c")).then_inc(inverse_ready, 1)

            def solve(f, k):
                r = slice(BLK * k, BLK * k + BLK)
                for g in range(NQ // GQ):
                    wait_full(act, ("w", f, k, g))
                    copy(group(om, g, r), bank_of(("w", f, k, g))[r, :]).then_inc(drained["act"], 1)

            def o(f, b):
                wait_full(act, ("o", f, HALF - 1))
                heads = slice(NH * b, NH * b + NH)
                for dst, func in ((osq, ACT.Square), (osb, ACT.Copy)):
                    ins = nc.scalar.activation(dst[:, heads, :].rearrange("p h d -> p (h d)"), bank_of(("o", f, b))[:, 0:NH * DV], func)
                    ins.then_inc(o_squared if func == ACT.Square else drained["act"], 1)

            def og(f, b):
                wait_full(act, ("og", f, b))
                copy(ogT[:, b, :, :].rearrange("p c t -> p (c t)"), bank_of(("og", f, b))[:, 0:3 * P]).then_inc(drained["act"], 1)

            def w_T(n):
                for i in range(4):
                    key = ("w_T", n, i)
                    wait_full(act, key)
                    if n == 2:
                        dst = downT[:, 2 * i:2 * i + 2, :].rearrange("p k n -> p (k n)")
                    else:
                        dst = (gateT, upT)[n][:, i % 2, 512 * (i // 2):512 * (i // 2) + 512]
                    copy(dst, bank_of(key)[:, :]).then_inc(drained["act"], 1)

            def project(n):
                act.wait_ge(cross_loaded, loaded[cross_loaded])
                act.wait_ge(xc_ready, n + 1)
                wait_full(act, ("thph", n))
                ps, th = bank_of(("thph", n)), S[slot_of[n]]["thph"]
                nc.scalar.activation(th[:, 0, :], ps[0:LAT, 0:HID], ACT.Identity, bias=th_b[:, 0:1])
                nc.scalar.activation(th[:, 1, :], ps[0:LAT, HID:2 * HID], ACT.Identity, bias=ph_b[:, 0:1]).then_inc(drained["act"], 1)

            def scores(n):
                d = S[slot_of[n]]
                act.wait_ge(max_ready, n + 1)
                for t in range(2):
                    ins = nc.scalar.activation(d["p"][:, t, :], bank_of(("scores", n))[:, HID * t:HID * t + HID], ACT.Exp,
                                               bias=d["sm"][:, t:t + 1], accum_out=d["sm"][:, 2 + t:3 + t])
                ins.then_inc(drained["act"], 1)

            def attend(n):
                wait_full(act, ("attend", n))
                copy(S[slot_of[n]]["pT"].rearrange("p k t -> p (k t)"), bank_of(("attend", n))[:, :]).then_inc(drained["act"], 1)

            def mix(n):
                wait_full(act, ("mix", n))
                copy(S[slot_of[n]]["h1"], bank_of(("mix", n))[0:LAT, 0:HID]).then_inc(drained["act"], 1)

            def affine(n):
                h1 = S[slot_of[n]]["h1"]
                act.wait_ge(affine_ready, n + 1)
                nc.scalar.activation(h1, h1, ACT.Relu).then_inc(relu_ready, 1)

            def quantise(n):
                wait_full(act, ("quantise", n))
                copy(S[slot_of[n]]["x2T"].rearrange("p k t -> p (k t)"), bank_of(("quantise", n))[:, 0:HID]).then_inc(drained["act"], 1)

            def gate_up(n):
                for j in range(2):
                    wait_full(act, ("gate_h", n, j))
                    nc.scalar.activation(S[slot_of[n]]["hh"][:, 512 * j:512 * j + 512], bank_of(("gate_h", n, j))[:, :],
                                         ACT.Silu).then_inc(drained["act"], 1)

            def transpose_h(n):
                for j in range(2):
                    wait_full(act, ("transpose_h", n, j))
                    copy(S[slot_of[n]]["hT"][:, 4 * j:4 * j + 4, :].rearrange("p k t -> p (k t)"),
                         bank_of(("transpose_h", n, j))[:, :]).then_inc(drained["act"], 1)

            run({"xT": x_T, "gate": gate, "ab": ab, "feat": feat, "feat_end": feat_end, "decay_in": decay_in, "decay": decay, "diag_in": diag_in,
                 "inverse": inverse, "solve": solve, "o": o, "og": og, "w_T": w_T, "project": project, "scores": scores,
                 "attend": attend, "mix": mix, "affine": affine, "quantise": quantise, "gate_up": gate_up,
                 "transpose_h": transpose_h})

        @block.vector
        def _(dve):
            link = [0]

            def linked(ins):
                link[0] += 1
                ins.then_inc(dve_link, 1)
                dve.wait_ge(dve_link, link[0])

            def blocks(a):
                return a.rearrange("p (k m) -> p k m", m=BLK)

            def w_scale(n):
                dve.wait_ge(wn_loaded, 16 * (n + 1))
                if n:
                    dve.wait_ge(wquant, n)
                linked(nc.vector.tensor_reduce(wsc[:, 0, :], blocks(wn), X, ALU.max, apply_absolute_value=True))
                linked(nc.vector.tensor_scalar(wsc[:, 1, :], wsc[:, 0, :], 1.0 / FP8_MAX, SCALE_MIN, ALU.mult, ALU.max))
                nc.vector.reciprocal(wsc[:, 2, :], wsc[:, 1, :]).then_inc(wamax, 1)

            def round_to(w, xq):
                linked(nc.vector.tensor_scalar(w.bitcast(I32), xq.bitcast(I32), EXP_MASK, HALF_BIT,
                                               ALU.bitwise_and, ALU.bitwise_or))
                return nc.vector.tensor_scalar(w, w, 1.5 * MIN_NORMAL, MAGIC_SHIFT, ALU.max, ALU.mult)

            def w_magic(n):
                dve.wait_ge(wscaled, n + 1)
                round_to(ww, wx).then_inc(wmagic, 1)

            def ab(f):
                a, b = slice(0, NH), slice(NH, 2 * NH)
                dve.wait_ge(ab_raw, HALF * (f + 1))
                dve.wait_ge(small_loaded, loaded[small_loaded])
                nc.vector.tensor_tensor(smalls[f][:, 0, :, a], smalls[f][:, 0, :, a], dt_b[:, :].unsqueeze(1).broadcast_to([P, HALF, NH]),
                                        ALU.add).then_inc(ab_biased, 1)
                dve.wait_ge(ab_biased, f + 1)
                nc.vector.scalar_tensor_tensor(smalls[f][:, 1, :, a], smalls[f][:, 0, :, a], -1.0, smalls[f][:, 0, :, a], ALU.mult, ALU.min).then_inc(ab_abs, 1)
                dve.wait_ge(ab_exp, 2 * (f + 1))
                nc.vector.tensor_scalar(smalls[f][:, 3], smalls[f][:, 2], 1.0, None, ALU.add).then_inc(ab_plus, 1)
                dve.wait_ge(ab_plus, f + 1)
                linked(nc.vector.reciprocal(smalls[f][:, 4, :, b], smalls[f][:, 3, :, b]))
                dve.wait_ge(ab_ln, f + 1)
                linked(nc.vector.scalar_tensor_tensor(smalls[f][:, 4, :, a], smalls[f][:, 0, :, a], 0.0, smalls[f][:, 3, :, a], ALU.max, ALU.add))
                dve.wait_ge(expA_ready, 1)
                nc.vector.scalar_tensor_tensor(smalls[f][:, 4, :, a], smalls[f][:, 4, :, a], -1.0,
                                               expA[:, :].unsqueeze(1).broadcast_to([P, HALF, NH]), ALU.mult, ALU.mult).then_inc(g_ready, 1)

            def feat(f, i):
                n = FT[i][1]
                src = bank_of(("feat", f, i))[0:n, :].rearrange("p (b t) -> p b t", b=HALF)
                dst = F[0:n, i, :].rearrange("p (b t) -> p b t", b=HALF)
                dve.wait_ge(conv_started, NFT * f + i + 1)
                for tap in range(TAPS - 2, -1, -1):
                    d = TAPS - 1 - tap
                    ins = nc.vector.scalar_tensor_tensor(dst[:, :, d:P], src[:, :, 0:P - d], conv_w[0:n, i, tap:tap + 1],
                                                         dst[:, :, d:P], ALU.mult, ALU.add)
                    if tap:
                        linked(ins)
                ins.then_inc(drained["dve"], 1)

            def norm(f):
                wait_full(dve, ("norm", f))
                nc.vector.tensor_copy(smalls[f][:, 5], bank_of(("norm", f))[:, 0:HALF * 2 * NH].rearrange("p (b n) -> p b n", b=HALF)).then_inc(drained["dve"], 1)
                wait_drained(dve, ("norm", f))
                dve.wait_ge(g_ready, f + 1)
                c = smalls[f][:, 7, :, 0:NH]
                nc.vector.reciprocal(c, smalls[f][:, 5, :, 0:NH]).then_inc(norms_ready, 1)
                dve.wait_ge(norms_ready, f + 1)
                linked(nc.vector.tensor_tensor(c, c, smalls[f][:, 4, :, NH:2 * NH], ALU.mult))

            def vT(f, b):
                dve.wait_ge(roots_ready, 2 * f + 1)
                if f and b == 0:
                    wait_full(dve, ("y", f - 1, HALF - 1))
                wait_full(dve, ("vT", f, b))
                nc.vector.tensor_tensor(u[:, NH * b:NH * b + NH, :], bank_of(("vT", f, b))[:, 0:NH * DV].rearrange("p (h d) -> p h d", h=NH),
                                        smalls[f][:, 6, b, 0:NH].unsqueeze(2).broadcast_to([P, NH, DV]), ALU.mult).then_inc(drained["dve"], 1)

            def kq(f, j, h):
                if (j, h) == (0, 0):
                    if f:
                        wait_full(dve, ("o", f - 1, HALF - 1))
                    dve.wait_ge(E_masked, NQ // 4 * (f + 1))
                wait_full(dve, ("kq", f, j, h))
                for k in range(2):
                    b = 2 * j + k
                    q = NH * b + h
                    src = bank_of(("kq", f, j, h))[:, 2 * P * k:2 * P * k + 2 * P].rearrange("p (a t) -> p a t", a=2)
                    ins = nc.vector.scalar_tensor_tensor(MP[:, q], src, smalls[f][:, 7, b, h:h + 1],
                                                         E[:, q, :].unsqueeze(1).broadcast_to([P, 2, P]), ALU.mult, ALU.mult)
                ins.then_inc(drained["dve"], 1)

            def diag(f):
                dve.wait_ge(consts_ready, 1)
                dve.wait_ge(diag_copied, HALF // 2 * (P // BLK) * (f + 1))
                linked(nc.vector.transpose(L[:, 0:BLK * BLK], CD[:, :, :].rearrange("p c q -> p (c q)")))

            def rows(f, i):
                M2, T2 = (a[:, :].rearrange("p (a m) -> p a m", a=2) for a in (L, T))
                for t in range(*ROWS[i]):
                    pr = prod[:, 0:2 * t * t].rearrange("p (a c j) -> p a c j", a=2, c=t)
                    above = T2[:, :, 0:BLK * t].rearrange("p a (j c) -> p a c j", c=BLK)[:, :, 0:t, :]
                    linked(nc.vector.tensor_tensor(pr, M2[:, :, BLK * t:BLK * t + t].unsqueeze(2).broadcast_to([P, 2, t, t]),
                                                   above, ALU.mult))
                    ins = nc.vector.tensor_reduce(T2[:, :, BLK * t:BLK * t + t], pr, X, ALU.add, negate=True)
                    if t < SUB - 1:
                        linked(ins)
                    else:
                        ins.then_inc(rows_ready, 1)
                        dve.wait_ge(rows_ready, f + 1)

            def below(f, i):
                for n, (dst, lhs, rhs, negate, by_pool) in enumerate(lane_products()):
                    if n == i:
                        pr = product_terms(n, lhs, rhs)
                        if by_pool:
                            dve.wait_ge(lane_product, 2 * f + (1 if n == 1 else 2))
                        else:
                            linked(nc.vector.tensor_tensor(pr, *factors(lhs, rhs), ALU.mult))
                        ins = nc.vector.tensor_reduce(dst, pr, X, ALU.add, negate=negate)
                        if n == 1:
                            ins.then_inc(Wl_ready, 1)
                            dve.wait_ge(Wl_ready, f + 1)
                        else:
                            linked(ins)

            def inverse(f):
                if f:
                    dve.wait_ge(inverse_ready, f)
                nc.vector.transpose(CT[:, :, :].rearrange("p c q -> p (c q)"), T[:, 0:BLK * BLK]).then_inc(inverse_out, 1)

            def solve(f, k):
                r = slice(BLK * k, BLK * k + BLK)
                if k:
                    for g in range(NQ // GQ):
                        wait_full(dve, ("r", f, k, g))
                        nc.vector.tensor_tensor(group(R, g, r), group(u, g, r), bank_of(("r", f, k, g))[r, :], ALU.subtract).then_inc(drained["dve"], 1)

            def o(f, b):
                dve.wait_ge(o_squared, HALF * f + b + 1)
                dve.wait_ge(roots_ready, 2 * (f + 1))
                s8, rq = smalls[f][:, 8, b, 0:NH], smalls[f][:, 6, b, NH:2 * NH]
                linked(nc.vector.tensor_reduce(s8, osq[:, NH * b:NH * b + NH, :], X, ALU.add))
                linked(nc.vector.tensor_tensor(s8, s8, rq, ALU.mult))
                linked(nc.vector.scalar_tensor_tensor(s8, s8, 1.0 / (DV * DK), rq, ALU.mult, ALU.mult))
                nc.vector.tensor_scalar(s8, s8, EPS, None, ALU.add).then_inc(ms_ready, 1)

            def o_scale(f, b):
                s9, rq, heads = smalls[f][:, 9, b, 0:NH], smalls[f][:, 6, b, NH:2 * NH], slice(NH * b, NH * b + NH)
                dve.wait_ge(rms_ready, HALF * f + b + 1)
                linked(nc.vector.scalar_tensor_tensor(s9, s9, float(DK) ** -0.5, rq, ALU.mult, ALU.mult))
                wait_drained(dve, ("o", f, b))
                dve.wait_ge(gatew_ready, f + 1)
                linked(nc.vector.tensor_tensor(osq[:, heads, :], osb[:, heads, :], s9.unsqueeze(2).broadcast_to([P, NH, DV]), ALU.mult))
                nc.vector.tensor_tensor(osb[:, heads, :], osq[:, heads, :], SGs[f][:, heads, :], ALU.mult).then_inc(og_ready, 1)

            def y(f, b):
                dve.wait_ge(x_loaded[f], 16)
                wait_full(dve, ("y", f, b))
                xb = xs[:, HALF * f + b, :]
                nc.vector.tensor_tensor(xb, xb, bank_of(("y", f, b))[:, 0:HID], ALU.add).then_inc(drained["dve"], 1)
                wait_drained(dve, ("y", f, b))
                linked(nc.vector.bn_stats(stats[:, b, :], xb))
                linked(nc.vector.bn_aggr(mv[:, b, :], stats[:, b, :]))
                nc.vector.tensor_scalar(mv[:, b, 1:2], mv[:, b, 1:2], EPS, None, ALU.add).then_inc(var_ready, 1)

            def x1(f, b):
                n = HALF * f + b
                dve.wait_ge(rstd_ready, n + 1)
                nc.vector.tensor_scalar(xs[:, n, :], xs[:, n, :], mv[:, b, 0:1], mv[:, b, 1:2], ALU.subtract, ALU.mult).then_inc(x1_ready, 1)

            def xw_T():
                wait_full(dve, ("xw", 1))
                nc.vector.tensor_copy(xw[:, :, :], bank_of(("xw", 0))[:, 0:3 * LAT].rearrange("p (i l) -> p i l", i=3)).then_inc(drained["dve"], 1)
                nc.vector.tensor_copy(owT[:, :], bank_of(("xw", 1))[0:LAT, 0:P]).then_inc(drained["dve"], 1)

            def project(n):
                d = S[slot_of[n]]
                dve.wait_ge(cross_loaded, loaded[cross_loaded])
                dve.wait_ge(xc_ready, n + 1)
                wait_full(dve, ("g", n))
                nc.vector.tensor_tensor(d["g"], bank_of(("g", n))[:, 0:2 * LAT].rearrange("p (k l) -> p k l", k=2),
                                        g_bb[:, :].unsqueeze(1).broadcast_to([P, 2, LAT]), ALU.add).then_inc(drained["dve"], 1)

            def scores(n):
                wait_full(dve, ("scores", n))
                nc.vector.tensor_reduce(S[slot_of[n]]["sm"][:, 0:2], bank_of(("scores", n))[:, :].rearrange("p (t s) -> p t s", t=2), X, ALU.max,
                                        negate=True).then_inc(max_ready, 1)

            def attend(n):
                d = S[slot_of[n]]
                wait_drained(dve, ("scores", n))
                linked(nc.vector.reciprocal(d["sm"][:, 4:6], d["sm"][:, 2:4]))
                for t in range(2):
                    nc.vector.tensor_scalar(d["p"][:, t, :], d["p"][:, t, :], d["sm"][:, 4 + t:5 + t], None, ALU.mult).then_inc(p_ready, 1)

            def stats_of(n):
                d = S[slot_of[n]]
                wait_drained(dve, ("mix", n))
                linked(nc.vector.bn_stats(d["bs"][0:LAT, :], d["h1"]))
                nc.vector.bn_aggr(d["st"][0:LAT, 0:2], d["bs"][0:LAT, :]).then_inc(mean_ready, 1)

            def centre(n):
                d = S[slot_of[n]]
                st = d["st"]
                dve.wait_ge(mean_ready, n + 1)
                wait_full(dve, ("centre", n))
                mu = bank_of(("centre", n))[0:LAT, 0:1]
                linked(nc.vector.tensor_tensor(st[0:LAT, 6:7], st[0:LAT, 0:1], mu, ALU.subtract))
                linked(nc.vector.tensor_tensor(st[0:LAT, 6:7], st[0:LAT, 6:7], st[0:LAT, 6:7], ALU.mult))
                nc.vector.tensor_tensor(st[0:LAT, 1:2], st[0:LAT, 1:2], st[0:LAT, 6:7], ALU.add).then_inc(dev_ready, 1)
                nc.vector.scalar_tensor_tensor(d["h1"], d["h1"], mu, gamma[:, :], ALU.subtract, ALU.mult).then_inc(drained["dve"], 1)

            def spread(n):
                wait_full(dve, ("spread", n))
                nc.vector.tensor_scalar(S[slot_of[n]]["st"][0:LAT, 2:3], bank_of(("spread", n))[0:LAT, 0:1], EPS, None, ALU.add).then_inc(drained["dve"], 1)

            def affine(n):
                d = S[slot_of[n]]
                dve.wait_ge(spread_rstd, n + 1)
                wait_drained(dve, ("centre", n))
                nc.vector.scalar_tensor_tensor(d["h1"], d["h1"], d["st"][0:LAT, 3:4], beta_ln[:, :], ALU.mult, ALU.add).then_inc(affine_ready, 1)

            def layer_stats(d, done):
                linked(nc.vector.bn_stats(d["bs"][:, :], d["x2"]))
                linked(nc.vector.bn_aggr(d["st"][:, 4:6], d["bs"][:, :]))
                nc.vector.tensor_scalar(d["st"][:, 5:6], d["st"][:, 5:6], EPS, None, ALU.add).then_inc(done, 1)

            def residual(n):
                d = S[slot_of[n]]
                wait_full(dve, ("residual", n))
                nc.vector.scalar_tensor_tensor(d["x2"], bank_of(("residual", n))[:, 0:HID], o_b[:, 0:1], d["xc"], ALU.add, ALU.add).then_inc(drained["dve"], 1)
                wait_drained(dve, ("residual", n))
                layer_stats(d, var2_ready)

            def scaled(d, src, xq, nb):
                v, qs = blocks(src), d["qs"]
                linked(nc.vector.tensor_reduce(qs[:, 0, 0:nb], v, X, ALU.max, apply_absolute_value=True))
                linked(nc.vector.tensor_scalar(qs[:, 1, 0:nb], qs[:, 0, 0:nb], 1.0 / FP8_MAX, SCALE_MIN, ALU.mult, ALU.max))
                linked(nc.vector.reciprocal(qs[:, 2, 0:nb], qs[:, 1, 0:nb]))
                linked(nc.vector.tensor_tensor(blocks(xq), v, qs[:, 2, 0:nb].unsqueeze(2).broadcast_to([P, nb, BLK]), ALU.mult))

            def times_scale(d, xq, nb):
                v = blocks(xq)
                return nc.vector.tensor_tensor(v, v, d["qs"][:, 1, 0:nb].unsqueeze(2).broadcast_to([P, nb, BLK]), ALU.mult)

            def quantise(n):
                d = S[slot_of[n]]
                dve.wait_ge(rstd2_ready, n + 1)
                nc.vector.tensor_scalar(d["x2"], d["x2"], d["st"][:, 4:5], d["st"][:, 5:6], ALU.subtract, ALU.mult).then_inc(x2_ready, 1)
                dve.wait_ge(x2_ready, n + 1)
                xq, w = d["xq"][:, 0:HID], d["w"][:, 0:HID]
                if slot_of[n] < 2 and n < HALF:
                    wait_full(dve, ("decay", 1, NQ // 4 - 1))
                    wait_full(dve, ("norm", 1))
                scaled(d, d["x2"], xq, HID // BLK)
                linked(round_to(w, xq))
                linked(nc.vector.tensor_tensor(xq, xq, w, ALU.add))
                linked(nc.vector.tensor_tensor(xq, xq, w, ALU.subtract))
                times_scale(d, xq, HID // BLK).then_inc(xdq_ready, 1)

            def gate_up(n):
                d = S[slot_of[n]]
                for j in range(2):
                    h = d["hh"][:, 512 * j:512 * j + 512]
                    wait_drained(dve, ("gate_h", n, j))
                    wait_full(dve, ("up_h", n, j))
                    nc.vector.tensor_tensor(h, h, bank_of(("up_h", n, j))[:, :], ALU.mult).then_inc(drained["dve"], 1)

            def quantise_h(n):
                d = S[slot_of[n]]
                wait_drained(dve, ("up_h", n, 1))
                scaled(d, d["hh"], d["xq"], INTER // BLK)
                if n < SEQ - 1:
                    round_to(d["w"], d["xq"]).then_inc(magic_ready, 1)
                else:
                    linked(round_to(d["w"], d["xq"]))
                    linked(nc.vector.tensor_tensor(d["xq"], d["xq"], d["w"], ALU.add))
                    linked(nc.vector.tensor_tensor(d["xq"], d["xq"], d["w"], ALU.subtract))
                    times_scale(d, d["xq"], INTER // BLK).then_inc(last_hdq_ready, 1)

            def down(n):
                d = S[slot_of[n]]
                wait_full(dve, ("down", n))
                nc.vector.tensor_tensor(d["x2"], d["x2"], bank_of(("down", n))[:, 0:HID], ALU.add).then_inc(drained["dve"], 1)
                wait_drained(dve, ("down", n))
                layer_stats(d, var3_ready)

            def final(n):
                d = S[slot_of[n]]
                dve.wait_ge(rstd3_ready, n + 1)
                nc.vector.tensor_scalar(d["x2"], d["x2"], d["st"][:, 4:5], d["st"][:, 5:6], ALU.subtract, ALU.mult).then_inc(final_ready, 1)

            run({"w_scale": w_scale, "w_magic": w_magic, "ab": ab, "feat": feat, "norm": norm,
                 "vT": vT, "kq": kq, "diag": diag, "rows": rows, "below": below, "inverse": inverse, "solve": solve,
                 "o": o, "o_scale": o_scale, "y": y, "x1": x1, "xw": xw_T, "project": project, "scores": scores, "attend": attend,
                 "stats": stats_of, "centre": centre, "spread": spread, "affine": affine, "residual": residual,
                 "quantise": quantise, "gate_up": gate_up, "quantise_h": quantise_h,
                 "down": down, "final": final})

        @block.tensor
        def _(pe):
            mm, tr = nc.tensor.matmul, nc.tensor.transpose

            def x_T(f):
                pe.wait_ge(x_loaded[f], 16)
                for c in range(2):
                    wait_free(pe, ("xT", f, c))
                    for b in range(HALF):
                        ins = tr(bank_of(("xT", f, c))[:, P * b:P * b + P], xs[:, HALF * f + b, P * c:P * c + P], ident[:, :])
                    ins.then_inc(psum_full, 1)

            def gate(f, b):
                key = ("gate", f, b)
                if b == 0:
                    pe.wait_ge(wg_loaded, loaded[wg_loaded])
                    for c in range(2):
                        wait_drained(pe, ("xT", f, c))
                wait_free(pe, key)
                for c in range(2):
                    ins = mm(bank_of(key)[:, 0:NH * DV + 2 * NH], xT[:, c, P * b:P * b + P], W_g[:, c, :], start=(c == 0), stop=(c == 1))
                ins.then_inc(psum_full, 1)

            def feat(f, i):
                key = ("feat", f, i)
                at, n = FT[i]
                if i == 0:
                    pe.wait_ge(wf_loaded, loaded[wf_loaded])
                    for c in range(2):
                        wait_drained(pe, ("xT", f, c))
                wait_free(pe, key)
                for c in range(2):
                    ins = mm(bank_of(key)[0:n, :], W_f[:, c, at:at + n], xT[:, c, :], start=(c == 0), stop=(c == 1))
                ins.then_inc(psum_full, 1)

            def decay(f, g):
                pe.wait_ge(consts_ready, 1)
                pe.wait_ge(GU_ready, HALF * f + (4 * g + 3) // NH + 1)
                wait_free(pe, ("decay", f, g))
                mm(bank_of(("decay", f, g))[:, :], after[:, :], GU[:, 4 * g:4 * g + 4, :], start=True, stop=True).then_inc(psum_full, 1)

            def norm(f):
                pe.wait_ge(consts_ready, 1)
                pe.wait_ge(squares_ready, 4 * (f + 1))
                wait_free(pe, ("norm", f))
                for b in range(HALF):
                    for i, (c0, m) in enumerate([(0, 4), (NH, 4), (4, 2), (NH + 4, 2)]):
                        c0 += 2 * NH * b
                        n = DK * m
                        ins = mm(bank_of(("norm", f))[:, c0:c0 + m], sq[0:n, i, P * b:P * b + P], headsel[0:n, 0:m], start=True, stop=True)
                ins.then_inc(psum_full, 1)

            def vT(f, b):
                pe.wait_ge(feat_ready, NFT * (f + 1))
                wait_free(pe, ("vT", f, b))
                for c in range(3):
                    ins = tr(bank_of(("vT", f, b))[:, P * c:P * c + P], F[:, 4 + c, P * b:P * b + P], ident[:, :])
                ins.then_inc(psum_full, 1)

            def kq(f, j, h):
                key = ("kq", f, j, h)
                wait_free(pe, key)
                r = slice(DK * (h % 4), DK * (h % 4) + DK)
                i = 2 * (h // 4)
                for k in range(2):
                    t = slice(P * (2 * j + k), P * (2 * j + k) + P)
                    ins = mm(bank_of(key)[:, 2 * P * k:2 * P * k + 2 * P], F[r, i, t], F[r, i:i + 2, t], start=True, stop=True)
                ins.then_inc(psum_full, 1)

            def products(key, rows, lhs, rhs, g):
                wait_free(pe, key)
                for q in range(GQ * g, GQ * g + GQ):
                    ins = mm(bank_of(key)[rows, DV * (q % GQ):DV * (q % GQ) + DV], lhs(q), rhs(q), start=True, stop=True)
                ins.then_inc(psum_full, 1)

            def solve(f, k):
                r, up = slice(BLK * k, BLK * k + BLK), slice(0, BLK * k)
                if k == 0:
                    wait_drained(pe, ("vT", f, HALF - 1))
                    pe.wait_ge(inverse_ready, f + 1)
                else:
                    for g in range(NQ // GQ):
                        wait_drained(pe, ("w", f, k - 1, g))
                        products(("r", f, k, g), r, lambda q: MP[up, q, 0, r], lambda q: om[up, q, :], g)
                for g in range(NQ // GQ):
                    if k:
                        wait_drained(pe, ("r", f, k, g))
                    products(("w", f, k, g), r, lambda q: TT[r, q, :], lambda q: (R if k else u)[r, q, :], g)

            def o(f, b):
                key = ("o", f, b)
                if b == 0:
                    wait_drained(pe, ("w", f, P // BLK - 1, NQ // GQ - 1))
                wait_free(pe, key)
                for h in range(NH):
                    q = NH * b + h
                    ins = mm(bank_of(key)[:, DV * h:DV * h + DV], MP[:, q, 1, :], om[:, q, :], start=True, stop=True)
                ins.then_inc(psum_full, 1)

            def og(f, b):
                key = ("og", f, b)
                pe.wait_ge(og_ready, HALF * f + b + 1)
                wait_free(pe, key)
                src = osb[:, NH * b:NH * b + NH, :].rearrange("p h d -> p (h d)")
                for c in range(3):
                    ins = tr(bank_of(key)[:, P * c:P * c + P], src[:, P * c:P * c + P], ident[:, :])
                ins.then_inc(psum_full, 1)

            def y(f, b):
                pe.wait_ge(wo_loaded, loaded[wo_loaded])
                key = ("y", f, b)
                wait_drained(pe, ("og", f, b))
                wait_free(pe, key)
                for c in range(3):
                    ins = mm(bank_of(key)[:, 0:HID], ogT[:, b, c, :], W_o[:, c, :], start=(c == 0), stop=(c == 2))
                ins.then_inc(psum_full, 1)

            def w_T(n):
                pe.wait_ge(wquant, n + 1)
                for i in range(4):
                    key = ("w_T", n, i)
                    wait_free(pe, key)
                    for m in range(4):
                        if n == 2:
                            k, t = 2 * i + m // 2, m % 2
                            src = wx[:, INTER * t + P * k:INTER * t + P * k + P]
                        else:
                            t = 4 * (i // 2) + m
                            src = wx[:, HID * t + P * (i % 2):HID * t + P * (i % 2) + P]
                        ins = tr(bank_of(key)[:, P * m:P * m + P], src, ident[:, :])
                    ins.then_inc(psum_full, 1)

            def xw_T():
                pe.wait_ge(cross_loaded, loaded[cross_loaded])
                wait_free(pe, ("xw", 0))
                for i in range(3):
                    ins = tr(bank_of(("xw", 0))[:, LAT * i:LAT * i + LAT], xw_in[:, i, :], ident[0:LAT, 0:LAT])
                ins.then_inc(psum_full, 1)
                wait_free(pe, ("xw", 1))
                tr(bank_of(("xw", 1))[0:LAT, 0:P], ow_in[:, :], ident[:, :]).then_inc(psum_full, 1)

            def project(n):
                wait_drained(pe, ("xw", 1))
                wait_free(pe, ("thph", n))
                wait_ctx(pe, n)
                pe.wait_ge(x1_ready, n + 1)
                ps = bank_of(("thph", n))
                mm(ps[0:LAT, 0:HID], xw[:, 0, :], S[slot_of[n]]["ctx"], start=True, stop=True)
                mm(ps[0:LAT, HID:2 * HID], xw[:, 1, :], xs[:, n, :], start=True, stop=True).then_inc(psum_full, 1)
                wait_free(pe, ("g", n))
                for t in range(2):
                    ins = mm(bank_of(("g", n))[:, LAT * t:LAT * t + LAT], xs[:, n, P * t:P * t + P], xw[:, 2, :], start=True, stop=True)
                ins.then_inc(psum_full, 1)

            def scores(n):
                th = S[slot_of[n]]["thph"]
                wait_free(pe, ("scores", n))
                wait_drained(pe, ("thph", n))
                for t in range(2):
                    ins = mm(bank_of(("scores", n))[:, HID * t:HID * t + HID], th[:, 0, P * t:P * t + P], th[:, 1, :], start=True, stop=True)
                ins.then_inc(psum_full, 1)

            def attend(n):
                wait_free(pe, ("attend", n))
                pe.wait_ge(p_ready, 2 * (n + 1))
                for k in range(2):
                    for t in range(2):
                        ins = tr(bank_of(("attend", n))[:, HID * k + P * t:HID * k + P * t + P],
                                 S[slot_of[n]]["p"][:, t, P * k:P * k + P], ident[:, :])
                ins.then_inc(psum_full, 1)

            def mix(n):
                d = S[slot_of[n]]
                wait_free(pe, ("mix", n))
                wait_drained(pe, ("attend", n))
                wait_drained(pe, ("g", n))
                for k in range(2):
                    ins = mm(bank_of(("mix", n))[0:LAT, 0:HID], d["g"][:, k, :], d["pT"][:, k, :], start=(k == 0), stop=(k == 1))
                ins.then_inc(psum_full, 1)

            def centre(n):
                wait_free(pe, ("centre", n))
                pe.wait_ge(mean_ready, n + 1)
                mm(bank_of(("centre", n))[0:LAT, 0:1], mean64[:, :], S[slot_of[n]]["st"][0:LAT, 0:1], start=True, stop=True).then_inc(psum_full, 1)

            def spread(n):
                wait_free(pe, ("spread", n))
                pe.wait_ge(dev_ready, n + 1)
                mm(bank_of(("spread", n))[0:LAT, 0:1], mean64[:, :], S[slot_of[n]]["st"][0:LAT, 1:2], start=True, stop=True).then_inc(psum_full, 1)

            def residual(n):
                wait_free(pe, ("residual", n))
                pe.wait_ge(relu_ready, n + 1)
                mm(bank_of(("residual", n))[:, 0:HID], owT[:, :], S[slot_of[n]]["h1"], start=True, stop=True).then_inc(psum_full, 1)

            def quantise(n):
                wait_free(pe, ("quantise", n))
                pe.wait_ge(xdq_ready, n + 1)
                for k in range(2):
                    ins = tr(bank_of(("quantise", n))[:, P * k:P * k + P], S[slot_of[n]]["xq"][:, P * k:P * k + P], ident[:, :])
                ins.then_inc(psum_full, 1)

            def gate_up(n):
                wait_drained(pe, ("quantise", n))
                for j in range(2):
                    for name, wt in (("gate_h", gateT), ("up_h", upT)):
                        key = (name, n, j)
                        wait_free(pe, key)
                        for k in range(2):
                            ins = mm(bank_of(key)[:, :], S[slot_of[n]]["x2T"][:, k, :], wt[:, k, 512 * j:512 * j + 512], start=(k == 0), stop=(k == 1))
                        ins.then_inc(psum_full, 1)

            def transpose_h(n):
                if n < SEQ - 1:
                    pe.wait_ge(hdq_ready, n + 1)
                else:
                    pe.wait_ge(last_hdq_ready, 1)
                for j in range(2):
                    key = ("transpose_h", n, j)
                    wait_free(pe, key)
                    for m in range(4):
                        k = 4 * j + m
                        ins = tr(bank_of(key)[:, P * m:P * m + P], S[slot_of[n]]["xq"][:, P * k:P * k + P], ident[:, :])
                    ins.then_inc(psum_full, 1)

            def down(n):
                wait_free(pe, ("down", n))
                for k in range(INTER // P):
                    if k % 4 == 0:
                        wait_drained(pe, ("transpose_h", n, k // 4))
                    ins = mm(bank_of(("down", n))[:, 0:HID], S[slot_of[n]]["hT"][:, k, :], downT[:, k, :], start=(k == 0), stop=(k == INTER // P - 1))
                ins.then_inc(psum_full, 1)

            pe.wait_ge(ident_ready, 1)
            run({"xT": x_T, "gate": gate, "feat": feat, "decay": decay, "norm": norm, "vT": vT, "kq": kq, "solve": solve,
                 "o": o, "og": og, "y": y, "w_T": w_T, "xw": xw_T, "project": project, "scores": scores,
                 "attend": attend, "mix": mix, "centre": centre, "spread": spread, "residual": residual,
                 "quantise": quantise, "gate_up": gate_up, "transpose_h": transpose_h, "down": down})


_INS = ["x", "ctx_2048", "L0_attn_Wq", "L0_attn_Wk", "L0_attn_Wv", "L0_attn_Wa", "L0_attn_Wb", "L0_attn_Wg", "L0_attn_Wo",
        "L0_attn_conv_wq", "L0_attn_conv_wk", "L0_attn_conv_wv", "L0_attn_A_log", "L0_attn_dt_bias",
        "L0_attn_norm_weight", "L0_xattn_theta_w", "L0_xattn_theta_b", "L0_xattn_phi_w", "L0_xattn_phi_b",
        "L0_xattn_g_w", "L0_xattn_g_b", "L0_xattn_ln_gamma", "L0_xattn_ln_beta", "L0_xattn_out_w",
        "L0_xattn_out_b", "L0_ffn_gate_w", "L0_ffn_up_w", "L0_ffn_down_w"]


def kernel(**inputs):
    import numpy as np
    import concourse.bacc as bacc
    from concourse.bass_utils import run_bass_kernel_spmd

    nc = bacc.Bacc("TRN2", target_bir_lowering=False, num_devices=1)
    arrays, args = {}, []
    for name in _INS:
        a = np.ascontiguousarray(inputs[name])
        arrays[f"in_{name}"] = a
        args.append(nc.dram_tensor(f"in_{name}", a.shape, mybir.dt.from_np(a.dtype), kind="ExternalInput").ap())
    args.append(nc.dram_tensor("out", (SEQ, P, HID), F32, kind="ExternalOutput").ap())
    program(nc, *args)
    r = run_bass_kernel_spmd(nc, [arrays], core_ids=[0])
    return r.results[0]["out"]
```
